# Optimizing a Trainium2 kernel written in Bass

```python
import numpy as np
import jax
import jax.numpy as jnp

def _softmax(x, axis=-1):
    return jax.nn.softmax(x, axis=axis)

def _gelu(x):
    return jax.nn.gelu(x, approximate=True)

def _silu(x):
    return jax.nn.silu(x)

def _sigmoid(x):
    return jax.nn.sigmoid(x)

def _layernorm(x, axis=-1, eps=1e-05):
    m = jnp.mean(x, axis=axis, keepdims=True)
    v = jnp.var(x, axis=axis, keepdims=True)
    return (x - m) / jnp.sqrt(v + eps)

def _scatter_add(tgt, idx, src, axis=0):
    return tgt.at[idx].add(src)

def _segment_sum(src, seg, n):
    return jax.ops.segment_sum(src, seg, n)
kernel_name = 'mk_xattn_seq_d4_seqx_r8_4ece1c'

def setup_inputs(seed: int=0):
    np.random.seed(seed)
    _w = jnp.asarray

    def _rec_inputs():
        import jax
        import jax.numpy as jnp
        _rk = jax.random.key(seed)
        x = -0.0001108 + 0.9999 * jax.random.normal(jax.random.fold_in(_rk, 1), (4, 256, 160), jnp.float32)
        _lenS = 256 - jax.random.randint(jax.random.fold_in(_rk, 7), (4,), 0, max(1, 256 // 4) + 1, jnp.int32)
        _lenS2 = 512 - jax.random.randint(jax.random.fold_in(_rk, 8), (4,), 0, max(1, 512 // 4) + 1, jnp.int32)
        _ctx_768P = jax.random.normal(jax.random.fold_in(_rk, 11), (4, 16, 96), jnp.float32)
        _ctx_768c = jax.random.dirichlet(jax.random.fold_in(_rk, 511), 0.3 * jnp.ones((16,), jnp.float32), (4, 512))
        _ctx_768t = jnp.einsum('bsk,bkd->bsd', _ctx_768c, _ctx_768P)
        _ctx_768t = _ctx_768t * jax.lax.rsqrt(jnp.mean(jnp.square(_ctx_768t)) + 1e-12) * 0.953939
        ctx_768 = 0.00114861 + 0.999593 * (_ctx_768t + 0.3 * jax.random.normal(jax.random.fold_in(_rk, 611), (4, 512, 96), jnp.float32))
        return (x, ctx_768)
    x, ctx_768 = _rec_inputs()

    def _L0_xattn_setup():
        import jax, jax.numpy as jnp
        import numpy as np
        HEADS = 20
        NUM_AOE = 16
        NUM_IP = 16
        key = jax.random.key(seed)
        ks = jax.random.split(key, 7)
        B, Sq, H = (8, 512, 160)
        Skv, C = (109, 96)
        scale = 0.02
        return {'hidden_states': jax.random.normal(ks[0], (B, Sq, H), jnp.float32), 'encoder_hidden_states': jax.random.normal(ks[1], (B, Skv, C), jnp.float32), 'Wq': jax.random.normal(ks[2], (H, H), jnp.float32) * scale, 'Wk': jax.random.normal(ks[3], (C, H), jnp.float32) * scale, 'Wv': jax.random.normal(ks[4], (C, H), jnp.float32) * scale, 'Wo': jax.random.normal(ks[5], (H, H), jnp.float32) * scale, 'bo': jnp.zeros((H,), jnp.float32)}
    _L0_xattn_all = _L0_xattn_setup()
    _L0_xattn_in = {k: v for k, v in _L0_xattn_all.items() if k in ('Wq', 'Wk', 'Wv', 'Wo', 'bo')}
    del _L0_xattn_all

    def _L1_xattn_setup():
        import jax, jax.numpy as jnp
        import numpy as np
        D = 160
        H = 20
        DH = D // H
        CTX = 96
        FF_IN = 4 * D
        EPS = 1e-05

        def _ln(x, g, b):
            m = jnp.mean(x, axis=-1, keepdims=True)
            v = jnp.mean(jnp.square(x - m), axis=-1, keepdims=True)
            return (x - m) * jax.lax.rsqrt(v + EPS) * g + b

        def _attn(x, ctx, wq, wk, wv, wo, bo, heads):
            b, n, _ = x.shape
            j = ctx.shape[1]
            dh = wq.shape[1] // heads
            scale = dh ** (-0.5)
            q = (x @ wq).reshape(b, n, heads, dh).transpose(0, 2, 1, 3)
            k = (ctx @ wk).reshape(b, j, heads, dh).transpose(0, 2, 1, 3)
            v = (ctx @ wv).reshape(b, j, heads, dh).transpose(0, 2, 1, 3)
            sim = jnp.einsum('bhid,bhjd->bhij', q, k) * scale
            a = jax.nn.softmax(sim, axis=-1)
            out = jnp.einsum('bhij,bhjd->bhid', a, v)
            out = out.transpose(0, 2, 1, 3).reshape(b, n, heads * dh)
            return out @ wo + bo
        key = jax.random.key(seed)
        ks = jax.random.split(key, 24)
        r = lambda k, shp, s: jax.random.normal(k, shp, dtype=jnp.float32) * s
        d = {'x': r(ks[0], (8, 128, D), 1.0), 'context': r(ks[1], (8, 77, CTX), 1.0), 'heads': H, 'n1_g': jnp.ones((D,), jnp.float32), 'n1_b': jnp.zeros((D,), jnp.float32), 'q1': r(ks[2], (D, D), D ** (-0.5)), 'k1': r(ks[3], (D, D), D ** (-0.5)), 'v1': r(ks[4], (D, D), D ** (-0.5)), 'o1_w': r(ks[5], (D, D), D ** (-0.5)), 'o1_b': jnp.zeros((D,), jnp.float32), 'n2_g': jnp.ones((D,), jnp.float32), 'n2_b': jnp.zeros((D,), jnp.float32), 'q2': r(ks[6], (D, D), D ** (-0.5)), 'k2': r(ks[7], (CTX, D), CTX ** (-0.5)), 'v2': r(ks[8], (CTX, D), CTX ** (-0.5)), 'o2_w': r(ks[9], (D, D), D ** (-0.5)), 'o2_b': jnp.zeros((D,), jnp.float32), 'n3_g': jnp.ones((D,), jnp.float32), 'n3_b': jnp.zeros((D,), jnp.float32), 'ff_w1': r(ks[10], (D, 2 * FF_IN), D ** (-0.5)), 'ff_b1': jnp.zeros((2 * FF_IN,), jnp.float32), 'ff_w2': r(ks[11], (FF_IN, D), FF_IN ** (-0.5)), 'ff_b2': jnp.zeros((D,), jnp.float32)}
        return d
    _L1_xattn_all = _L1_xattn_setup()
    _L1_xattn_in = {k: v for k, v in _L1_xattn_all.items() if k in ('n1_g', 'n1_b', 'q1', 'k1', 'v1', 'o1_w', 'o1_b', 'n2_g', 'n2_b', 'q2', 'k2', 'v2', 'o2_w', 'o2_b', 'n3_g', 'n3_b', 'ff_w1', 'ff_b1', 'ff_w2', 'ff_b2')}
    del _L1_xattn_all

    def _L2_xattn_setup():
        import jax, jax.numpy as jnp
        import numpy as np
        HEADS = 8
        NUM_TOKENS = 4
        CROSS_ATTENTION_DIM = 96

        def _mha(q, k, v, heads=HEADS):
            B, Sq, H = q.shape
            Sk = k.shape[1]
            d = H // heads
            qh = q.reshape(B, Sq, heads, d).transpose(0, 2, 1, 3)
            kh = k.reshape(B, Sk, heads, d).transpose(0, 2, 1, 3)
            vh = v.reshape(B, Sk, heads, d).transpose(0, 2, 1, 3)
            scores = jnp.einsum('bhqd,bhkd->bhqk', qh, kh) * jnp.asarray(d, q.dtype) ** (-0.5)
            probs = jax.nn.softmax(scores, axis=-1)
            out = jnp.einsum('bhqk,bhkd->bhqd', probs, vh)
            return out.transpose(0, 2, 1, 3).reshape(B, Sq, H)
        key = jax.random.key(seed)
        ks = jax.random.split(key, 10)
        B, S, H, CAD, T = (4, 128, 160, CROSS_ATTENTION_DIM, NUM_TOKENS)
        sc = 0.02
        return {'hidden_states': jax.random.normal(ks[0], (B, S, H), jnp.float32), 'encoder_hidden_states': jax.random.normal(ks[1], (B, 77 + T, CAD), jnp.float32), 'Wq': jax.random.normal(ks[2], (H, H), jnp.float32) * sc, 'Wk': jax.random.normal(ks[3], (CAD, H), jnp.float32) * sc, 'Wv': jax.random.normal(ks[4], (CAD, H), jnp.float32) * sc, 'Wq_ca': jax.random.normal(ks[5], (T, H), jnp.float32) * sc, 'Wk_ca': jax.random.normal(ks[6], (CAD, H), jnp.float32) * sc, 'Wv_ca': jax.random.normal(ks[7], (CAD, H), jnp.float32) * sc, 'Wout': jax.random.normal(ks[8], (H, H), jnp.float32) * sc, 'b_out': jnp.zeros((H,), jnp.float32)}
    _L2_xattn_all = _L2_xattn_setup()
    _L2_xattn_in = {k: v for k, v in _L2_xattn_all.items() if k in ('Wq', 'Wk', 'Wv', 'Wq_ca', 'Wk_ca', 'Wv_ca', 'Wout', 'b_out')}
    del _L2_xattn_all

    def _L3_xattn_setup():
        import jax, jax.numpy as jnp
        import numpy as np
        D = 160
        H = 20
        DH = D // H
        CTX = 96
        FF_IN = 4 * D
        EPS = 1e-05

        def _ln(x, g, b):
            m = jnp.mean(x, axis=-1, keepdims=True)
            v = jnp.mean(jnp.square(x - m), axis=-1, keepdims=True)
            return (x - m) * jax.lax.rsqrt(v + EPS) * g + b

        def _attn(x, ctx, wq, wk, wv, wo, bo, heads):
            b, n, _ = x.shape
            j = ctx.shape[1]
            dh = wq.shape[1] // heads
            scale = dh ** (-0.5)
            q = (x @ wq).reshape(b, n, heads, dh).transpose(0, 2, 1, 3)
            k = (ctx @ wk).reshape(b, j, heads, dh).transpose(0, 2, 1, 3)
            v = (ctx @ wv).reshape(b, j, heads, dh).transpose(0, 2, 1, 3)
            sim = jnp.einsum('bhid,bhjd->bhij', q, k) * scale
            a = jax.nn.softmax(sim, axis=-1)
            out = jnp.einsum('bhij,bhjd->bhid', a, v)
            out = out.transpose(0, 2, 1, 3).reshape(b, n, heads * dh)
            return out @ wo + bo
        key = jax.random.key(seed)
        ks = jax.random.split(key, 24)
        r = lambda k, shp, s: jax.random.normal(k, shp, dtype=jnp.float32) * s
        d = {'x': r(ks[0], (8, 128, D), 1.0), 'context': r(ks[1], (8, 77, CTX), 1.0), 'heads': H, 'n1_g': jnp.ones((D,), jnp.float32), 'n1_b': jnp.zeros((D,), jnp.float32), 'q1': r(ks[2], (D, D), D ** (-0.5)), 'k1': r(ks[3], (D, D), D ** (-0.5)), 'v1': r(ks[4], (D, D), D ** (-0.5)), 'o1_w': r(ks[5], (D, D), D ** (-0.5)), 'o1_b': jnp.zeros((D,), jnp.float32), 'n2_g': jnp.ones((D,), jnp.float32), 'n2_b': jnp.zeros((D,), jnp.float32), 'q2': r(ks[6], (D, D), D ** (-0.5)), 'k2': r(ks[7], (CTX, D), CTX ** (-0.5)), 'v2': r(ks[8], (CTX, D), CTX ** (-0.5)), 'o2_w': r(ks[9], (D, D), D ** (-0.5)), 'o2_b': jnp.zeros((D,), jnp.float32), 'n3_g': jnp.ones((D,), jnp.float32), 'n3_b': jnp.zeros((D,), jnp.float32), 'ff_w1': r(ks[10], (D, 2 * FF_IN), D ** (-0.5)), 'ff_b1': jnp.zeros((2 * FF_IN,), jnp.float32), 'ff_w2': r(ks[11], (FF_IN, D), FF_IN ** (-0.5)), 'ff_b2': jnp.zeros((D,), jnp.float32)}
        return d
    _L3_xattn_all = _L3_xattn_setup()
    _L3_xattn_in = {k: v for k, v in _L3_xattn_all.items() if k in ('n1_g', 'n1_b', 'q1', 'k1', 'v1', 'o1_w', 'o1_b', 'n2_g', 'n2_b', 'q2', 'k2', 'v2', 'o2_w', 'o2_b', 'n3_g', 'n3_b', 'ff_w1', 'ff_b1', 'ff_w2', 'ff_b2')}
    del _L3_xattn_all
    return {'x': x, 'ctx_768': ctx_768, 'L0_xattn_Wq': _L0_xattn_in['Wq'], 'L0_xattn_Wk': _L0_xattn_in['Wk'], 'L0_xattn_Wv': _L0_xattn_in['Wv'], 'L0_xattn_Wo': _L0_xattn_in['Wo'], 'L0_xattn_bo': _L0_xattn_in['bo'], 'L1_xattn_n1_g': _L1_xattn_in['n1_g'], 'L1_xattn_n1_b': _L1_xattn_in['n1_b'], 'L1_xattn_q1': _L1_xattn_in['q1'], 'L1_xattn_k1': _L1_xattn_in['k1'], 'L1_xattn_v1': _L1_xattn_in['v1'], 'L1_xattn_o1_w': _L1_xattn_in['o1_w'], 'L1_xattn_o1_b': _L1_xattn_in['o1_b'], 'L1_xattn_n2_g': _L1_xattn_in['n2_g'], 'L1_xattn_n2_b': _L1_xattn_in['n2_b'], 'L1_xattn_q2': _L1_xattn_in['q2'], 'L1_xattn_k2': _L1_xattn_in['k2'], 'L1_xattn_v2': _L1_xattn_in['v2'], 'L1_xattn_o2_w': _L1_xattn_in['o2_w'], 'L1_xattn_o2_b': _L1_xattn_in['o2_b'], 'L1_xattn_n3_g': _L1_xattn_in['n3_g'], 'L1_xattn_n3_b': _L1_xattn_in['n3_b'], 'L1_xattn_ff_w1': _L1_xattn_in['ff_w1'], 'L1_xattn_ff_b1': _L1_xattn_in['ff_b1'], 'L1_xattn_ff_w2': _L1_xattn_in['ff_w2'], 'L1_xattn_ff_b2': _L1_xattn_in['ff_b2'], 'L2_xattn_Wq': _L2_xattn_in['Wq'], 'L2_xattn_Wk': _L2_xattn_in['Wk'], 'L2_xattn_Wv': _L2_xattn_in['Wv'], 'L2_xattn_Wq_ca': _L2_xattn_in['Wq_ca'], 'L2_xattn_Wk_ca': _L2_xattn_in['Wk_ca'], 'L2_xattn_Wv_ca': _L2_xattn_in['Wv_ca'], 'L2_xattn_Wout': _L2_xattn_in['Wout'], 'L2_xattn_b_out': _L2_xattn_in['b_out'], 'L3_xattn_n1_g': _L3_xattn_in['n1_g'], 'L3_xattn_n1_b': _L3_xattn_in['n1_b'], 'L3_xattn_q1': _L3_xattn_in['q1'], 'L3_xattn_k1': _L3_xattn_in['k1'], 'L3_xattn_v1': _L3_xattn_in['v1'], 'L3_xattn_o1_w': _L3_xattn_in['o1_w'], 'L3_xattn_o1_b': _L3_xattn_in['o1_b'], 'L3_xattn_n2_g': _L3_xattn_in['n2_g'], 'L3_xattn_n2_b': _L3_xattn_in['n2_b'], 'L3_xattn_q2': _L3_xattn_in['q2'], 'L3_xattn_k2': _L3_xattn_in['k2'], 'L3_xattn_v2': _L3_xattn_in['v2'], 'L3_xattn_o2_w': _L3_xattn_in['o2_w'], 'L3_xattn_o2_b': _L3_xattn_in['o2_b'], 'L3_xattn_n3_g': _L3_xattn_in['n3_g'], 'L3_xattn_n3_b': _L3_xattn_in['n3_b'], 'L3_xattn_ff_w1': _L3_xattn_in['ff_w1'], 'L3_xattn_ff_b1': _L3_xattn_in['ff_b1'], 'L3_xattn_ff_w2': _L3_xattn_in['ff_w2'], 'L3_xattn_ff_b2': _L3_xattn_in['ff_b2']}

def reference(x, ctx_768, L0_xattn_Wq, L0_xattn_Wk, L0_xattn_Wv, L0_xattn_Wo, L0_xattn_bo, L1_xattn_n1_g, L1_xattn_n1_b, L1_xattn_q1, L1_xattn_k1, L1_xattn_v1, L1_xattn_o1_w, L1_xattn_o1_b, L1_xattn_n2_g, L1_xattn_n2_b, L1_xattn_q2, L1_xattn_k2, L1_xattn_v2, L1_xattn_o2_w, L1_xattn_o2_b, L1_xattn_n3_g, L1_xattn_n3_b, L1_xattn_ff_w1, L1_xattn_ff_b1, L1_xattn_ff_w2, L1_xattn_ff_b2, L2_xattn_Wq, L2_xattn_Wk, L2_xattn_Wv, L2_xattn_Wq_ca, L2_xattn_Wk_ca, L2_xattn_Wv_ca, L2_xattn_Wout, L2_xattn_b_out, L3_xattn_n1_g, L3_xattn_n1_b, L3_xattn_q1, L3_xattn_k1, L3_xattn_v1, L3_xattn_o1_w, L3_xattn_o1_b, L3_xattn_n2_g, L3_xattn_n2_b, L3_xattn_q2, L3_xattn_k2, L3_xattn_v2, L3_xattn_o2_w, L3_xattn_o2_b, L3_xattn_n3_g, L3_xattn_n3_b, L3_xattn_ff_w1, L3_xattn_ff_b1, L3_xattn_ff_w2, L3_xattn_ff_b2):
    import jax
    import jax.numpy as jnp

    def _L0_xattn_ref(hidden_states, encoder_hidden_states, Wq, Wk, Wv, Wo, bo):
        import jax, jax.numpy as jnp
        import numpy as np
        HEADS = 20
        NUM_AOE = 16
        NUM_IP = 16
        B, Sq, H = hidden_states.shape
        Skv = encoder_hidden_states.shape[1]
        head_dim = H // HEADS
        residual = hidden_states
        q = (hidden_states @ Wq).reshape(B, Sq, HEADS, head_dim).transpose(0, 2, 1, 3)
        k = (encoder_hidden_states @ Wk).reshape(B, Skv, HEADS, head_dim).transpose(0, 2, 1, 3)
        v = (encoder_hidden_states @ Wv).reshape(B, Skv, HEADS, head_dim).transpose(0, 2, 1, 3)
        scores = jnp.einsum('bhqd,bhkd->bhqk', q, k) / jnp.sqrt(jnp.asarray(head_dim, q.dtype))
        probs = jax.nn.softmax(scores, axis=-1)
        scale_aoe = jnp.asarray(1.0, probs.dtype)
        scale_ip = jnp.asarray(1.0, probs.dtype)
        idx = jnp.arange(Skv)
        scale_vector = jnp.where(idx < NUM_AOE, scale_aoe, 1.0)
        scale_vector = jnp.where(idx >= Skv - NUM_IP, scale_vector * scale_ip, scale_vector)
        probs = probs * scale_vector
        probs = probs / probs.sum(axis=-1, keepdims=True)
        out = jnp.einsum('bhqk,bhkd->bhqd', probs, v)
        out = out.transpose(0, 2, 1, 3).reshape(B, Sq, H)
        out = out @ Wo + bo
        return out + residual

    def _L1_xattn_ref(x, context, heads, n1_g, n1_b, q1, k1, v1, o1_w, o1_b, n2_g, n2_b, q2, k2, v2, o2_w, o2_b, n3_g, n3_b, ff_w1, ff_b1, ff_w2, ff_b2):
        import jax, jax.numpy as jnp
        import numpy as np
        D = 160
        H = 20
        DH = D // H
        CTX = 96
        FF_IN = 4 * D
        EPS = 1e-05

        def _ln(x, g, b):
            m = jnp.mean(x, axis=-1, keepdims=True)
            v = jnp.mean(jnp.square(x - m), axis=-1, keepdims=True)
            return (x - m) * jax.lax.rsqrt(v + EPS) * g + b

        def _attn(x, ctx, wq, wk, wv, wo, bo, heads):
            b, n, _ = x.shape
            j = ctx.shape[1]
            dh = wq.shape[1] // heads
            scale = dh ** (-0.5)
            q = (x @ wq).reshape(b, n, heads, dh).transpose(0, 2, 1, 3)
            k = (ctx @ wk).reshape(b, j, heads, dh).transpose(0, 2, 1, 3)
            v = (ctx @ wv).reshape(b, j, heads, dh).transpose(0, 2, 1, 3)
            sim = jnp.einsum('bhid,bhjd->bhij', q, k) * scale
            a = jax.nn.softmax(sim, axis=-1)
            out = jnp.einsum('bhij,bhjd->bhid', a, v)
            out = out.transpose(0, 2, 1, 3).reshape(b, n, heads * dh)
            return out @ wo + bo
        h1 = _ln(x, n1_g, n1_b)
        x = _attn(h1, h1, q1, k1, v1, o1_w, o1_b, heads) + x
        h2 = _ln(x, n2_g, n2_b)
        x = _attn(h2, context, q2, k2, v2, o2_w, o2_b, heads) + x
        h3 = _ln(x, n3_g, n3_b)
        proj = h3 @ ff_w1 + ff_b1
        a, g = jnp.split(proj, 2, axis=-1)
        ff = a * jax.nn.gelu(g, approximate=False) @ ff_w2 + ff_b2
        return ff + x

    def _L2_xattn_ref(hidden_states, encoder_hidden_states, Wq, Wk, Wv, Wq_ca, Wk_ca, Wv_ca, Wout, b_out):
        import jax, jax.numpy as jnp
        import numpy as np
        HEADS = 8
        NUM_TOKENS = 4
        CROSS_ATTENTION_DIM = 96

        def _mha(q, k, v, heads=HEADS):
            B, Sq, H = q.shape
            Sk = k.shape[1]
            d = H // heads
            qh = q.reshape(B, Sq, heads, d).transpose(0, 2, 1, 3)
            kh = k.reshape(B, Sk, heads, d).transpose(0, 2, 1, 3)
            vh = v.reshape(B, Sk, heads, d).transpose(0, 2, 1, 3)
            scores = jnp.einsum('bhqd,bhkd->bhqk', qh, kh) * jnp.asarray(d, q.dtype) ** (-0.5)
            probs = jax.nn.softmax(scores, axis=-1)
            out = jnp.einsum('bhqk,bhkd->bhqd', probs, vh)
            return out.transpose(0, 2, 1, 3).reshape(B, Sq, H)
        residual = hidden_states
        unet_size = residual.shape[1]
        end_pos = encoder_hidden_states.shape[1] - NUM_TOKENS
        enc = encoder_hidden_states[:, :end_pos, :]
        ca = encoder_hidden_states[:, end_pos:, :]
        query = hidden_states @ Wq
        keyt = enc @ Wk
        valt = enc @ Wv
        hs = _mha(query, keyt, valt)
        ca_q1 = jnp.einsum('btc,th->bch', ca, Wq_ca)
        indices = np.linspace(0, CROSS_ATTENTION_DIM - 1, unet_size).astype(np.int64)
        ca_q1 = ca_q1[:, indices, :]
        ca_hs1 = _mha(ca_q1, residual, residual)
        ca_q2 = ca_hs1 @ Wq
        ca_k2 = ca @ Wk_ca
        ca_v2 = ca @ Wv_ca
        ca_hs2 = _mha(ca_q2, ca_k2, ca_v2)
        out = hs + ca_hs2
        out = out @ Wout + b_out
        out = out + residual
        return out

    def _L3_xattn_ref(x, context, heads, n1_g, n1_b, q1, k1, v1, o1_w, o1_b, n2_g, n2_b, q2, k2, v2, o2_w, o2_b, n3_g, n3_b, ff_w1, ff_b1, ff_w2, ff_b2):
        import jax, jax.numpy as jnp
        import numpy as np
        D = 160
        H = 20
        DH = D // H
        CTX = 96
        FF_IN = 4 * D
        EPS = 1e-05

        def _ln(x, g, b):
            m = jnp.mean(x, axis=-1, keepdims=True)
            v = jnp.mean(jnp.square(x - m), axis=-1, keepdims=True)
            return (x - m) * jax.lax.rsqrt(v + EPS) * g + b

        def _attn(x, ctx, wq, wk, wv, wo, bo, heads):
            b, n, _ = x.shape
            j = ctx.shape[1]
            dh = wq.shape[1] // heads
            scale = dh ** (-0.5)
            q = (x @ wq).reshape(b, n, heads, dh).transpose(0, 2, 1, 3)
            k = (ctx @ wk).reshape(b, j, heads, dh).transpose(0, 2, 1, 3)
            v = (ctx @ wv).reshape(b, j, heads, dh).transpose(0, 2, 1, 3)
            sim = jnp.einsum('bhid,bhjd->bhij', q, k) * scale
            a = jax.nn.softmax(sim, axis=-1)
            out = jnp.einsum('bhij,bhjd->bhid', a, v)
            out = out.transpose(0, 2, 1, 3).reshape(b, n, heads * dh)
            return out @ wo + bo
        h1 = _ln(x, n1_g, n1_b)
        x = _attn(h1, h1, q1, k1, v1, o1_w, o1_b, heads) + x
        h2 = _ln(x, n2_g, n2_b)
        x = _attn(h2, context, q2, k2, v2, o2_w, o2_b, heads) + x
        h3 = _ln(x, n3_g, n3_b)
        proj = h3 @ ff_w1 + ff_b1
        a, g = jnp.split(proj, 2, axis=-1)
        ff = a * jax.nn.gelu(g, approximate=False) @ ff_w2 + ff_b2
        return ff + x
    x = _L0_xattn_ref(x, ctx_768, L0_xattn_Wq, L0_xattn_Wk, L0_xattn_Wv, L0_xattn_Wo, L0_xattn_bo)
    x = _L1_xattn_ref(x, ctx_768, 20, L1_xattn_n1_g, L1_xattn_n1_b, L1_xattn_q1, L1_xattn_k1, L1_xattn_v1, L1_xattn_o1_w, L1_xattn_o1_b, L1_xattn_n2_g, L1_xattn_n2_b, L1_xattn_q2, L1_xattn_k2, L1_xattn_v2, L1_xattn_o2_w, L1_xattn_o2_b, L1_xattn_n3_g, L1_xattn_n3_b, L1_xattn_ff_w1, L1_xattn_ff_b1, L1_xattn_ff_w2, L1_xattn_ff_b2)
    x = _L2_xattn_ref(x, ctx_768, L2_xattn_Wq, L2_xattn_Wk, L2_xattn_Wv, L2_xattn_Wq_ca, L2_xattn_Wk_ca, L2_xattn_Wv_ca, L2_xattn_Wout, L2_xattn_b_out)
    x = _L3_xattn_ref(x, ctx_768, 20, L3_xattn_n1_g, L3_xattn_n1_b, L3_xattn_q1, L3_xattn_k1, L3_xattn_v1, L3_xattn_o1_w, L3_xattn_o1_b, L3_xattn_n2_g, L3_xattn_n2_b, L3_xattn_q2, L3_xattn_k2, L3_xattn_v2, L3_xattn_o2_w, L3_xattn_o2_b, L3_xattn_n3_g, L3_xattn_n3_b, L3_xattn_ff_w1, L3_xattn_ff_b1, L3_xattn_ff_w2, L3_xattn_ff_b2)
    return x

_drawn_inputs = setup_inputs


def setup_inputs(seed=0):
    import zlib

    import numpy as np

    out = dict(_drawn_inputs(seed))
    spreads = {'L0_xattn_bo': (0.0, 0.1),
     'L1_xattn_n1_g': (1.0, 0.2),
     'L1_xattn_n1_b': (0.0, 0.1),
     'L1_xattn_o1_b': (0.0, 0.1),
     'L1_xattn_n2_g': (1.0, 0.2),
     'L1_xattn_n2_b': (0.0, 0.388),
     'L1_xattn_o2_b': (0.0, 0.1),
     'L1_xattn_n3_g': (1.0, 0.2),
     'L1_xattn_n3_b': (0.0, 0.1),
     'L1_xattn_ff_b1': (0.0, 0.1),
     'L1_xattn_ff_b2': (0.0, 0.1),
     'L2_xattn_b_out': (0.0, 0.1),
     'L3_xattn_n1_g': (1.0, 0.2),
     'L3_xattn_n1_b': (0.0, 0.1),
     'L3_xattn_o1_b': (0.0, 0.1),
     'L3_xattn_n2_g': (1.0, 0.556),
     'L3_xattn_n2_b': (0.0, 0.713),
     'L3_xattn_o2_b': (0.0, 0.1),
     'L3_xattn_n3_g': (1.0, 0.2),
     'L3_xattn_n3_b': (0.0, 0.1),
     'L3_xattn_ff_b1': (0.0, 0.1),
     'L3_xattn_ff_b2': (0.0, 0.1)}
    factors = {'L0_xattn_Wq': 8.0,
     'L0_xattn_Wk': 8.0,
     'L2_xattn_Wq': 8.0,
     'L2_xattn_Wk': 8.0,
     'L2_xattn_Wv': 3.125,
     'L2_xattn_Wq_ca': 200.0,
     'L2_xattn_Wk_ca': 76.205}
    for name, (base, spread) in spreads.items():
        noise = np.random.default_rng([zlib.crc32(name.encode()), seed]).standard_normal(out[name].shape)
        drawn = base * np.exp(spread * noise) if base else spread * noise
        out[name] = jnp.asarray(drawn.astype(out[name].dtype))
    for name, factor in factors.items():
        out[name] = (out[name] * factor).astype(out[name].dtype)
    return out
```

```python
from contextlib import ExitStack

import numpy as np

import concourse.bass as bass
from concourse import mybir

F32 = mybir.dt.float32
FR = mybir.dt.float32r
ALU = mybir.AluOpType
ACT = mybir.ActivationFunctionType
AX = mybir.AxisListType

B, SQ, D = 4, 256, 160
SK, C = 512, 96
P = 128
TQ = SQ // P
D2 = D - P
FF = 4 * D
FC = FF // P
NCA = 4
NENC = SK - NCA
EPS = 1e-5
PAIRS = B // 2

ATT = {
    0: dict(kind="cross", H=20, dh=8, sr=32, nq=SQ, nk=SK, hps=2, hpm=1),
    1: dict(kind="self", H=20, dh=8, sr=32, nq=SQ, nk=SQ, hps=2, hpm=2),
    2: dict(kind="cross", H=20, dh=8, sr=32, nq=SQ, nk=SK, hps=2, hpm=1),
    3: dict(kind="enc", H=8, dh=20, sr=64, nq=SQ, nk=NENC, hps=2, hpm=1),
    4: dict(kind="ca", H=8, dh=20, sr=64, nq=C, nk=SQ, hps=4, hpm=2),
    5: dict(kind="self", H=20, dh=8, sr=32, nq=SQ, nk=SQ, hps=2, hpm=2),
    6: dict(kind="cross", H=20, dh=8, sr=32, nq=SQ, nk=SK, hps=2, hpm=1),
}
PHASES = [(0,), (1,), (2,), (4, 3), (5,), (6,)]
N_ST, N_MX, N_P = 3, 2, 6
RING = 4
PV_LAG = 2
M_LEAD = 3

W_MAIN = {"q0": (0, 160), "o0": (160, 320), "q3": (320, 480), "o3": (480, 640)}
W_BLOCK = {"qkv": (0, 480), "o1": (480, 640), "q2": (640, 800), "o2": (800, 960), "w1": (960, 2240)}
W_CTX = {0: (0, 320), 3: (320, 640), "ca": (640, 960)}
BIAS = {0: 0, 1: 1, 2: 2, "ff1": 3, 3: 4, 5: 5, 6: 6, "ff3": 7}
LNS = {1: 0, 2: 1, "ff1": 2, 5: 3, 6: 4, "ff3": 5}


def chunk_rows(nk, c):
    return min(P, nk - P * c)


def q_tiles(u):
    return [(t, P) for t in range(TQ)] if ATT[u]["nq"] == SQ else [(TQ, ATT[u]["nq"])]


def background(ph, p):
    def ctx_keys(u):
        s = []
        for pair in range(2):
            s += [("kv_proj", u, p, t) for t in (2 * pair, 2 * pair + 1)]
            s += [("k_tr", u, p, pair, gg) for gg in range(3 if ATT[u]["sr"] == 32 else 2)]
        return s

    def queries(u):
        n = 3 if ATT[u]["sr"] == 32 else 2
        return [("m_zero", u, p), ("q_proj", u, p)] + [("q_tr", u, p, gg) for gg in range(n)]

    def own_keys(u):
        return ([("m_zero", u, p)] + [("qkv_proj", u, p, t) for t in range(TQ)] + [("k_tr", u, p, 0, gg) for gg in range(3)]
                + [("q_tr", u, p, gg) for gg in range(3)])

    def output(u):
        return [("o_nat", u, p, i) for i in range(3)] + [("o_tr", u, p), ("o_proj", u, p)]

    def feed(tag):
        return ([("ln", tag, p), ("x_bias", tag, p), ("h_tr", tag, p)] + [("ff_g", tag, p, i) for i in range(3)] + [("gelu", tag, p)]
                + [("ff_a", tag, p, i) for i in range(3)] + [("ff_o", tag, p)])

    def merge(a, b):
        out, j = [], 0
        for i, s in enumerate(a):
            out.append(s)
            while j < (i + 1) * len(b) // len(a):
                out.append(b[j])
                j += 1
        return out + b[j:]

    if ph == -1:
        return [("ctx_tr", p)] + merge(ctx_keys(0), [("x_bias", 0, p), ("h_tr", 0, p)] + queries(0))
    if ph == 0:
        return output(0) + [("ln", 1, p), ("x_bias", 1, p), ("h_tr", 1, p)] + own_keys(1)
    if ph == 1:
        return merge(output(1) + [("ln", 2, p), ("x_bias", 2, p), ("h_tr", 2, p)] + queries(2), ctx_keys(2))
    if ph == 2:
        return (merge(output(2) + feed("ff1"), [("m_zero", 4, p), ("ca_q", p), ("q_tr", 4, p, 0)] + ctx_keys(3) + [("ca_kv", p)])
                + [("x_keys", p), ("k_tr", 4, p, 0, 0), ("k_tr", 4, p, 0, 1), ("x_bias", 3, p), ("h_tr", 3, p)] + queries(3))
    if ph == 3:
        return ([("o_nat", 4, p, 0), ("c_tr", p), ("c_q", p), ("c_s", p), ("c_p", p), ("o_nat", 3, p, 0), ("o_tr", 3, p),
                 ("c_o", p), ("o_proj", 3, p), ("ln", 5, p), ("x_bias", 5, p), ("h_tr", 5, p)] + own_keys(5))
    if ph == 4:
        return merge(output(5) + [("ln", 6, p), ("x_bias", 6, p), ("h_tr", 6, p)] + queries(6), ctx_keys(6))
    return output(6) + feed("ff3") + [("store", p)]


def plan():
    quads, slots, span = [], [], {}
    for ph, us in enumerate(PHASES):
        for p in range(2):
            first = len(slots)
            for u in us:
                a = ATT[u]
                for qd in range(a["H"] // 4):
                    n = len(quads)
                    q = dict(n=n, ph=ph, p=p, u=u, qd=qd, start=len(slots))
                    nc_ = -(-a["nk"] // P)
                    for c in range(nc_):
                        for h in range(4 * qd, 4 * qd + 4, a["hps"]):
                            slots.append(dict(n=n, u=u, p=p, c=c, heads=list(range(h, h + a["hps"])), last=c == nc_ - 1 and h + a["hps"] == 4 * qd + 4))
                    q["slots"] = list(range(q["start"], len(slots)))
                    q["items"] = [(t, rows, list(range(h, h + a["hpm"])))
                                  for h in range(4 * qd, 4 * qd + 4, a["hpm"]) for t, rows in q_tiles(u)]
                    quads.append(q)
            span[ph, p] = (first, len(slots))
    at = {}

    def put(s, rank, step):
        at.setdefault(s, []).append((rank, len(at.get(s, [])), step))

    for q in quads:
        n, s0 = q["n"], q["start"]
        w = len(quads[n - 1]["slots"]) if n else 1
        hi = s0 - M_LEAD
        lo = hi - w
        m = len(q["items"])
        put(lo, 0, ("kdma", n))
        for i in range(m):
            put(lo + (i * w) // m, 1, ("max", n, i))
        put(hi, 2, ("negm", n))
        put(hi + 1, 3, ("mtr", n))
        a = ATT[q["u"]]
        for c in range(-(-a["nk"] // P)):
            last = max(s for s in q["slots"] if slots[s]["c"] == c)
            put(last + PV_LAG, 2, ("pv", n, c))
        put(q["slots"][-1] + PV_LAG, 3, ("oev", n))
    total = len(slots)
    lead = 12
    before = [s for s in background(-1, 0)]
    for p in range(2):
        for ph in range(-1, len(PHASES)):
            if (ph, p) == (-1, 0):
                continue
            lo = span[ph, p][1] + PV_LAG + 1 if ph >= 0 else 0
            hi = span[ph + 1, p][0] - lead if ph + 1 < len(PHASES) else total + 8
            steps = background(ph, p)
            for i, s in enumerate(steps):
                put(max(lo, 0) + (i * max(hi - lo, 1)) // len(steps), 4, s)
    order = list(before)
    for s in range(min(at), max(max(at), total) + 1):
        if 0 <= s < total:
            order.append(("st", s))
        order += [x[2] for x in sorted(at.get(s, []), key=lambda x: (x[0], x[1]))]
    return order, quads, slots


SPARE = {"ctx_tr", "kv_proj", "k_tr", "q_proj", "q_tr", "qkv_proj", "o_nat", "o_tr", "o_proj", "h_tr", "ff_g", "ff_a",
         "ff_o", "ca_q", "ca_kv", "c_tr", "c_q", "c_s", "c_p", "c_o", "mtr"}

SIGNALS = {
    "scores_full": {"st"}, "probs_ready": {"st"}, "max_full": {"max"}, "max_taken": {"max"}, "negm_ready": {"negm"},
    "out_full": {"pv_last"}, "out_taken": {"oev"}, "k_high": {"kv_proj", "x_keys", "qkv_proj"}, "x_split": {"x_keys"},
    "q_high": {"q_proj", "ca_q"}, "m_zeroed": {"m_zero"}, "x_biased": {"x_bias"}, "var_ready": {"ln"},
    "rstd_ready": {"ln"}, "xn_ready": {"ln"}, "gate_ready": {"gelu"}, "c_exp": {"c_s"}, "c_probs": {"c_s"},
}

ROWS_FROM = {1: ("o_proj", 0), 2: ("o_proj", 1), "ff1": ("o_proj", 2), 3: ("ff_o", "ff1"), 5: ("o_proj", 3),
             6: ("o_proj", 5), "ff3": ("o_proj", 6)}


def parts_of(u, i):
    if u == 4:
        return [(qd, 0, C) for qd in range(2)]
    if u == 3:
        return [(qd, t, P) for t in range(TQ) for qd in range(2)]
    return [(qd, i, P) for qd in range(4)] if i < 2 else [(4, t, P) for t in range(TQ)]


def build(nc, io):
    order, quads, slots = plan()
    value, seen, turn, uses = {}, {}, {}, 0
    for step in order:
        kinds = {step[0]}
        if step[0] == "pv" and step[2] == -(-ATT[quads[step[1]]["u"]]["nk"] // P) - 1:
            kinds.add("pv_last")
        for name, by in SIGNALS.items():
            if kinds & by:
                seen[name] = seen.get(name, 0) + 1
                value[name, step] = seen[name]
        if step[0] in SPARE:
            turn[step] = (uses % 2, uses // 2)
            uses += 1

    def slot_value(name, s):
        return value[name, ("st", s)]

    with ExitStack() as ctx:
        def sb(name, shape, dt=F32):
            return ctx.enter_context(nc.sbuf_tensor(name, shape, dt))

        def sem(name):
            return ctx.enter_context(nc.semaphore(name))

        st_ps = [ctx.enter_context(nc.psum_tensor(f"st_ps{i}", [P, 512], F32)) for i in range(N_ST)]
        mx_ps = [ctx.enter_context(nc.psum_tensor(f"mx_ps{i}", [P, 512], F32)) for i in range(N_MX)]
        pv_ps = ctx.enter_context(nc.psum_tensor("pv_ps", [P, 512], F32))
        sp_ps = [ctx.enter_context(nc.psum_tensor(f"sp_ps{i}", [P, 512], F32)) for i in range(2)]

        wm = sb("wm", [P, 640])
        wm2 = sb("wm2", [D2, 640])
        wb = sb("wb", [P, 3040])
        wb2 = sb("wb2", [D2, 2240])
        wbc = sb("wbc", [C, 320])
        wc = sb("wc", [C, 960])
        wqca = sb("wqca", [NCA, D])
        cols = sb("cols", [P, 32])
        cols2 = sb("cols2", [D2, 12])
        bias = sb("bias", [P, 8 * D])
        ident = sb("ident", [P, P])
        identr = sb("identr", [P, P], FR)
        spread = sb("spread", [C, SQ])
        kmask = sb("kmask", [P, 32])
        kmask2 = sb("kmask2", [D2, 32])
        vmask = sb("vmask", [32, D])
        halfpow = sb("halfpow", [P, TQ])
        def two(name, shape, dt=F32):
            return [sb(f"{name}{p}", shape, dt) for p in range(2)]

        x = two("x", [P, TQ, D])
        xb = two("xb", [P, TQ, D])
        nat = two("nat", [P, TQ, D])
        natc = two("natc", [C, D])
        hT = two("hT", [P, SQ])
        hT2 = two("hT2", [D2, SQ])
        ctxT = two("ctxT", [C, SK])
        caT8 = two("caT8", [C, 32])
        ca_n = two("ca_n", [NCA, C])
        kdense = two("kdense", [P, 5, SK])
        v20 = two("v20", [P, 4, 20, 9])
        v8 = two("v8", [P, 6, 8, 21])
        qs20 = two("qs20", [P, TQ, 20, 32], FR)
        qs8 = two("qs8", [P, TQ + 1, 8, 64], FR)
        qT = two("qT", [P, 5, SQ], FR)
        qTc = two("qTc", [P, 4, C], FR)
        mx = two("mx", [P, TQ + 1, 20])
        oT = two("oT", [P, 5, SQ])
        oTc = two("oTc", [P, 2, C])
        kbd = two("kbd", [P, 32])
        kbd2 = two("kbd2", [D2, 32])
        vbd = two("vbd", [32, D])
        ks20 = sb("ks20", [P, 2, 20, 32], FR)
        ks8 = sb("ks8", [P, 2, 8, 64], FR)
        ring = sb("ring", [P, RING, 4, SK], FR)
        zeros = sb("zeros", [P, SK])
        probs = sb("probs", [P, N_P, 512])
        gate = sb("gate", [P, FC, SQ])
        ctx_n = gate[:, :, :].rearrange("p a b -> p (a b)")[:, 0:2 * 4 * C].rearrange("p (s t c) -> p s t c", s=2, t=4)
        stats = sb("stats", [P, TQ, 6])
        mv = sb("mv", [P, TQ, 2])
        rstd = sb("rstd", [P, TQ])
        rinv = sb("rinv", [P, 4, 20])
        cT = sb("cT", [P, C])
        cT2 = sb("cT2", [D2, C])
        cq = sb("cq", [P, C])
        cq2 = sb("cq2", [D2, C])
        cs = sb("cs", [C, 32])
        cmax = sb("cmax", [C, 8])
        cpT = sb("cpT", [32, SQ])

        S = {name: sem(name) for name in SIGNALS}
        spare_full = [sem(f"spare_full{i}") for i in range(2)]
        spare_taken = [sem(f"spare_taken{i}") for i in range(2)]
        ring_in = [sem(f"ring_in{i}") for i in range(RING)]
        s_in = sem("inputs_in")
        s_blk = [sem(f"block_weights{i}") for i in range(2)]
        s_used = sem("probs_used")
        dve_link = sem("dve_link")
        act_link = sem("act_link")
        pool_link = sem("pool_link")
        s_out = sem("stored")
        s_w = sem("weights_in")
        s_setup = sem("setup_done")
        per_turn = (list(S.values()) + spare_full + spare_taken + ring_in
                    + [s_in, *s_blk, s_used, dve_link, act_link, pool_link, s_out])

        def of(u):
            return P // ATT[u]["sr"]

        def region(u, h):
            return h % 4 if of(u) == 4 else 2 * (h % 2) + h % 4 // 2

        def key_op(n, h):
            return ring[:, n % RING, region(quads[n]["u"], h), :]

        def dirty(n):
            return n >= RING and of(quads[n]["u"]) == 4 and of(quads[n - RING]["u"]) == 2

        ring_dmas = {n: sum(8 if dirty(m) else 4 for m in range(n % RING, n + 1, RING)) for n in range(len(quads))}

        used_after, count = {}, 0
        for step in order:
            if step[0] == "pv":
                for s in quads[step[1]]["slots"]:
                    if slots[s]["c"] == step[2]:
                        if slots[s]["last"]:
                            used_after[s] = (S["out_full"], step[1] + 1)
                        else:
                            count += 1
                            used_after[s] = (s_used, count)

        def query_op(u, p):
            return qTc[p] if ATT[u]["kind"] == "ca" else qT[p]

        def dense_keys(u, p, g):
            if u == 4:
                return oT[p][:, 2 + g, :] if g < 2 else kdense[p][:, 4, (g - 2) * SQ:(g - 1) * SQ]
            return kdense[p][:, g, :]

        def taken(eng, step):
            b, k = turn[step]
            eng.wait_ge(spare_taken[b], k + 1)

        def query_stack(u, p):
            return qs20[p] if ATT[u]["sr"] == 32 else qs8[p]

        def block_of(u):
            return s_blk[0] if u in (1, 2, "ff1") else s_blk[1]

        def wts(name, lo=0, hi=None):
            a, b = W_BLOCK[name]
            return slice(a + lo, a + hi if hi is not None else b)

        with nc.Block() as block:
            @block.sync
            def _(sp):
                for dst, src in ((ident, "ident"), (wc, "w_ctx"), (wm, "w_main"), (wm2, "w_main2"), (cols, "cols"),
                                 (cols2, "cols2"), (wqca, "w_qca"), (spread, "spread"), (kmask, "kmask"),
                                 (kmask2, "kmask2"), (vmask, "vmask")):
                    sp.dma_start(dst[:, :], io[src]).then_inc(s_w, 16)
                sp.dma_start(bias[:, :], io["bias"].broadcast_to([P, 8 * D])).then_inc(s_w, 16)
                sp.wait_ge(s_w, 12 * 16)

            @block.scalar
            def _(act):
                act.wait_ge(s_w, 12 * 16)
                nc.scalar.activation(identr[:, :], ident[:, :], ACT.Copy).then_inc(s_setup, 1)

            @block.vector
            def _(dve):
                nc.vector.memset(ring[:, :, :, :].bitcast(F32), 0.0)
                nc.vector.memset(zeros[:, :], 0.0)
                nc.vector.memset(pv_ps[:, :], 0.0)
                nc.vector.memset(v20[0][:, :, :, 8:9], 1.0)
                nc.vector.memset(v20[1][:, :, :, 8:9], 1.0)
                nc.vector.memset(v8[0][:, :, :, 20:21], 1.0)
                nc.vector.memset(v8[1][:, :, :, 20:21], 1.0).then_inc(s_setup, 1)

            @block.gpsimd
            def _(pool):
                for t in (ks20, ks8, *qs20, *qs8):
                    nc.gpsimd.memset(t[:, :, :, :].bitcast(F32), 0.0).then_inc(pool_link, 1)
                pool.wait_ge(pool_link, 6)
                nc.gpsimd.memset(ks20[:, :, :, 24:26].bitcast(F32), 1.0)
                nc.gpsimd.memset(ks8[:, :, :, 60:62].bitcast(F32), 1.0)
                nc.gpsimd.memset(halfpow[:, :], -0.5).then_inc(s_setup, 1)

        with nc.Block() as block:
            @block.sync
            def _(sp):
                sp.sem_clear(pool_link)

        with nc.Fori(0, PAIRS) as pair:
            turn_block = nc.Block()
            block = turn_block.__enter__()

            @block.sync
            def _(sp):
                for p in range(2):
                    b = pair * 2 + p
                    sp.dma_start(ctx_n[:, p, :, :], io["ctx"][bass.ds(b, 1), :, :].rearrange("a (t r) c -> r (a t) c", r=P)).then_inc(s_in, 16)
                    sp.dma_start(x[p][:, :, :], io["x"][bass.ds(b, 1), :, :].rearrange("a (t r) d -> r (a t) d", r=P)).then_inc(s_in, 16)
                    sp.dma_start(ca_n[p][:, :], io["ctx"][bass.ds(b, 1), NENC:SK, :].rearrange("a r c -> (a r) c")).then_inc(s_in, 16)

                def block_weights(layer):
                    for dst, src in ((wb, "w_blk"), (wb2, "w_blk2"), (wbc, "w_blkc")):
                        sp.dma_start(dst[:, :], io[src][layer]).then_inc(s_blk[layer], 16)

                block_weights(0)
                for step in order:
                    if step[0] == "kdma":
                        n = step[1]
                        u, p, qd = quads[n]["u"], quads[n]["p"], quads[n]["qd"]
                        a = ATT[u]
                        taken(sp, [s for s in order if s[0] == "k_tr" and s[1] == u and s[2] == p][-1])
                        if n >= RING:
                            sp.wait_ge(S["scores_full"], quads[n - RING]["slots"][-1] + 1)
                        if dirty(n):
                            for r in range(4):
                                other = slice(32 * (r ^ 1), 32 * (r ^ 1) + 32)
                                sp.dma_start(ring[other, n % RING, r, :].bitcast(F32), zeros[other, :]).then_inc(ring_in[n % RING], 16)
                        for h in range(4 * qd, 4 * qd + 4):
                            j, g = h % of(u), h // of(u)
                            rows = slice(a["sr"] * j, a["sr"] * (j + 1))
                            sp.dma_start(ring[rows, n % RING, region(u, h), 0:a["nk"]].bitcast(F32),
                                         dense_keys(u, p, g)[rows, 0:a["nk"]]).then_inc(ring_in[n % RING], 16)
                    elif step == ("ff_o", "ff1", 1):
                        taken(sp, step)
                        block_weights(1)
                    elif step[0] == "store":
                        p = step[1]
                        taken(sp, ("ff_o", "ff3", p))
                        sp.dma_start(io["out"][bass.ds(pair * 2 + p, 1), :, :].rearrange("a (t r) d -> r (a t) d", r=P), x[p][:, :, :]).then_inc(s_out, 16)
                sp.wait_ge(s_out, 32)

            @block.tensor
            def _(pe):
                def take(step):
                    b, k = turn[step]
                    if k:
                        pe.wait_ge(spare_taken[b], k)
                    return sp_ps[b], spare_full[b]

                def two_part(out, lhs, lhs2, rhs, rhs2):
                    pe.matmul(out, lhs, rhs, start=True, stop=False)
                    return pe.matmul(out, lhs2, rhs2, start=False, stop=True)

                pe.wait_ge(s_in, 6 * 16)
                for step in order:
                    kind = step[0]
                    if kind == "st":
                        s = step[1]
                        sl = slots[s]
                        n, u, p, c = sl["n"], sl["u"], sl["p"], sl["c"]
                        a = ATT[u]
                        if s == quads[n]["start"]:
                            taken(pe, ("mtr", n))
                        if s >= N_ST:
                            pe.wait_ge(S["probs_ready"], slot_value("probs_ready", s - N_ST))
                        kr = chunk_rows(a["nk"], c)
                        for i, h in enumerate(sl["heads"]):
                            mm = pe.matmul(st_ps[s % N_ST][0:kr, i * a["nq"]:(i + 1) * a["nq"]],
                                           key_op(n, h)[:, c * P:c * P + kr], query_op(u, p)[:, h // of(u), :],
                                           start=True, stop=True)
                        mm.then_inc(S["scores_full"], 1)
                    elif kind == "max":
                        _, n, i = step
                        u, p = quads[n]["u"], quads[n]["p"]
                        a = ATT[u]
                        t, rows, heads = quads[n]["items"][i]
                        if i == 0:
                            last = [s for s in order if s[0] == "q_tr" and s[1] == u and s[2] == p][-1]
                            taken(pe, last)
                            pe.wait_ge(ring_in[n % RING], 16 * ring_dmas[n])
                        o = value["max_full", step] - 1
                        if o >= N_MX:
                            pe.wait_ge(S["max_taken"], o - N_MX + 1)
                        tt = 0 if t == TQ else t
                        for j, h in enumerate(heads):
                            mm = pe.matmul(mx_ps[o % N_MX][0:rows, j * a["nk"]:(j + 1) * a["nk"]],
                                           query_op(u, p)[:, h // of(u), tt * P:tt * P + rows],
                                           key_op(n, h)[:, 0:a["nk"]], start=True, stop=True)
                        mm.then_inc(S["max_full"], 1)
                    elif kind == "mtr":
                        n = step[1]
                        u, p, qd = quads[n]["u"], quads[n]["p"], quads[n]["qd"]
                        a = ATT[u]
                        bank, full = take(step)
                        pe.wait_ge(S["negm_ready"], value["negm_ready", ("negm", n)])
                        gs = range(4 * qd // of(u), (4 * qd + 4) // of(u))
                        for k, g in enumerate(gs):
                            for i, (t, rows) in enumerate(q_tiles(u)):
                                mm = pe.matmul(bank[:, k * a["nq"] + i * P:k * a["nq"] + i * P + rows],
                                               query_stack(u, p)[0:rows, t, g * of(u):(g + 1) * of(u), :].rearrange("p h s -> p (h s)"),
                                               identr[0:rows, 0:rows], start=True, stop=True)
                        mm.then_inc(full, 1)
                    elif kind == "pv":
                        _, n, c = step
                        u, p, qd = quads[n]["u"], quads[n]["p"], quads[n]["qd"]
                        a = ATT[u]
                        mine = [s for s in quads[n]["slots"] if slots[s]["c"] == c]
                        if c == 0 and n:
                            pe.wait_ge(S["out_taken"], n)
                        pe.wait_ge(S["probs_ready"], slot_value("probs_ready", mine[-1]))
                        if c == 0 and qd == 0:
                            last = [s for s in order if s[0] in ("kv_proj", "qkv_proj", "x_keys") and
                                    (s[1:3] == (u, p) if s[0] != "x_keys" else (u == 4 and s[1] == p))][-1]
                            pe.wait_ge(S["k_high"], value["k_high", last])
                        kr = chunk_rows(a["nk"], c)
                        for s in mine:
                            for i, h in enumerate(slots[s]["heads"]):
                                j = h % 4
                                v = v20[p][0:kr, c, h, :] if a["dh"] == 8 else v8[p][0:kr, c + (4 if u == 4 else 0), h, :]
                                mm = pe.matmul(pv_ps[32 * j:32 * j + a["dh"] + 1, 0:a["nq"]], v,
                                               probs[0:kr, s % N_P, i * a["nq"]:(i + 1) * a["nq"]],
                                               start=(c == 0), stop=(c == -(-a["nk"] // P) - 1), tile_position=(0, 32 * j))
                            if s == mine[-1] and c == -(-a["nk"] // P) - 1:
                                mm.then_inc(S["out_full"], 1)
                            else:
                                mm.then_inc(s_used, 1)
                    elif kind == "ctx_tr":
                        p = step[1]
                        bank, full = take(step)
                        for t in range(4):
                            mm = pe.transpose(bank[0:C, t * P:(t + 1) * P], ctx_n[:, p, t, :], ident[:, :])
                        mm.then_inc(full, 1)
                    elif kind == "kv_proj":
                        _, u, p, t = step
                        bank, full = take(step)
                        if t == 0:
                            taken(pe, ("ctx_tr", p))
                            if u in (2, 6):
                                pe.wait_ge(block_of(u), 48)
                        kr = chunk_rows(ATT[u]["nk"], t)
                        w = wbc[:, :] if u in (2, 6) else wc[:, W_CTX[u][0]:W_CTX[u][1]]
                        pe.matmul(bank[0:kr, 0:320], ctxT[p][:, t * P:t * P + kr], w, start=True, stop=True).then_inc(full, 1)
                    elif kind == "k_tr":
                        _, u, p, pr, gg = step
                        bank, full = take(step)
                        if u == 4:
                            pe.wait_ge(S["x_split"], value["x_split", ("x_keys", p)])
                        elif ATT[u]["kind"] == "self":
                            for t in range(2):
                                taken(pe, ("qkv_proj", u, p, t))
                        else:
                            for t in range(2):
                                taken(pe, ("kv_proj", u, p, 2 * pr + t))
                        ks = ks20 if ATT[u]["sr"] == 32 else ks8
                        ng = ATT[u]["H"] // of(u)
                        for k, g in enumerate(range(2 * gg, min(2 * gg + 2, ng))):
                            for t in range(2):
                                kr = chunk_rows(ATT[u]["nk"], 2 * pr + t)
                                mm = pe.matmul(bank[:, k * SQ + t * P:k * SQ + t * P + kr],
                                               ks[0:kr, t, g * of(u):(g + 1) * of(u), :].rearrange("p h s -> p (h s)"),
                                               identr[0:kr, 0:kr], start=True, stop=True)
                        mm.then_inc(full, 1)
                    elif kind == "h_tr":
                        _, tag, p = step
                        bank, full = take(step)
                        src = nat[p] if tag in LNS else x[p]
                        if tag in LNS:
                            pe.wait_ge(S["xn_ready"], value["xn_ready", ("ln", tag, p)])
                        elif tag == 3:
                            taken(pe, ("ff_o", "ff1", p))
                        for t in range(TQ):
                            pe.transpose(bank[:, t * P:(t + 1) * P], src[:, t, 0:P], ident[:, :])
                            mm = pe.matmul(bank[0:D2, SQ + t * P:SQ + (t + 1) * P], src[:, t, P:D], ident[:, :], start=True, stop=True)
                        mm.then_inc(full, 1)
                    elif kind == "q_proj":
                        _, u, p = step
                        bank, full = take(step)
                        taken(pe, ("h_tr", u, p))
                        if u in (0, 3):
                            w, w2 = (wm[:, slice(*W_MAIN[f"q{u}"])], wm2[:, slice(*W_MAIN[f"q{u}"])])
                        else:
                            w, w2 = wb[:, wts("q2")], wb2[:, wts("q2")]
                        for t in range(TQ):
                            ts = slice(t * P, (t + 1) * P)
                            mm = two_part(bank[:, t * D:(t + 1) * D], hT[p][:, ts], hT2[p][:, ts], w, w2)
                        mm.then_inc(full, 1)
                    elif kind == "qkv_proj":
                        _, u, p, t = step
                        bank, full = take(step)
                        taken(pe, ("h_tr", u, p))
                        pe.wait_ge(block_of(u), 48)
                        ts = slice(t * P, (t + 1) * P)
                        two_part(bank[:, 0:480], hT[p][:, ts], hT2[p][:, ts], wb[:, wts("qkv")], wb2[:, wts("qkv")]).then_inc(full, 1)
                    elif kind == "ca_q":
                        p = step[1]
                        bank, full = take(step)
                        pe.matmul(bank[0:C, 0:D], ca_n[p][:, :], wqca[:, :], start=True, stop=True).then_inc(full, 1)
                    elif kind == "q_tr":
                        _, u, p, gg = step
                        bank, full = take(step)
                        if ATT[u]["kind"] == "self":
                            for t in range(TQ):
                                taken(pe, ("qkv_proj", u, p, t))
                        else:
                            taken(pe, ("ca_q", p) if u == 4 else ("q_proj", u, p))
                        if gg == 0:
                            pe.wait_ge(S["m_zeroed"], value["m_zeroed", ("m_zero", u, p)])
                        ng = ATT[u]["H"] // of(u)
                        nq = ATT[u]["nq"]
                        for k, g in enumerate(range(4) if u == 4 else range(2 * gg, min(2 * gg + 2, ng))):
                            for i, (t, rows) in enumerate(q_tiles(u)):
                                mm = pe.matmul(bank[:, k * nq + i * P:k * nq + i * P + rows],
                                               query_stack(u, p)[0:rows, t, g * of(u):(g + 1) * of(u), :].rearrange("p h s -> p (h s)"),
                                               identr[0:rows, 0:rows], start=True, stop=True)
                        mm.then_inc(full, 1)
                    elif kind == "o_nat":
                        _, u, p, i = step
                        bank, full = take(step)
                        last = [q["n"] for q in quads if q["u"] == u and q["p"] == p][-1]
                        pe.wait_ge(S["out_taken"], last + 1)
                        for k, (qd, t, rows) in enumerate(parts_of(u, i)):
                            src = oTc[p][:, qd, :] if u == 4 else oT[p][:, qd, t * P:(t + 1) * P]
                            mm = pe.transpose(bank[0:rows, k * P:(k + 1) * P], src, ident[:, :])
                        mm.then_inc(full, 1)
                    elif kind == "o_tr":
                        _, u, p = step
                        bank, full = take(step)
                        for i in range(1 if u == 3 else 3):
                            taken(pe, ("o_nat", u, p, i))
                        for t in range(TQ):
                            pe.transpose(bank[:, t * P:(t + 1) * P], nat[p][:, t, 0:P], ident[:, :])
                            mm = pe.matmul(bank[0:D2, SQ + t * P:SQ + (t + 1) * P], nat[p][:, t, P:D], ident[:, :], start=True, stop=True)
                        mm.then_inc(full, 1)
                    elif kind == "o_proj":
                        _, u, p = step
                        bank, full = take(step)
                        taken(pe, ("c_o", p) if u == 3 else ("o_tr", u, p))
                        if u in (0, 3):
                            w, w2 = (wm[:, slice(*W_MAIN[f"o{u}"])], wm2[:, slice(*W_MAIN[f"o{u}"])])
                        else:
                            name = "o1" if u in (1, 5) else "o2"
                            w, w2 = wb[:, wts(name)], wb2[:, wts(name)]
                        for t in range(TQ):
                            ts = slice(t * P, (t + 1) * P)
                            mm = two_part(bank[:, t * D:(t + 1) * D], hT[p][:, ts], hT2[p][:, ts], w, w2)
                        mm.then_inc(full, 1)
                    elif kind in ("ff_g", "ff_a"):
                        _, tag, p, i = step
                        bank, full = take(step)
                        taken(pe, ("h_tr", tag, p))
                        for k, m in enumerate(range(2 * i, min(2 * i + 2, FC))):
                            lo = (FF if kind == "ff_g" else 0) + m * P
                            mm = two_part(bank[:, k * SQ:(k + 1) * SQ], wb[:, wts("w1", lo, lo + P)], wb2[:, wts("w1", lo, lo + P)],
                                          hT[p][:, :], hT2[p][:, :])
                        mm.then_inc(full, 1)
                    elif kind == "ff_o":
                        _, tag, p = step
                        bank, full = take(step)
                        for i in (1, 2):
                            taken(pe, ("ff_a", tag, p, i))
                        for t in range(TQ):
                            for m in range(FC):
                                mm = pe.matmul(bank[:, t * D:(t + 1) * D], gate[:, m, t * P:(t + 1) * P],
                                               wb[:, 2240 + m * D:2240 + (m + 1) * D], start=(m == 0), stop=(m == FC - 1))
                        mm.then_inc(full, 1)
                    elif kind == "ca_kv":
                        p = step[1]
                        bank, full = take(step)
                        wk = W_CTX["ca"][0]
                        pe.matmul(bank[:, 0:NCA], wc[:, wk:wk + P], ctxT[p][:, NENC:SK], start=True, stop=True)
                        pe.matmul(bank[0:D2, 8:8 + NCA], wc[:, wk + P:wk + D], ctxT[p][:, NENC:SK], start=True, stop=True)
                        pe.matmul(bank[0:32, 64:64 + D], caT8[p][:, :], wc[:, wk + D:wk + 2 * D], start=True, stop=True).then_inc(full, 1)
                    elif kind == "c_tr":
                        p = step[1]
                        bank, full = take(step)
                        taken(pe, ("o_nat", 4, p, 0))
                        pe.transpose(bank[:, 0:C], natc[p][:, 0:P], ident[0:C, 0:C])
                        pe.matmul(bank[0:D2, P:P + C], natc[p][:, P:D], ident[0:C, 0:C], start=True, stop=True).then_inc(full, 1)
                    elif kind == "c_q":
                        bank, full = take(step)
                        taken(pe, ("c_tr", step[1]))
                        a = W_MAIN["q3"][0]
                        two_part(bank[:, 0:C], wm[:, a:a + P], wm2[:, a:a + P], cT[:, :], cT2[:, :])
                        two_part(bank[0:D2, P:P + C], wm[:, a + P:a + D], wm2[:, a + P:a + D], cT[:, :], cT2[:, :]).then_inc(full, 1)
                    elif kind == "c_s":
                        p = step[1]
                        bank, full = take(step)
                        taken(pe, ("c_q", p))
                        taken(pe, ("ca_kv", p))
                        two_part(bank[0:C, 0:32], cq[:, :], cq2[:, :], kbd[p][:, :], kbd2[p][:, :]).then_inc(full, 1)
                    elif kind == "c_p":
                        p = step[1]
                        bank, full = take(step)
                        pe.wait_ge(S["c_probs"], value["c_probs", ("c_s", p)])
                        pe.matmul(bank[0:32, 0:SQ], cs[:, :], spread[:, :], start=True, stop=True).then_inc(full, 1)
                    elif kind == "c_o":
                        p = step[1]
                        bank, full = take(step)
                        taken(pe, ("c_p", p))
                        pe.matmul(bank[:, 0:SQ], vbd[p][:, 0:P], cpT[:, :], start=True, stop=True)
                        pe.matmul(bank[0:D2, SQ:2 * SQ], vbd[p][:, P:D], cpT[:, :], start=True, stop=True).then_inc(full, 1)

            def filled(eng, step):
                b, k = turn[step]
                eng.wait_ge(spare_full[b], k + 1)
                return sp_ps[b], spare_taken[b]

            def high_slots(stack, t0, t1, rows, dh, which):
                step = 2 * dh if which == "k" else dh
                v = stack[0:rows, t0:t1, :, 0:3 * dh].rearrange("p t h (s d) -> p (t h) s d", s=3)
                return v[:, :, 0:3:2, :] if which == "k" else v[:, :, 0:2, :]

            @block.scalar
            def _(act):
                def split_high(stack, t0, t1, rows, dh, which, src):
                    out = high_slots(stack, t0, t1, rows, dh, which)
                    n = (t1 - t0) * (D // dh)
                    v = src.rearrange("p (h d) -> p h d", d=dh).unsqueeze(2).broadcast_to([rows, n, 2, dh])
                    return nc.scalar.activation(out, v, ACT.Copy)

                for step in order:
                    kind = step[0]
                    if kind == "st":
                        s = step[1]
                        a = ATT[slots[s]["u"]]
                        act.wait_ge(S["scores_full"], s + 1)
                        if s >= N_P:
                            act.wait_ge(*used_after[s - N_P])
                        kr = chunk_rows(a["nk"], slots[s]["c"])
                        w = a["hps"] * a["nq"]
                        nc.scalar.activation(probs[0:kr, s % N_P, 0:w], st_ps[s % N_ST][0:kr, 0:w], ACT.Exp,
                                             scale=float(a["dh"]) ** -0.5).then_inc(S["probs_ready"], 1)
                    elif kind == "oev":
                        n = step[1]
                        u, p, qd = quads[n]["u"], quads[n]["p"], quads[n]["qd"]
                        act.wait_ge(S["out_full"], n + 1)
                        dst = oTc[p][:, qd, :] if u == 4 else oT[p][:, qd, :]
                        nc.scalar.activation(dst, pv_ps[:, 0:ATT[u]["nq"]], ACT.Copy).then_inc(S["out_taken"], 1)
                    elif kind == "ctx_tr":
                        p = step[1]
                        bank, free = filled(act, step)
                        nc.scalar.activation(caT8[p][:, :].rearrange("p (h k) -> p h k", h=8),
                                             bank[0:C, NENC:SK].unsqueeze(1).broadcast_to([C, 8, NCA]), ACT.Copy)
                        nc.scalar.activation(ctxT[p][:, :], bank[0:C, :], ACT.Copy).then_inc(free, 1)
                    elif kind == "kv_proj":
                        _, u, p, t = step
                        dh = ATT[u]["dh"]
                        bank, free = filled(act, step)
                        kr = chunk_rows(ATT[u]["nk"], t)
                        ks, v = (ks20, v20[p]) if dh == 8 else (ks8, v8[p])
                        split_high(ks, t % 2, t % 2 + 1, kr, dh, "k", bank[0:kr, 0:D])
                        nc.scalar.activation(v[0:kr, t, :, 0:dh], bank[0:kr, D:2 * D].rearrange("p (h d) -> p h d", d=dh),
                                             ACT.Copy).then_inc(S["k_high"], 1)
                    elif kind == "qkv_proj":
                        _, u, p, t = step
                        bank, free = filled(act, step)
                        split_high(ks20, t, t + 1, P, 8, "k", bank[:, D:2 * D])
                        split_high(qs20[p], t, t + 1, P, 8, "q", bank[:, 0:D])
                        nc.scalar.activation(v20[p][:, t, :, 0:8], bank[:, 2 * D:3 * D].rearrange("p (h d) -> p h d", d=8),
                                             ACT.Copy).then_inc(S["k_high"], 1)
                    elif kind == "x_keys":
                        p = step[1]
                        taken(act, ("ff_o", "ff1", p))
                        prev = [s for s in order[:order.index(step)] if s[0] == "k_tr"][-1]
                        act.wait_ge(spare_full[turn[prev][0]], turn[prev][1] + 1)
                        split_high(ks8, 0, TQ, P, 20, "k", x[p][:, :, :].rearrange("p t d -> p (t d)"))
                        nc.scalar.activation(v8[p][:, 4:6, :, 0:20].rearrange("p t h d -> p (t h) d"),
                                             x[p][:, :, :].rearrange("p t (h d) -> p (t h) d", d=20), ACT.Copy).then_inc(S["k_high"], 1)
                    elif kind == "k_tr":
                        _, u, p, pr, gg = step
                        bank, free = filled(act, step)
                        ng = ATT[u]["H"] // of(u)
                        n = min(2, ng - 2 * gg)
                        w = chunk_rows(ATT[u]["nk"], 2 * pr) + chunk_rows(ATT[u]["nk"], 2 * pr + 1)
                        if u == 4:
                            dst = (oT[p][:, 2:4, :] if gg == 0 else kdense[p][:, 4, :].rearrange("p (g k) -> p g k", g=2))
                        else:
                            dst = kdense[p][:, 2 * gg:2 * gg + n, pr * SQ:pr * SQ + w]
                        nc.scalar.activation(dst, bank[:, 0:n * SQ].rearrange("p (g k) -> p g k", g=n)[:, :, 0:w], ACT.Copy).then_inc(free, 1)
                    elif kind == "h_tr":
                        _, tag, p = step
                        bank, free = filled(act, step)
                        if tag in LNS:
                            c = 2 * LNS[tag]
                            nc.scalar.activation(hT[p][:, :], bank[:, 0:SQ], ACT.Identity, scale=cols[:, c:c + 1], bias=cols[:, c + 1:c + 2])
                            nc.scalar.activation(hT2[p][:, :], bank[0:D2, SQ:2 * SQ], ACT.Identity, scale=cols2[:, c:c + 1], bias=cols2[:, c + 1:c + 2]).then_inc(free, 1)
                        else:
                            nc.scalar.activation(hT[p][:, :], bank[:, 0:SQ], ACT.Copy)
                            nc.scalar.activation(hT2[p][:, :], bank[0:D2, SQ:2 * SQ], ACT.Copy).then_inc(free, 1)
                    elif kind == "o_tr":
                        p = step[2]
                        bank, free = filled(act, step)
                        nc.scalar.activation(hT[p][:, :], bank[:, 0:SQ], ACT.Copy)
                        nc.scalar.activation(hT2[p][:, :], bank[0:D2, SQ:2 * SQ], ACT.Copy).then_inc(free, 1)
                    elif kind in ("c_tr", "c_q"):
                        bank, free = filled(act, step)
                        dst, dst2 = (cT, cT2) if kind == "c_tr" else (cq, cq2)
                        nc.scalar.activation(dst[:, :], bank[:, 0:C], ACT.Copy)
                        nc.scalar.activation(dst2[:, :], bank[0:D2, P:P + C], ACT.Copy).then_inc(free, 1)
                    elif kind == "c_p":
                        bank, free = filled(act, step)
                        nc.scalar.activation(cpT[:, :], bank[0:32, 0:SQ], ACT.Copy).then_inc(free, 1)
                    elif kind == "q_proj":
                        _, u, p = step
                        bank, free = filled(act, step)
                        dh = ATT[u]["dh"]
                        split_high(query_stack(u, p), 0, TQ, P, dh, "q", bank[:, 0:TQ * D]).then_inc(S["q_high"], 1)
                    elif kind == "ca_q":
                        p = step[1]
                        bank, free = filled(act, step)
                        split_high(qs8[p], TQ, TQ + 1, C, 20, "q", bank[0:C, 0:D]).then_inc(S["q_high"], 1)
                    elif kind == "q_tr":
                        _, u, p, gg = step
                        bank, free = filled(act, step)
                        if u == 4:
                            dst, w = qTc[p][:, :, :].rearrange("p g q -> p (g q)"), 4 * C
                        else:
                            n = min(2, ATT[u]["H"] // of(u) - 2 * gg)
                            dst, w = qT[p][:, 2 * gg:2 * gg + n, :].rearrange("p g q -> p (g q)"), n * SQ
                        nc.scalar.activation(dst, bank[:, 0:w], ACT.Copy).then_inc(free, 1)
                    elif kind == "ff_g":
                        _, tag, p, i = step
                        bank, free = filled(act, step)
                        for k, m in enumerate(range(2 * i, min(2 * i + 2, FC))):
                            c = 12 + (0 if tag == "ff1" else 10) + FC + m
                            ins = nc.scalar.activation(gate[:, m, :], bank[:, k * SQ:(k + 1) * SQ], ACT.Identity, bias=cols[:, c:c + 1])
                        ins.then_inc(free, 1)
                    elif kind == "gelu":
                        _, tag, p = step
                        for i in (1, 2):
                            taken(act, ("ff_g", tag, p, i))
                        nc.scalar.activation(gate[:, :, :], gate[:, :, :], ACT.Gelu).then_inc(S["gate_ready"], 1)
                    elif kind == "c_s":
                        taken(act, step)
                        nc.scalar.activation(cs[:, :], cs[:, :], ACT.Exp, scale=20.0 ** -0.5).then_inc(S["c_exp"], 1)

            @block.vector
            def _(dve):
                links = [0]

                def link(ins):
                    links[0] += 1
                    ins.then_inc(dve_link, 1)
                    dve.wait_ge(dve_link, links[0])

                def split_low(stack, t0, t1, rows, dh, which, src):
                    lo = dh if which == "k" else 2 * dh
                    high = stack[0:rows, t0:t1, :, 0:dh].rearrange("p t h d -> p (t h) d").bitcast(F32)
                    out = stack[0:rows, t0:t1, :, lo:lo + dh].rearrange("p t h d -> p (t h) d")
                    return nc.vector.tensor_tensor(out, src.rearrange("p (h d) -> p h d", d=dh), high, ALU.subtract)

                for step in order:
                    kind = step[0]
                    if kind == "max":
                        _, n, i = step
                        u, p = quads[n]["u"], quads[n]["p"]
                        a = ATT[u]
                        t, rows, heads = quads[n]["items"][i]
                        o = value["max_full", step]
                        dve.wait_ge(S["max_full"], o)
                        nc.vector.tensor_reduce(mx[p][0:rows, t, heads[0]:heads[-1] + 1],
                                                mx_ps[(o - 1) % N_MX][0:rows, 0:a["hpm"] * a["nk"]].rearrange("p (h k) -> p h k", k=a["nk"]),
                                                AX.X, ALU.max).then_inc(S["max_taken"], 1)
                    elif kind == "negm":
                        n = step[1]
                        u, p, qd = quads[n]["u"], quads[n]["p"], quads[n]["qd"]
                        dh = ATT[u]["dh"]
                        tiles = q_tiles(u)
                        t0, t1, rows = tiles[0][0], tiles[-1][0] + 1, tiles[0][1]
                        dve.wait_ge(S["max_taken"], value["max_taken", ("max", n, len(quads[n]["items"]) - 1)])
                        m = mx[p][0:rows, t0:t1, 4 * qd:4 * qd + 4]
                        st = query_stack(u, p)[0:rows, t0:t1, 4 * qd:4 * qd + 4, :]
                        link(nc.vector.tensor_scalar(st[:, :, :, 3 * dh], m, -1.0, None, ALU.mult))
                        nc.vector.scalar_tensor_tensor(out=st[:, :, :, 3 * dh + 1], in0=m, scalar=-1.0,
                                                       in1=st[:, :, :, 3 * dh].bitcast(F32),
                                                       op0=ALU.mult, op1=ALU.subtract).then_inc(S["negm_ready"], 1)
                    elif kind == "mtr":
                        n = step[1]
                        u, p, qd = quads[n]["u"], quads[n]["p"], quads[n]["qd"]
                        bank, done = filled(dve, step)
                        g0, g1 = 4 * qd // of(u), (4 * qd + 4) // of(u)
                        nq = ATT[u]["nq"]
                        nc.vector.tensor_copy(query_op(u, p)[:, g0:g1, :].rearrange("p g q -> p (g q)"),
                                              bank[:, 0:(g1 - g0) * nq]).then_inc(done, 1)
                    elif kind == "kv_proj":
                        _, u, p, t = step
                        bank, done = filled(dve, step)
                        dve.wait_ge(S["k_high"], value["k_high", step])
                        kr = chunk_rows(ATT[u]["nk"], t)
                        ks = ks20 if ATT[u]["dh"] == 8 else ks8
                        split_low(ks, t % 2, t % 2 + 1, kr, ATT[u]["dh"], "k", bank[0:kr, 0:D]).then_inc(done, 1)
                    elif kind == "qkv_proj":
                        _, u, p, t = step
                        bank, done = filled(dve, step)
                        dve.wait_ge(S["k_high"], value["k_high", step])
                        split_low(ks20, t, t + 1, P, 8, "k", bank[:, D:2 * D])
                        split_low(qs20[p], t, t + 1, P, 8, "q", bank[:, 0:D]).then_inc(done, 1)
                    elif kind == "x_keys":
                        p = step[1]
                        dve.wait_ge(S["k_high"], value["k_high", step])
                        split_low(ks8, 0, TQ, P, 20, "k", x[p][:, :, :].rearrange("p t d -> p (t d)")).then_inc(S["x_split"], 1)
                    elif kind in ("q_proj", "ca_q"):
                        p = step[-1]
                        bank, done = filled(dve, step)
                        dve.wait_ge(S["q_high"], value["q_high", step])
                        if kind == "ca_q":
                            split_low(qs8[p], TQ, TQ + 1, C, 20, "q", bank[0:C, 0:D]).then_inc(done, 1)
                        else:
                            u = step[1]
                            split_low(query_stack(u, p), 0, TQ, P, ATT[u]["dh"], "q", bank[:, 0:TQ * D]).then_inc(done, 1)
                    elif kind == "ln":
                        _, tag, p = step
                        taken(dve, (*ROWS_FROM[tag], p))
                        nc.vector.bn_stats(stats[:, 0, :], x[p][:, 0, :])
                        link(nc.vector.bn_stats(stats[:, 1, :], x[p][:, 1, :]))
                        nc.vector.bn_aggr(mv[:, 0, :], stats[:, 0, :])
                        nc.vector.bn_aggr(mv[:, 1, :], stats[:, 1, :]).then_inc(S["var_ready"], 1)
                        dve.wait_ge(S["rstd_ready"], value["rstd_ready", step])
                        for t in range(TQ):
                            ins = nc.vector.tensor_scalar(nat[p][:, t, :], x[p][:, t, :], mv[:, t, 0:1], rstd[:, t:t + 1],
                                                          ALU.subtract, ALU.mult)
                        ins.then_inc(S["xn_ready"], 1)
                    elif kind == "o_nat":
                        _, u, p, i = step
                        bank, done = filled(dve, step)
                        parts = parts_of(u, i)
                        rows, dh, nh = parts[0][2], ATT[u]["dh"], 4 * len(parts)
                        v = bank[0:rows, 0:nh * 32].rearrange("p (h s) -> p h s", s=32)
                        k = 3 if u == 4 else i
                        link(nc.vector.reciprocal(rinv[0:rows, k, 0:nh], v[:, :, dh]))
                        inv = rinv[0:rows, k, 0:nh].unsqueeze(2).broadcast_to([rows, nh, dh])
                        if u == 4:
                            out = natc[p][:, :].rearrange("p (h d) -> p h d", d=dh)
                        elif u == 3:
                            out = nat[p][:, :, :].rearrange("p t (h d) -> p (t h) d", d=dh)
                        elif i < 2:
                            out = nat[p][:, i, 0:P].rearrange("p (h d) -> p h d", d=dh)
                        if u in (3, 4) or i < 2:
                            nc.vector.tensor_tensor(out, v[:, :, 0:dh], inv, ALU.mult).then_inc(done, 1)
                        else:
                            for t in range(TQ):
                                ins = nc.vector.tensor_tensor(nat[p][:, t, P:D].rearrange("p (h d) -> p h d", d=dh),
                                                              v[:, 4 * t:4 * t + 4, 0:dh], inv[:, 4 * t:4 * t + 4, :], ALU.mult)
                            ins.then_inc(done, 1)
                    elif kind in ("o_proj", "ff_o"):
                        _, u, p = step
                        bank, done = filled(dve, step)
                        dve.wait_ge(S["x_biased"], value["x_biased", ("x_bias", u, p)])
                        nc.vector.tensor_tensor(x[p][:, :, :].rearrange("p t d -> p (t d)"), bank[:, 0:TQ * D],
                                                xb[p][:, :, :].rearrange("p t d -> p (t d)"), ALU.add).then_inc(done, 1)
                    elif kind == "ff_a":
                        _, tag, p, i = step
                        bank, done = filled(dve, step)
                        dve.wait_ge(S["gate_ready"], value["gate_ready", ("gelu", tag, p)])
                        for k, m in enumerate(range(2 * i, min(2 * i + 2, FC))):
                            c = 12 + (0 if tag == "ff1" else 10) + m
                            ins = nc.vector.scalar_tensor_tensor(out=gate[:, m, :], in0=bank[:, k * SQ:(k + 1) * SQ],
                                                                 scalar=cols[:, c:c + 1], in1=gate[:, m, :],
                                                                 op0=ALU.add, op1=ALU.mult)
                        ins.then_inc(done, 1)
                    elif kind == "ca_kv":
                        p = step[1]
                        bank, done = filled(dve, step)
                        for dst, mask, k in ((kbd[p], kmask, bank[:, 0:NCA]), (kbd2[p], kmask2, bank[0:D2, 8:8 + NCA])):
                            rows = mask.shape[0]
                            nc.vector.tensor_tensor(dst[:, :].rearrange("p (h k) -> p h k", h=8),
                                                    k.unsqueeze(1).broadcast_to([rows, 8, NCA]),
                                                    mask[:, :].rearrange("p (h k) -> p h k", h=8), ALU.mult)
                        nc.vector.tensor_tensor(vbd[p][:, :], bank[0:32, 64:64 + D], vmask[:, :], ALU.mult).then_inc(done, 1)
                    elif kind == "c_s":
                        bank, done = filled(dve, step)
                        v = bank[0:C, 0:32].rearrange("p (h k) -> p h k", h=8)
                        cv = cs[:, :].rearrange("p (h k) -> p h k", h=8)
                        spread_h = cmax[:, :].unsqueeze(2).broadcast_to([C, 8, NCA])
                        link(nc.vector.tensor_reduce(cmax[:, :], v, AX.X, ALU.max))
                        nc.vector.tensor_tensor(cv, v, spread_h, ALU.subtract).then_inc(done, 1)
                        dve.wait_ge(S["c_exp"], value["c_exp", step])
                        link(nc.vector.tensor_reduce(cmax[:, :], cv, AX.X, ALU.add))
                        link(nc.vector.reciprocal(cmax[:, :], cmax[:, :]))
                        nc.vector.tensor_tensor(cv, cv, spread_h, ALU.mult).then_inc(S["c_probs"], 1)
                    elif kind == "c_o":
                        p = step[1]
                        bank, done = filled(dve, step)
                        taken(dve, ("o_tr", 3, p))
                        nc.vector.tensor_tensor(hT[p][:, :], bank[:, 0:SQ], hT[p][:, :], ALU.add)
                        nc.vector.tensor_tensor(hT2[p][:, :], bank[0:D2, SQ:2 * SQ], hT2[p][:, :], ALU.add).then_inc(done, 1)

            @block.gpsimd
            def _(pool):
                links = 0
                pool.wait_ge(s_in, 6 * 16)
                for step in order:
                    kind = step[0]
                    if kind == "ln":
                        pool.wait_ge(S["var_ready"], value["var_ready", step])
                        links += 1
                        nc.gpsimd.tensor_scalar(rstd[:, :], mv[:, :, 1], EPS, None, ALU.add).then_inc(pool_link, 1)
                        pool.wait_ge(pool_link, links)
                        nc.gpsimd.tensor_tensor(rstd[:, :], rstd[:, :], halfpow[:, :], ALU.pow).then_inc(S["rstd_ready"], 1)
                    elif kind == "x_bias":
                        _, tag, p = step
                        if tag != 0:
                            taken(pool, (*ROWS_FROM[tag], p))
                        c = BIAS[tag] * D
                        nc.gpsimd.tensor_tensor(xb[p][:, :, :], x[p][:, :, :],
                                                bias[:, c:c + D].unsqueeze(1).broadcast_to([P, TQ, D]), ALU.add).then_inc(S["x_biased"], 1)
                    elif kind == "m_zero":
                        _, u, p = step
                        before = [q["n"] for q in quads if q["p"] == p and ATT[q["u"]]["sr"] == ATT[u]["sr"] and
                                  q["ph"] < [q2["ph"] for q2 in quads if q2["u"] == u][0]]
                        if before:
                            taken(pool, ("mtr", before[-1]))
                        tiles = q_tiles(u)
                        dh = ATT[u]["dh"]
                        nc.gpsimd.memset(query_stack(u, p)[:, tiles[0][0]:tiles[-1][0] + 1, :, 3 * dh:3 * dh + 2].bitcast(F32), 0.0).then_inc(S["m_zeroed"], 1)

            turn_block.__exit__(None, None, None)
            with nc.Block() as block:
                @block.sync
                def _(sp):
                    for s in per_turn:
                        sp.sem_clear(s)


def kernel(**inputs):
    import concourse.bacc as bacc
    from concourse.bass_utils import run_bass_kernel_spmd

    w = {k: np.asarray(v) for k, v in inputs.items()}
    blocks = ("L1_xattn_", "L3_xattn_")
    ln_names = [b + n for b in blocks for n in ("n1", "n2", "n3")]
    mains = [w["L0_xattn_Wq"], w["L0_xattn_Wo"], w["L2_xattn_Wq"], w["L2_xattn_Wout"]]
    wide = [np.concatenate([w[b + n] for n in ("q1", "k1", "v1", "o1_w", "q2", "o2_w", "ff_w1")], axis=1) for b in blocks]
    down = [w[b + "ff_w2"].reshape(FC, P, D).transpose(1, 0, 2).reshape(P, FC * D) for b in blocks]
    idx = np.linspace(0, C - 1, SQ).astype(np.int64)
    head = np.arange(D) // 20
    kmask = np.repeat((head[:, None] == np.arange(8)[None, :]).astype(np.float32), NCA, axis=1)
    arrays = {
        "x": w["x"], "ctx": w["ctx_768"],
        "w_main": np.concatenate([m[:P] for m in mains], axis=1),
        "w_main2": np.concatenate([m[P:] for m in mains], axis=1),
        "w_blk": np.stack([np.concatenate([a[:P], d], axis=1) for a, d in zip(wide, down)]),
        "w_blk2": np.stack([a[P:] for a in wide]),
        "w_blkc": np.stack([np.concatenate([w[b + "k2"], w[b + "v2"]], axis=1) for b in blocks]),
        "w_ctx": np.concatenate([w["L0_xattn_Wk"], w["L0_xattn_Wv"], w["L2_xattn_Wk"], w["L2_xattn_Wv"],
                                 w["L2_xattn_Wk_ca"], w["L2_xattn_Wv_ca"]], axis=1),
        "w_qca": w["L2_xattn_Wq_ca"],
        "cols": np.concatenate([np.stack([w[n + s][:P] for n in ln_names for s in ("_g", "_b")], axis=1)]
                               + [w[b + "ff_b1"].reshape(2 * FC, P).T for b in blocks], axis=1),
        "cols2": np.stack([w[n + s][P:] for n in ln_names for s in ("_g", "_b")], axis=1),
        "bias": np.concatenate([w[n] for n in (
            "L0_xattn_bo", "L1_xattn_o1_b", "L1_xattn_o2_b", "L1_xattn_ff_b2", "L2_xattn_b_out", "L3_xattn_o1_b",
            "L3_xattn_o2_b", "L3_xattn_ff_b2")])[None, :],
        "ident": np.eye(P, dtype=np.float32),
        "spread": (np.arange(C)[:, None] == idx[None, :]).astype(np.float32),
        "kmask": kmask[:P], "kmask2": kmask[P:],
        "vmask": kmask.T,
    }
    nc = bacc.Bacc("TRN2", target_bir_lowering=False, num_devices=1)
    arrays = {k: np.ascontiguousarray(v) for k, v in arrays.items()}
    io = {k: nc.dram_tensor("in_" + k, v.shape, mybir.dt.from_np(v.dtype), kind="ExternalInput").ap() for k, v in arrays.items()}
    io["out"] = nc.dram_tensor("out_rows", (B, SQ, D), F32, kind="ExternalOutput").ap()
    build(nc, io)
    r = run_bass_kernel_spmd(nc, [{"in_" + k: v for k, v in arrays.items()}], core_ids=[0])
    return r.results[0]["out_rows"]
```

```python
from contextlib import ExitStack

import numpy as np

import concourse.bass as bass
from concourse import mybir

F32 = mybir.dt.float32
FR = mybir.dt.float32r
ALU = mybir.AluOpType
ACT = mybir.ActivationFunctionType
AX = mybir.AxisListType

B, SQ, D = 4, 256, 160
SK, C = 512, 96
P = 128
TQ = SQ // P
D2 = D - P
FF = 4 * D
FC = FF // P
NCA = 4
NENC = SK - NCA
EPS = 1e-5
PAIRS = B // 2

ATT = {
    0: dict(kind="cross", H=20, dh=8, sr=32, nq=SQ, nk=SK, hps=2, hpm=1),
    1: dict(kind="self", H=20, dh=8, sr=32, nq=SQ, nk=SQ, hps=2, hpm=2),
    2: dict(kind="cross", H=20, dh=8, sr=32, nq=SQ, nk=SK, hps=2, hpm=1),
    3: dict(kind="enc", H=8, dh=20, sr=64, nq=SQ, nk=NENC, hps=2, hpm=1),
    4: dict(kind="ca", H=8, dh=20, sr=64, nq=C, nk=SQ, hps=4, hpm=2),
    5: dict(kind="self", H=20, dh=8, sr=32, nq=SQ, nk=SQ, hps=2, hpm=2),
    6: dict(kind="cross", H=20, dh=8, sr=32, nq=SQ, nk=SK, hps=2, hpm=1),
}
PHASES = [(0,), (1,), (2,), (4, 3), (5,), (6,)]
N_ST = 3
N_MX = 2
N_P = 6
RING = 4
PV_LAG = 2
FIRST_W = 4
K_LEAD = 2
TAIL = 20
M_LEAD = 4

W_MAIN = {"q0": (0, 160), "o0": (160, 320), "q3": (320, 480), "o3": (480, 640)}
W_BLOCK = {"qkv": (0, 480), "o1": (480, 640), "q2": (640, 800), "o2": (800, 960), "w1": (960, 2240)}
W_CTX = {0: (0, 320), 3: (320, 640), "ca": (640, 960)}
BIAS = {0: 0, 1: 1, 2: 2, "ff1": 3, 3: 4, 5: 5, 6: 6, "ff3": 7}
LNS = {1: 0, 2: 1, "ff1": 2, 5: 3, 6: 4, "ff3": 5}


def chunk_rows(nk, c):
    return min(P, nk - P * c)


def q_tiles(u):
    return [(t, P) for t in range(TQ)] if ATT[u]["nq"] == SQ else [(TQ, ATT[u]["nq"])]


def merge(one, other):
    out, j = [], 0
    for i, s in enumerate(one):
        out.append(s)
        while j < (i + 1) * len(other) // len(one):
            out.append(other[j])
            j += 1
    return out + other[j:]


def background(ph, b):
    def ctx_keys(u):
        s = []
        for pair in range(2):
            s += [("kv_proj", u, b, t) for t in (2 * pair, 2 * pair + 1)]
            s += [("k_tr", u, b, pair, gg) for gg in range(3 if ATT[u]["sr"] == 32 else 2)]
        return s

    def queries(u):
        n = 3 if ATT[u]["sr"] == 32 else 2
        return [("m_zero", u, b), ("q_proj", u, b)] + [("q_tr", u, b, gg) for gg in range(n)]

    def own_keys(u):
        return ([("m_zero", u, b)] + [("qkv_proj", u, b, t) for t in range(TQ)] + [("k_tr", u, b, 0, gg) for gg in range(3)]
                + [("q_tr", u, b, gg) for gg in range(3)])

    def output(u):
        return [("o_nat", u, b, i) for i in range(3)] + [("o_tr", u, b), ("o_proj", u, b)]

    def feed(tag):
        return ([("ln", tag, b), ("x_bias", tag, b), ("h_tr", tag, b)] + [("ff_g", tag, b, i) for i in range(3)] + [("gelu", tag, b)]
                + [("ff_a", tag, b, i) for i in range(3)] + [("ff_o", tag, b)])

    if ph == -1:
        return [[[("ctx_tr", b)] + ctx_keys(0), [("x_bias", 0, b), ("h_tr", 0, b)] + queries(0)]]
    if ph == 0:
        return [[output(0) + [("ln", 1, b), ("x_bias", 1, b), ("h_tr", 1, b)] + own_keys(1)]]
    if ph == 1:
        return [[output(1) + [("ln", 2, b), ("x_bias", 2, b), ("h_tr", 2, b)] + queries(2), ctx_keys(2)]]
    if ph == 2:
        return [[output(2) + feed("ff1"), [("m_zero", 4, b), ("ca_q", b), ("q_tr", 4, b, 0)] + ctx_keys(3) + [("ca_kv", b)]],
                [[("x_keys", b), ("k_tr", 4, b, 0, 0), ("k_tr", 4, b, 0, 1)], [("x_bias", 3, b), ("h_tr", 3, b)] + queries(3)]]
    if ph == 3:
        return [[[("o_nat", 4, b, 0), ("c_tr", b), ("c_q", b), ("c_s", b), ("c_p", b)], [("o_nat", 3, b, 0), ("o_tr", 3, b)]],
                [[("c_o", b), ("o_proj", 3, b), ("ln", 5, b), ("x_bias", 5, b), ("h_tr", 5, b)] + own_keys(5)]]
    if ph == 4:
        return [[output(5) + [("ln", 6, b), ("x_bias", 6, b), ("h_tr", 6, b)] + queries(6), ctx_keys(6)]]
    last = [output(6) + feed("ff3") + [("store", b)]]
    if b + 2 >= B:
        return [last]
    keys, rest = background(-1, b + 2)[0]
    return [last + [keys], [rest]]


def plan():
    quads, slots, span = [], [], {}
    for r in range(PAIRS):
        for ph, us in enumerate(PHASES):
            for b in (2 * r, 2 * r + 1):
                first = len(slots)
                for u in us:
                    a = ATT[u]
                    n_c = -(-a["nk"] // P)
                    for qd in range(a["H"] // 4):
                        n, start = len(quads), len(slots)
                        for c in range(n_c):
                            for h in range(4 * qd, 4 * qd + 4, a["hps"]):
                                slots.append(dict(n=n, u=u, b=b, c=c, heads=list(range(h, h + a["hps"])),
                                                  last=c == n_c - 1 and h + a["hps"] == 4 * qd + 4))
                        quads.append(dict(n=n, b=b, u=u, qd=qd, start=start, n_c=n_c, first=start == first,
                                          slots=list(range(start, len(slots))),
                                          items=[(t, rows, list(range(h, h + a["hpm"])))
                                                 for h in range(4 * qd, 4 * qd + 4, a["hpm"]) for t, rows in q_tiles(u)]))
                span[ph, b] = (first, len(slots))
    due = {}

    def put(s, rank, step):
        due[step] = (s, rank, len(due))

    for q in quads:
        n, s0 = q["n"], q["start"]
        w = FIRST_W if q["first"] else len(quads[n - 1]["slots"])
        hi = s0 - M_LEAD
        lo = hi - w
        m = len(q["items"])
        put(lo - K_LEAD, 0, ("kdma", n))
        for i in range(m):
            put(lo + (i * w) // m, 1, ("max", n, i))
        put(hi, 2, ("negm", n))
        put(hi + 1, 3, ("mtr", n))
        for c in range(q["n_c"]):
            last = max(s for s in q["slots"] if slots[s]["c"] == c)
            put(last + PV_LAG, 2, ("pv", n, c))
        put(q["slots"][-1] + PV_LAG, 3, ("oev", n))
    total = len(slots)
    windows = [(-80, 0, background(-1, 0), None), (0, span[0, 1][0], background(-1, 1), None)]
    for r in range(PAIRS):
        for ph in range(len(PHASES)):
            for b in (2 * r, 2 * r + 1):
                if ph + 1 < len(PHASES):
                    hi = span[ph + 1, b][0]
                else:
                    hi = span[0, b + 2][0] if r + 1 < PAIRS else total + TAIL
                windows.append((span[ph, b][1] + PV_LAG + 1, hi, background(ph, b),
                                ("oev", [q["n"] for q in quads if q["b"] == b and q["u"] in PHASES[ph]][-1])))
    stages = []
    for lo, hi, parts, after in windows:
        hi -= M_LEAD + FIRST_W + K_LEAD + 1
        steps = [s for lists in parts for s in spread_lists(lists)]
        for i, s in enumerate(steps):
            put(lo + (i * max(hi - lo, 1)) // len(steps), 4, s)
        stages += [(after, lists) for lists in parts]
    for s in range(total):
        put(s, -1, ("st", s))
    order = simulate(quads, slots, due, stages)
    return order, quads, slots


def spread_lists(lists):
    return merge(*lists) if len(lists) == 2 else lists[0]


COST = {
    "kdma": (0, [("dma", 2400)]), "max": (243, [("dve", 600)]), "negm": (0, [("dve", 160)]), "mtr": (250, [("dve", 350)]),
    "st": (238, [("act", 475)]), "pv": (524, []), "oev": (0, [("act", 264)]), "ctx_tr": (500, [("act", 600)]),
    "kv_proj": (600, [("act", 500), ("dve", 235)]), "k_tr": (250, [("act", 418)]), "q_tr": (250, [("act", 415)]),
    "q_proj": (1200, [("act", 436), ("dve", 310)]), "qkv_proj": (1800, [("act", 820), ("dve", 470)]),
    "h_tr": (730, [("act", 690)]), "o_tr": (730, [("act", 690)]), "o_nat": (500, [("dve", 320)]),
    "o_proj": (1200, [("dve", 402)]), "ln": (0, [("dve", 620), ("pool", 850), ("dve", 546)]), "x_bias": (0, [("pool", 821)]),
    "m_zero": (0, [("pool", 340)]), "x_keys": (0, [("act", 1250), ("dve", 400)]), "ff_g": (1925, [("act", 720)]),
    "ff_a": (1925, [("dve", 790)]), "gelu": (0, [("act", 3700)]), "ff_o": (3000, [("dve", 402)]), "ca_q": (300, [("act", 300), ("dve", 200)]),
    "ca_kv": (350, [("dve", 300)]), "c_tr": (300, [("act", 250)]), "c_q": (700, [("act", 250)]),
    "c_s": (130, [("dve", 150), ("act", 100), ("dve", 300)]), "c_p": (480, [("act", 260)]), "c_o": (960, [("dve", 600)]),
    "store": (0, []),
}
HANDOFF = 70
DMA_LATENCY = 2000


def simulate(quads, slots, due, stages):
    streams = [[("st", s) for s in range(len(slots))], [], [], []]
    for q in quads:
        n = q["n"]
        streams[1] += [("kdma", n)] + [("max", n, i) for i in range(len(q["items"]))] + [("negm", n)]
        streams[2].append(("mtr", n))
        streams[3] += [("pv", n, c) for c in range(q["n_c"])] + [("oev", n)]
    last_of, produced = {}, {}
    for step in due:
        if step[0] in ("k_tr", "q_tr"):
            last_of[step[:3]] = step
    pv_of = {}
    for q in quads:
        for c in range(q["n_c"]):
            for s in q["slots"]:
                if slots[s]["c"] == c:
                    pv_of[s] = ("pv", q["n"], c)

    def needs(step):
        kind = step[0]
        if kind == "kdma":
            q = quads[step[1]]
            return [last_of["k_tr", q["u"], q["b"]]] + ([("st", quads[q["n"] - RING]["slots"][-1])] if q["n"] >= RING else [])
        if kind == "max":
            q = quads[step[1]]
            return [last_of["q_tr", q["u"], q["b"]], ("kdma", q["n"])]
        if kind == "negm":
            return [("max", step[1], len(quads[step[1]]["items"]) - 1)]
        if kind == "mtr":
            return [("negm", step[1])]
        if kind == "st":
            s = step[1]
            return [("mtr", slots[s]["n"])] + ([("st", s - N_ST)] if s >= N_ST else []) + ([pv_of[s - N_P]] if s >= N_P else [])
        if kind == "pv":
            return ([("st", max(s for s in quads[step[1]]["slots"] if slots[s]["c"] == step[2]))]
                    + ([("oev", step[1] - 1)] if step[1] and step[2] == 0 else []))
        if kind == "oev":
            return [("pv", step[1], quads[step[1]]["n_c"] - 1)]
        if kind == "kv_proj":
            return [("ctx_tr", step[2])]
        if kind == "k_tr":
            u, b, pr = step[1:4]
            return [("x_keys", b)] if u == 4 else [("qkv_proj", u, b, 1)] if ATT[u]["kind"] == "self" else [("kv_proj", u, b, 2 * pr + 1)]
        if kind == "q_tr":
            u, b = step[1:3]
            return [("ca_q", b) if u == 4 else ("qkv_proj", u, b, 1) if ATT[u]["kind"] == "self" else ("q_proj", u, b), ("m_zero", u, b)]
        if kind in ("q_proj", "qkv_proj"):
            return [("h_tr", step[1], step[2])]
        if kind == "o_tr":
            return [("o_nat", step[1], step[2], i) for i in range(1 if step[1] == 3 else 3)]
        if kind == "o_proj":
            return [("c_o", step[2]) if step[1] == 3 else ("o_tr", *step[1:]), ("x_bias", *step[1:])]
        if kind == "h_tr":
            tag, b = step[1:]
            return [("ln", tag, b)] if tag in LNS else [("ff_o", "ff1", b)] if tag == 3 else []
        if kind in ("ln", "x_bias"):
            return [(*ROWS_FROM[step[1]], step[2])] if step[1] else []
        if kind in ("ff_g", "ff_a"):
            return [("h_tr", *step[1:3])]
        if kind == "gelu":
            return [("ff_g", *step[1:], i) for i in range(3)]
        if kind == "ff_o":
            return [("ff_a", *step[1:], i) for i in range(3)]
        if kind == "x_keys":
            return [("ff_o", "ff1", step[1])]
        chain = {"c_tr": ("o_nat", 4, step[1], 0), "c_q": ("c_tr", step[1]), "c_s": ("c_q", step[1]),
                 "c_p": ("c_s", step[1]), "c_o": ("c_p", step[1]), "store": ("ff_o", "ff3", step[1])}
        return [chain[kind]] if kind in chain else []

    clock = dict(pe=0, act=0, dve=0, pool=0, dma=0)
    done, order, uses, maxes = {}, [], [], []
    stages, active = list(stages), []
    heads = [list(x) for x in streams]
    while any(heads) or stages or any(active):
        if not any(active) and stages and (stages[0][0] is None or stages[0][0] in done):
            active = [list(x) for x in stages.pop(0)[1]]
        best = None
        for li in heads + active:
            if not li:
                continue
            step = li[0]
            need = needs(step)
            if any(x not in done for x in need):
                continue
            start = max([done[x] for x in need], default=0)
            if step[0] in SPARE and len(uses) > 1:
                start = max(start, done[uses[-2]])
            if step[0] == "max" and len(maxes) >= N_MX:
                start = max(start, done[maxes[-N_MX]])
            key = (max(start, clock["pe"]), due[step]) if COST[step[0]][0] else (max(start, clock["pe"]), (-10**6, 0, 0))
            if best is None or key < best[0]:
                best = (key, start, li, step)
        key, start, li, step = best
        li.pop(0)
        order.append(step)
        pe, after = COST[step[0]]
        if step[0] in ("ff_g", "ff_a") and step[3] == 2:
            pe, after = pe // 2, [(after[0][0], after[0][1] // 2)]
        t = start
        if pe:
            t = clock["pe"] = max(start, clock["pe"]) + pe
        for eng, ns in after:
            t = clock[eng] = max(t + HANDOFF, clock[eng]) + ns
        done[step] = t + (DMA_LATENCY if step[0] == "kdma" else HANDOFF)
        if step[0] in SPARE:
            uses.append(step)
        if step[0] == "max":
            maxes.append(step)
    return order


SPARE = {"ctx_tr", "kv_proj", "k_tr", "q_proj", "q_tr", "qkv_proj", "o_nat", "o_tr", "o_proj", "h_tr", "ff_g", "ff_a",
         "ff_o", "ca_q", "ca_kv", "c_tr", "c_q", "c_s", "c_p", "c_o", "mtr"}

SIGNALS = {
    "scores_full": {"st"}, "probs_ready": {"st"}, "max_full": {"max"}, "max_taken": {"max"}, "negm_ready": {"negm"},
    "out_full": {"pv_last"}, "out_taken": {"oev"}, "k_high": {"kv_proj", "x_keys", "qkv_proj"}, "x_split": {"x_keys"},
    "q_high": {"q_proj", "ca_q"}, "m_zeroed": {"m_zero"}, "x_biased": {"x_bias"}, "var_ready": {"ln"},
    "rstd_ready": {"ln"}, "xn_ready": {"ln"}, "gate_ready": {"gelu"}, "c_exp": {"c_s"}, "c_probs": {"c_s"},
}

ROWS_FROM = {1: ("o_proj", 0), 2: ("o_proj", 1), "ff1": ("o_proj", 2), 3: ("ff_o", "ff1"), 5: ("o_proj", 3),
             6: ("o_proj", 5), "ff3": ("o_proj", 6)}


def parts_of(u, i):
    if u == 4:
        return [(qd, 0, C) for qd in range(2)]
    if u == 3:
        return [(qd, t, P) for t in range(TQ) for qd in range(2)]
    return [(qd, i, P) for qd in range(4)] if i < 2 else [(4, t, P) for t in range(TQ)]


def build(nc, io):
    order, quads, slots = plan()
    value, seen, turn, uses = {}, {}, {}, 0
    for step in order:
        kinds = {step[0]}
        if step[0] == "pv" and step[2] == -(-ATT[quads[step[1]]["u"]]["nk"] // P) - 1:
            kinds.add("pv_last")
        for name, by in SIGNALS.items():
            if kinds & by:
                seen[name] = seen.get(name, 0) + 1
                value[name, step] = seen[name]
        if step[0] in SPARE:
            turn[step] = (uses % 2, uses // 2)
            uses += 1

    def slot_value(name, s):
        return value[name, ("st", s)]

    with ExitStack() as ctx:
        def sb(name, shape, dt=F32):
            return ctx.enter_context(nc.sbuf_tensor(name, shape, dt))

        def sem(name):
            return ctx.enter_context(nc.semaphore(name))

        st_ps = [ctx.enter_context(nc.psum_tensor(f"st_ps{i}", [P, 512], F32)) for i in range(N_ST)]
        mx_ps = [ctx.enter_context(nc.psum_tensor(f"mx_ps{i}", [P, 512], F32)) for i in range(N_MX)]
        pv_ps = ctx.enter_context(nc.psum_tensor("pv_ps", [P, 512], F32))
        sp_ps = [ctx.enter_context(nc.psum_tensor(f"sp_ps{i}", [P, 512], F32)) for i in range(2)]

        wm = sb("wm", [P, 640])
        wm2 = sb("wm2", [D2, 640])
        wb = sb("wb", [P, 3040])
        wb2 = sb("wb2", [D2, 2240])
        wbc = sb("wbc", [C, 320])
        wc = sb("wc", [C, 960])
        wqca = sb("wqca", [NCA, D])
        cols = sb("cols", [P, 32])
        cols2 = sb("cols2", [D2, 12])
        bias = sb("bias", [P, 8 * D])
        ident = sb("ident", [P, P])
        identr = sb("identr", [P, P], FR)
        spread = sb("spread", [C, SQ])
        kmask = sb("kmask", [P, 32])
        kmask2 = sb("kmask2", [D2, 32])
        vmask = sb("vmask", [32, D])
        halfpow = sb("halfpow", [P, TQ])
        def two(name, shape, dt=F32):
            return PAIRS * [sb(f"{name}{i}", shape, dt) for i in range(2)]

        x = [sb(f"x{b}", [P, TQ, D]) for b in range(B)]
        ctx_n = two("ctx_n", [P, 4, C])
        ca_n = two("ca_n", [NCA, C])
        xb = two("xb", [P, TQ, D])
        nat = two("nat", [P, TQ, D])
        natc = sb("natc", [C, D])
        hT = two("hT", [P, SQ])
        hT2 = two("hT2", [D2, SQ])
        ctxT = two("ctxT", [C, SK])
        caT8 = two("caT8", [C, 32])
        kdense = two("kdense", [P, 5, SK])
        v20 = two("v20", [P, 4, 20, 9])
        v8 = two("v8", [P, 6, 8, 21])
        qs20 = two("qs20", [P, TQ, 20, 32], FR)
        qs8 = two("qs8", [P, TQ + 1, 8, 64], FR)
        qT = two("qT", [P, 5, SQ], FR)
        qTc = two("qTc", [P, 4, C], FR)
        mx = two("mx", [P, TQ + 1, 20])
        oT = two("oT", [P, 5, SQ])
        oTc = two("oTc", [P, 2, C])
        kbd = two("kbd", [P, 32])
        kbd2 = two("kbd2", [D2, 32])
        vbd = two("vbd", [32, D])
        ks20 = sb("ks20", [P, 2, 20, 32], FR)
        ks8 = sb("ks8", [P, 2, 8, 64], FR)
        ring = sb("ring", [P, RING, 4, SK], FR)
        zeros = sb("zeros", [P, SK])
        probs = sb("probs", [P, N_P, 512])
        gate = sb("gate", [P, FC, SQ])
        stats = sb("stats", [P, TQ, 6])
        mv = sb("mv", [P, TQ, 2])
        rstd = sb("rstd", [P, TQ])
        rinv = sb("rinv", [P, 4, 20])
        cT = sb("cT", [P, C])
        cT2 = sb("cT2", [D2, C])
        cq = sb("cq", [P, C])
        cq2 = sb("cq2", [D2, C])
        cs = sb("cs", [C, 32])
        cmax = sb("cmax", [C, 8])
        cpT = sb("cpT", [32, SQ])

        S = {name: sem(name) for name in SIGNALS}
        spare_full = [sem(f"spare_full{i}") for i in range(2)]
        spare_taken = [sem(f"spare_taken{i}") for i in range(2)]
        ring_in = [sem(f"ring_in{i}") for i in range(RING)]
        s_in = [sem(f"inputs_in{b}") for b in range(B)]
        s_ca = [sem(f"last_rows_in{b}") for b in range(B)]
        s_blk = [sem(f"block_weights{i}") for i in range(2 * PAIRS)]
        s_used = sem("probs_used")
        dve_link = sem("dve_link")
        act_link = sem("act_link")
        pool_link = sem("pool_link")
        s_out = sem("stored")
        s_w = sem("weights_in")
        s_setup = sem("setup_done")
        def of(u):
            return P // ATT[u]["sr"]

        def region(u, h):
            return h % 4 if of(u) == 4 else 2 * (h % 2) + h % 4 // 2

        def key_op(n, h):
            return ring[:, n % RING, region(quads[n]["u"], h), :]

        def dirty(n):
            return n >= RING and of(quads[n]["u"]) == 4 and of(quads[n - RING]["u"]) == 2

        ring_dmas = {n: sum(8 if dirty(m) else 4 for m in range(n % RING, n + 1, RING)) for n in range(len(quads))}

        used_after, count = {}, 0
        for step in order:
            if step[0] == "pv":
                for s in quads[step[1]]["slots"]:
                    if slots[s]["c"] == step[2]:
                        if slots[s]["last"]:
                            used_after[s] = (S["out_full"], step[1] + 1)
                        else:
                            count += 1
                            used_after[s] = (s_used, count)

        def query_op(u, b):
            return qTc[b] if ATT[u]["kind"] == "ca" else qT[b]

        def dense_keys(u, b, g):
            if u == 4:
                return oT[b][:, 2 + g, :] if g < 2 else kdense[b][:, 4, (g - 2) * SQ:(g - 1) * SQ]
            return kdense[b][:, g, :]

        def taken(eng, step):
            b, k = turn[step]
            eng.wait_ge(spare_taken[b], k + 1)

        def query_stack(u, b):
            return qs20[b] if ATT[u]["sr"] == 32 else qs8[b]

        def block_in(eng, u, b):
            eng.wait_ge(s_blk[2 * (b // 2) + (0 if u in (1, 2) else 1)], 48)

        def wts(name, lo=0, hi=None):
            a, b = W_BLOCK[name]
            return slice(a + lo, a + hi if hi is not None else b)

        with nc.Block() as block:
            @block.sync
            def _(sp):
                for dst, src in ((ident, "ident"), (wc, "w_ctx"), (wm, "w_main"), (wm2, "w_main2"), (cols, "cols"),
                                 (cols2, "cols2"), (wqca, "w_qca"), (spread, "spread"), (kmask, "kmask"),
                                 (kmask2, "kmask2"), (vmask, "vmask")):
                    sp.dma_start(dst[:, :], io[src]).then_inc(s_w, 16)
                sp.dma_start(bias[:, :], io["bias"].broadcast_to([P, 8 * D])).then_inc(s_w, 16)
                sp.wait_ge(s_w, 12 * 16)

            @block.scalar
            def _(act):
                act.wait_ge(s_w, 12 * 16)
                nc.scalar.activation(identr[:, :], ident[:, :], ACT.Copy).then_inc(s_setup, 1)

            @block.vector
            def _(dve):
                nc.vector.memset(ring[:, :, :, :].bitcast(F32), 0.0)
                nc.vector.memset(zeros[:, :], 0.0)
                nc.vector.memset(pv_ps[:, :], 0.0)
                nc.vector.memset(v20[0][:, :, :, 8:9], 1.0)
                nc.vector.memset(v20[1][:, :, :, 8:9], 1.0)
                nc.vector.memset(v8[0][:, :, :, 20:21], 1.0)
                nc.vector.memset(v8[1][:, :, :, 20:21], 1.0).then_inc(s_setup, 1)

            @block.gpsimd
            def _(pool):
                for t in (ks20, ks8, *qs20[:2], *qs8[:2]):
                    nc.gpsimd.memset(t[:, :, :, :].bitcast(F32), 0.0).then_inc(pool_link, 1)
                pool.wait_ge(pool_link, 6)
                nc.gpsimd.memset(ks20[:, :, :, 24:26].bitcast(F32), 1.0)
                nc.gpsimd.memset(ks8[:, :, :, 60:62].bitcast(F32), 1.0)
                nc.gpsimd.memset(halfpow[:, :], -0.5).then_inc(s_setup, 1)

        with nc.Block() as block:
            @block.sync
            def _(sp):
                def block_weights(k):
                    for dst, src in ((wb, "w_blk"), (wb2, "w_blk2"), (wbc, "w_blkc")):
                        sp.dma_start(dst[:, :], io[src][k % 2]).then_inc(s_blk[k], 16)

                def context_in(b):
                    sp.dma_start(ctx_n[b][:, :, :], io["ctx"][b].rearrange("(t r) c -> r t c", r=P)).then_inc(s_in[b], 16)

                def last_rows_in(b):
                    sp.dma_start(ca_n[b][:, :], io["ctx"][b][NENC:SK, :]).then_inc(s_ca[b], 16)

                for b in range(B):
                    if b < 2:
                        context_in(b)
                    sp.dma_start(x[b][:, :, :], io["x"][b].rearrange("(t r) d -> r t d", r=P)).then_inc(s_in[b], 16)
                    if b < 2:
                        last_rows_in(b)
                block_weights(0)
                for step in order:
                    if step[0] == "kdma":
                        n = step[1]
                        u, b, qd = quads[n]["u"], quads[n]["b"], quads[n]["qd"]
                        a = ATT[u]
                        taken(sp, [s for s in order if s[0] == "k_tr" and s[1] == u and s[2] == b][-1])
                        if n >= RING:
                            sp.wait_ge(S["scores_full"], quads[n - RING]["slots"][-1] + 1)
                        if dirty(n):
                            for r in range(4):
                                other = slice(32 * (r ^ 1), 32 * (r ^ 1) + 32)
                                sp.dma_start(ring[other, n % RING, r, :].bitcast(F32), zeros[other, :]).then_inc(ring_in[n % RING], 16)
                        for h in range(4 * qd, 4 * qd + 4):
                            j, g = h % of(u), h // of(u)
                            rows = slice(a["sr"] * j, a["sr"] * (j + 1))
                            sp.dma_start(ring[rows, n % RING, region(u, h), 0:a["nk"]].bitcast(F32),
                                         dense_keys(u, b, g)[rows, 0:a["nk"]]).then_inc(ring_in[n % RING], 16)
                    elif step[0] == "ctx_tr" and step[1] + 2 < B:
                        taken(sp, step)
                        context_in(step[1] + 2)
                    elif step[0] == "ca_q" and step[1] + 2 < B:
                        taken(sp, step)
                        last_rows_in(step[1] + 2)
                    elif step[0] == "ff_o" and step[2] % 2 == 1 and step != ("ff_o", "ff3", B - 1):
                        taken(sp, step)
                        block_weights(2 * (step[2] // 2) + (1 if step[1] == "ff1" else 2))
                    elif step[0] == "store":
                        b = step[1]
                        taken(sp, ("ff_o", "ff3", b))
                        sp.dma_start(io["out"][b].rearrange("(t r) d -> r t d", r=P), x[b][:, :, :]).then_inc(s_out, 16)
                sp.wait_ge(s_out, 16 * B)

            @block.tensor
            def _(pe):
                def take(step):
                    b, k = turn[step]
                    if k:
                        pe.wait_ge(spare_taken[b], k)
                    return sp_ps[b], spare_full[b]

                def two_part(out, lhs, lhs2, rhs, rhs2):
                    pe.matmul(out, lhs, rhs, start=True, stop=False)
                    return pe.matmul(out, lhs2, rhs2, start=False, stop=True)

                for step in order:
                    kind = step[0]
                    if kind == "st":
                        s = step[1]
                        sl = slots[s]
                        n, u, b, c = sl["n"], sl["u"], sl["b"], sl["c"]
                        a = ATT[u]
                        if s == quads[n]["start"]:
                            taken(pe, ("mtr", n))
                        if s >= N_ST:
                            pe.wait_ge(S["probs_ready"], slot_value("probs_ready", s - N_ST))
                        kr = chunk_rows(a["nk"], c)
                        for i, h in enumerate(sl["heads"]):
                            mm = pe.matmul(st_ps[s % N_ST][0:kr, i * a["nq"]:(i + 1) * a["nq"]],
                                           key_op(n, h)[:, c * P:c * P + kr], query_op(u, b)[:, h // of(u), :],
                                           start=True, stop=True)
                        mm.then_inc(S["scores_full"], 1)
                    elif kind == "max":
                        _, n, i = step
                        u, b = quads[n]["u"], quads[n]["b"]
                        a = ATT[u]
                        t, rows, heads = quads[n]["items"][i]
                        if i == 0:
                            last = [s for s in order if s[0] == "q_tr" and s[1] == u and s[2] == b][-1]
                            taken(pe, last)
                            pe.wait_ge(ring_in[n % RING], 16 * ring_dmas[n])
                        o = value["max_full", step] - 1
                        if o >= N_MX:
                            pe.wait_ge(S["max_taken"], o - N_MX + 1)
                        tt = 0 if t == TQ else t
                        for j, h in enumerate(heads):
                            mm = pe.matmul(mx_ps[o % N_MX][0:rows, j * a["nk"]:(j + 1) * a["nk"]],
                                           query_op(u, b)[:, h // of(u), tt * P:tt * P + rows],
                                           key_op(n, h)[:, 0:a["nk"]], start=True, stop=True)
                        mm.then_inc(S["max_full"], 1)
                    elif kind == "mtr":
                        n = step[1]
                        u, b, qd = quads[n]["u"], quads[n]["b"], quads[n]["qd"]
                        a = ATT[u]
                        bank, full = take(step)
                        pe.wait_ge(S["negm_ready"], value["negm_ready", ("negm", n)])
                        gs = range(4 * qd // of(u), (4 * qd + 4) // of(u))
                        for k, g in enumerate(gs):
                            for i, (t, rows) in enumerate(q_tiles(u)):
                                mm = pe.matmul(bank[:, k * a["nq"] + i * P:k * a["nq"] + i * P + rows],
                                               query_stack(u, b)[0:rows, t, g * of(u):(g + 1) * of(u), :].rearrange("p h s -> p (h s)"),
                                               identr[0:rows, 0:rows], start=True, stop=True)
                        mm.then_inc(full, 1)
                    elif kind == "pv":
                        _, n, c = step
                        u, b, qd = quads[n]["u"], quads[n]["b"], quads[n]["qd"]
                        a = ATT[u]
                        mine = [s for s in quads[n]["slots"] if slots[s]["c"] == c]
                        if c == 0 and n:
                            pe.wait_ge(S["out_taken"], n)
                        pe.wait_ge(S["probs_ready"], slot_value("probs_ready", mine[-1]))
                        if c == 0 and qd == 0:
                            last = [s for s in order if s[0] in ("kv_proj", "qkv_proj", "x_keys") and
                                    (s[1:3] == (u, b) if s[0] != "x_keys" else (u == 4 and s[1] == b))][-1]
                            pe.wait_ge(S["k_high"], value["k_high", last])
                        kr = chunk_rows(a["nk"], c)
                        for s in mine:
                            for i, h in enumerate(slots[s]["heads"]):
                                j = h % 4
                                v = v20[b][0:kr, c, h, :] if a["dh"] == 8 else v8[b][0:kr, c + (4 if u == 4 else 0), h, :]
                                mm = pe.matmul(pv_ps[32 * j:32 * j + a["dh"] + 1, 0:a["nq"]], v,
                                               probs[0:kr, s % N_P, i * a["nq"]:(i + 1) * a["nq"]],
                                               start=(c == 0), stop=(c == -(-a["nk"] // P) - 1), tile_position=(0, 32 * j))
                            if s == mine[-1] and c == -(-a["nk"] // P) - 1:
                                mm.then_inc(S["out_full"], 1)
                            else:
                                mm.then_inc(s_used, 1)
                    elif kind == "ctx_tr":
                        b = step[1]
                        bank, full = take(step)
                        pe.wait_ge(s_in[b], 2 * 16)
                        for t in range(4):
                            mm = pe.transpose(bank[0:C, t * P:(t + 1) * P], ctx_n[b][:, t, :], ident[:, :])
                        mm.then_inc(full, 1)
                    elif kind == "kv_proj":
                        _, u, b, t = step
                        bank, full = take(step)
                        if t == 0:
                            taken(pe, ("ctx_tr", b))
                            if u in (2, 6):
                                block_in(pe, u, b)
                        kr = chunk_rows(ATT[u]["nk"], t)
                        w = wbc[:, :] if u in (2, 6) else wc[:, W_CTX[u][0]:W_CTX[u][1]]
                        pe.matmul(bank[0:kr, 0:320], ctxT[b][:, t * P:t * P + kr], w, start=True, stop=True).then_inc(full, 1)
                    elif kind == "k_tr":
                        _, u, b, pr, gg = step
                        bank, full = take(step)
                        if u == 4:
                            pe.wait_ge(S["x_split"], value["x_split", ("x_keys", b)])
                        elif ATT[u]["kind"] == "self":
                            for t in range(2):
                                taken(pe, ("qkv_proj", u, b, t))
                        else:
                            for t in range(2):
                                taken(pe, ("kv_proj", u, b, 2 * pr + t))
                        ks = ks20 if ATT[u]["sr"] == 32 else ks8
                        ng = ATT[u]["H"] // of(u)
                        for k, g in enumerate(range(2 * gg, min(2 * gg + 2, ng))):
                            for t in range(2):
                                kr = chunk_rows(ATT[u]["nk"], 2 * pr + t)
                                mm = pe.matmul(bank[:, k * SQ + t * P:k * SQ + t * P + kr],
                                               ks[0:kr, t, g * of(u):(g + 1) * of(u), :].rearrange("p h s -> p (h s)"),
                                               identr[0:kr, 0:kr], start=True, stop=True)
                        mm.then_inc(full, 1)
                    elif kind == "h_tr":
                        _, tag, b = step
                        bank, full = take(step)
                        src = nat[b] if tag in LNS else x[b]
                        if tag in LNS:
                            pe.wait_ge(S["xn_ready"], value["xn_ready", ("ln", tag, b)])
                        elif tag == 3:
                            taken(pe, ("ff_o", "ff1", b))
                        for t in range(TQ):
                            pe.transpose(bank[:, t * P:(t + 1) * P], src[:, t, 0:P], ident[:, :])
                            mm = pe.matmul(bank[0:D2, SQ + t * P:SQ + (t + 1) * P], src[:, t, P:D], ident[:, :], start=True, stop=True)
                        mm.then_inc(full, 1)
                    elif kind == "q_proj":
                        _, u, b = step
                        bank, full = take(step)
                        taken(pe, ("h_tr", u, b))
                        if u in (0, 3):
                            w, w2 = (wm[:, slice(*W_MAIN[f"q{u}"])], wm2[:, slice(*W_MAIN[f"q{u}"])])
                        else:
                            w, w2 = wb[:, wts("q2")], wb2[:, wts("q2")]
                        for t in range(TQ):
                            ts = slice(t * P, (t + 1) * P)
                            mm = two_part(bank[:, t * D:(t + 1) * D], hT[b][:, ts], hT2[b][:, ts], w, w2)
                        mm.then_inc(full, 1)
                    elif kind == "qkv_proj":
                        _, u, b, t = step
                        bank, full = take(step)
                        taken(pe, ("h_tr", u, b))
                        block_in(pe, u, b)
                        ts = slice(t * P, (t + 1) * P)
                        two_part(bank[:, 0:480], hT[b][:, ts], hT2[b][:, ts], wb[:, wts("qkv")], wb2[:, wts("qkv")]).then_inc(full, 1)
                    elif kind == "ca_q":
                        b = step[1]
                        bank, full = take(step)
                        pe.wait_ge(s_ca[b], 16)
                        pe.matmul(bank[0:C, 0:D], ca_n[b][:, :], wqca[:, :], start=True, stop=True).then_inc(full, 1)
                    elif kind == "q_tr":
                        _, u, b, gg = step
                        bank, full = take(step)
                        if ATT[u]["kind"] == "self":
                            for t in range(TQ):
                                taken(pe, ("qkv_proj", u, b, t))
                        else:
                            taken(pe, ("ca_q", b) if u == 4 else ("q_proj", u, b))
                        if gg == 0:
                            pe.wait_ge(S["m_zeroed"], value["m_zeroed", ("m_zero", u, b)])
                        ng = ATT[u]["H"] // of(u)
                        nq = ATT[u]["nq"]
                        for k, g in enumerate(range(4) if u == 4 else range(2 * gg, min(2 * gg + 2, ng))):
                            for i, (t, rows) in enumerate(q_tiles(u)):
                                mm = pe.matmul(bank[:, k * nq + i * P:k * nq + i * P + rows],
                                               query_stack(u, b)[0:rows, t, g * of(u):(g + 1) * of(u), :].rearrange("p h s -> p (h s)"),
                                               identr[0:rows, 0:rows], start=True, stop=True)
                        mm.then_inc(full, 1)
                    elif kind == "o_nat":
                        _, u, b, i = step
                        bank, full = take(step)
                        last = [q["n"] for q in quads if q["u"] == u and q["b"] == b][-1]
                        pe.wait_ge(S["out_taken"], last + 1)
                        for k, (qd, t, rows) in enumerate(parts_of(u, i)):
                            src = oTc[b][:, qd, :] if u == 4 else oT[b][:, qd, t * P:(t + 1) * P]
                            mm = pe.transpose(bank[0:rows, k * P:(k + 1) * P], src, ident[:, :])
                        mm.then_inc(full, 1)
                    elif kind == "o_tr":
                        _, u, b = step
                        bank, full = take(step)
                        for i in range(1 if u == 3 else 3):
                            taken(pe, ("o_nat", u, b, i))
                        for t in range(TQ):
                            pe.transpose(bank[:, t * P:(t + 1) * P], nat[b][:, t, 0:P], ident[:, :])
                            mm = pe.matmul(bank[0:D2, SQ + t * P:SQ + (t + 1) * P], nat[b][:, t, P:D], ident[:, :], start=True, stop=True)
                        mm.then_inc(full, 1)
                    elif kind == "o_proj":
                        _, u, b = step
                        bank, full = take(step)
                        taken(pe, ("c_o", b) if u == 3 else ("o_tr", u, b))
                        if u in (0, 3):
                            w, w2 = (wm[:, slice(*W_MAIN[f"o{u}"])], wm2[:, slice(*W_MAIN[f"o{u}"])])
                        else:
                            name = "o1" if u in (1, 5) else "o2"
                            w, w2 = wb[:, wts(name)], wb2[:, wts(name)]
                        for t in range(TQ):
                            ts = slice(t * P, (t + 1) * P)
                            mm = two_part(bank[:, t * D:(t + 1) * D], hT[b][:, ts], hT2[b][:, ts], w, w2)
                        mm.then_inc(full, 1)
                    elif kind in ("ff_g", "ff_a"):
                        _, tag, b, i = step
                        bank, full = take(step)
                        taken(pe, ("h_tr", tag, b))
                        for k, m in enumerate(range(2 * i, min(2 * i + 2, FC))):
                            lo = (FF if kind == "ff_g" else 0) + m * P
                            mm = two_part(bank[:, k * SQ:(k + 1) * SQ], wb[:, wts("w1", lo, lo + P)], wb2[:, wts("w1", lo, lo + P)],
                                          hT[b][:, :], hT2[b][:, :])
                        mm.then_inc(full, 1)
                    elif kind == "ff_o":
                        _, tag, b = step
                        bank, full = take(step)
                        for i in (1, 2):
                            taken(pe, ("ff_a", tag, b, i))
                        for t in range(TQ):
                            for m in range(FC):
                                mm = pe.matmul(bank[:, t * D:(t + 1) * D], gate[:, m, t * P:(t + 1) * P],
                                               wb[:, 2240 + m * D:2240 + (m + 1) * D], start=(m == 0), stop=(m == FC - 1))
                        mm.then_inc(full, 1)
                    elif kind == "ca_kv":
                        b = step[1]
                        bank, full = take(step)
                        wk = W_CTX["ca"][0]
                        pe.matmul(bank[:, 0:NCA], wc[:, wk:wk + P], ctxT[b][:, NENC:SK], start=True, stop=True)
                        pe.matmul(bank[0:D2, 8:8 + NCA], wc[:, wk + P:wk + D], ctxT[b][:, NENC:SK], start=True, stop=True)
                        pe.matmul(bank[0:32, 64:64 + D], caT8[b][:, :], wc[:, wk + D:wk + 2 * D], start=True, stop=True).then_inc(full, 1)
                    elif kind == "c_tr":
                        b = step[1]
                        bank, full = take(step)
                        taken(pe, ("o_nat", 4, b, 0))
                        pe.transpose(bank[:, 0:C], natc[:, 0:P], ident[0:C, 0:C])
                        pe.matmul(bank[0:D2, P:P + C], natc[:, P:D], ident[0:C, 0:C], start=True, stop=True).then_inc(full, 1)
                    elif kind == "c_q":
                        bank, full = take(step)
                        taken(pe, ("c_tr", step[1]))
                        a = W_MAIN["q3"][0]
                        two_part(bank[:, 0:C], wm[:, a:a + P], wm2[:, a:a + P], cT[:, :], cT2[:, :])
                        two_part(bank[0:D2, P:P + C], wm[:, a + P:a + D], wm2[:, a + P:a + D], cT[:, :], cT2[:, :]).then_inc(full, 1)
                    elif kind == "c_s":
                        b = step[1]
                        bank, full = take(step)
                        taken(pe, ("c_q", b))
                        taken(pe, ("ca_kv", b))
                        two_part(bank[0:C, 0:32], cq[:, :], cq2[:, :], kbd[b][:, :], kbd2[b][:, :]).then_inc(full, 1)
                    elif kind == "c_p":
                        b = step[1]
                        bank, full = take(step)
                        pe.wait_ge(S["c_probs"], value["c_probs", ("c_s", b)])
                        pe.matmul(bank[0:32, 0:SQ], cs[:, :], spread[:, :], start=True, stop=True).then_inc(full, 1)
                    elif kind == "c_o":
                        b = step[1]
                        bank, full = take(step)
                        taken(pe, ("c_p", b))
                        pe.matmul(bank[:, 0:SQ], vbd[b][:, 0:P], cpT[:, :], start=True, stop=True)
                        pe.matmul(bank[0:D2, SQ:2 * SQ], vbd[b][:, P:D], cpT[:, :], start=True, stop=True).then_inc(full, 1)

            def filled(eng, step):
                b, k = turn[step]
                eng.wait_ge(spare_full[b], k + 1)
                return sp_ps[b], spare_taken[b]

            def high_slots(stack, t0, t1, rows, dh, which):
                step = 2 * dh if which == "k" else dh
                v = stack[0:rows, t0:t1, :, 0:3 * dh].rearrange("p t h (s d) -> p (t h) s d", s=3)
                return v[:, :, 0:3:2, :] if which == "k" else v[:, :, 0:2, :]

            @block.scalar
            def _(act):
                def split_high(stack, t0, t1, rows, dh, which, src):
                    out = high_slots(stack, t0, t1, rows, dh, which)
                    n = (t1 - t0) * (D // dh)
                    v = src.rearrange("p (h d) -> p h d", d=dh).unsqueeze(2).broadcast_to([rows, n, 2, dh])
                    return nc.scalar.activation(out, v, ACT.Copy)

                for step in order:
                    kind = step[0]
                    if kind == "st":
                        s = step[1]
                        a = ATT[slots[s]["u"]]
                        act.wait_ge(S["scores_full"], s + 1)
                        if s >= N_P:
                            act.wait_ge(*used_after[s - N_P])
                        kr = chunk_rows(a["nk"], slots[s]["c"])
                        w = a["hps"] * a["nq"]
                        nc.scalar.activation(probs[0:kr, s % N_P, 0:w], st_ps[s % N_ST][0:kr, 0:w], ACT.Exp,
                                             scale=float(a["dh"]) ** -0.5).then_inc(S["probs_ready"], 1)
                    elif kind == "oev":
                        n = step[1]
                        u, b, qd = quads[n]["u"], quads[n]["b"], quads[n]["qd"]
                        act.wait_ge(S["out_full"], n + 1)
                        dst = oTc[b][:, qd, :] if u == 4 else oT[b][:, qd, :]
                        nc.scalar.activation(dst, pv_ps[:, 0:ATT[u]["nq"]], ACT.Copy).then_inc(S["out_taken"], 1)
                    elif kind == "ctx_tr":
                        b = step[1]
                        bank, free = filled(act, step)
                        nc.scalar.activation(caT8[b][:, :].rearrange("p (h k) -> p h k", h=8),
                                             bank[0:C, NENC:SK].unsqueeze(1).broadcast_to([C, 8, NCA]), ACT.Copy)
                        nc.scalar.activation(ctxT[b][:, :], bank[0:C, :], ACT.Copy).then_inc(free, 1)
                    elif kind == "kv_proj":
                        _, u, b, t = step
                        dh = ATT[u]["dh"]
                        bank, free = filled(act, step)
                        kr = chunk_rows(ATT[u]["nk"], t)
                        ks, v = (ks20, v20[b]) if dh == 8 else (ks8, v8[b])
                        split_high(ks, t % 2, t % 2 + 1, kr, dh, "k", bank[0:kr, 0:D])
                        nc.scalar.activation(v[0:kr, t, :, 0:dh], bank[0:kr, D:2 * D].rearrange("p (h d) -> p h d", d=dh),
                                             ACT.Copy).then_inc(S["k_high"], 1)
                    elif kind == "qkv_proj":
                        _, u, b, t = step
                        bank, free = filled(act, step)
                        split_high(ks20, t, t + 1, P, 8, "k", bank[:, D:2 * D])
                        split_high(qs20[b], t, t + 1, P, 8, "q", bank[:, 0:D])
                        nc.scalar.activation(v20[b][:, t, :, 0:8], bank[:, 2 * D:3 * D].rearrange("p (h d) -> p h d", d=8),
                                             ACT.Copy).then_inc(S["k_high"], 1)
                    elif kind == "x_keys":
                        b = step[1]
                        taken(act, ("ff_o", "ff1", b))
                        prev = [s for s in order[:order.index(step)] if s[0] == "k_tr"][-1]
                        act.wait_ge(spare_full[turn[prev][0]], turn[prev][1] + 1)
                        split_high(ks8, 0, TQ, P, 20, "k", x[b][:, :, :].rearrange("p t d -> p (t d)"))
                        nc.scalar.activation(v8[b][:, 4:6, :, 0:20].rearrange("p t h d -> p (t h) d"),
                                             x[b][:, :, :].rearrange("p t (h d) -> p (t h) d", d=20), ACT.Copy).then_inc(S["k_high"], 1)
                    elif kind == "k_tr":
                        _, u, b, pr, gg = step
                        bank, free = filled(act, step)
                        ng = ATT[u]["H"] // of(u)
                        n = min(2, ng - 2 * gg)
                        w = chunk_rows(ATT[u]["nk"], 2 * pr) + chunk_rows(ATT[u]["nk"], 2 * pr + 1)
                        if u == 4:
                            dst = (oT[b][:, 2:4, :] if gg == 0 else kdense[b][:, 4, :].rearrange("p (g k) -> p g k", g=2))
                        else:
                            dst = kdense[b][:, 2 * gg:2 * gg + n, pr * SQ:pr * SQ + w]
                        nc.scalar.activation(dst, bank[:, 0:n * SQ].rearrange("p (g k) -> p g k", g=n)[:, :, 0:w], ACT.Copy).then_inc(free, 1)
                    elif kind == "h_tr":
                        _, tag, b = step
                        bank, free = filled(act, step)
                        if tag in LNS:
                            c = 2 * LNS[tag]
                            nc.scalar.activation(hT[b][:, :], bank[:, 0:SQ], ACT.Identity, scale=cols[:, c:c + 1], bias=cols[:, c + 1:c + 2])
                            nc.scalar.activation(hT2[b][:, :], bank[0:D2, SQ:2 * SQ], ACT.Identity, scale=cols2[:, c:c + 1], bias=cols2[:, c + 1:c + 2]).then_inc(free, 1)
                        else:
                            nc.scalar.activation(hT[b][:, :], bank[:, 0:SQ], ACT.Copy)
                            nc.scalar.activation(hT2[b][:, :], bank[0:D2, SQ:2 * SQ], ACT.Copy).then_inc(free, 1)
                    elif kind == "o_tr":
                        b = step[2]
                        bank, free = filled(act, step)
                        nc.scalar.activation(hT[b][:, :], bank[:, 0:SQ], ACT.Copy)
                        nc.scalar.activation(hT2[b][:, :], bank[0:D2, SQ:2 * SQ], ACT.Copy).then_inc(free, 1)
                    elif kind in ("c_tr", "c_q"):
                        bank, free = filled(act, step)
                        dst, dst2 = (cT, cT2) if kind == "c_tr" else (cq, cq2)
                        nc.scalar.activation(dst[:, :], bank[:, 0:C], ACT.Copy)
                        nc.scalar.activation(dst2[:, :], bank[0:D2, P:P + C], ACT.Copy).then_inc(free, 1)
                    elif kind == "c_p":
                        bank, free = filled(act, step)
                        nc.scalar.activation(cpT[:, :], bank[0:32, 0:SQ], ACT.Copy).then_inc(free, 1)
                    elif kind == "q_proj":
                        _, u, b = step
                        bank, free = filled(act, step)
                        dh = ATT[u]["dh"]
                        split_high(query_stack(u, b), 0, TQ, P, dh, "q", bank[:, 0:TQ * D]).then_inc(S["q_high"], 1)
                    elif kind == "ca_q":
                        b = step[1]
                        bank, free = filled(act, step)
                        split_high(qs8[b], TQ, TQ + 1, C, 20, "q", bank[0:C, 0:D]).then_inc(S["q_high"], 1)
                    elif kind == "q_tr":
                        _, u, b, gg = step
                        bank, free = filled(act, step)
                        if u == 4:
                            dst, w = qTc[b][:, :, :].rearrange("p g q -> p (g q)"), 4 * C
                        else:
                            n = min(2, ATT[u]["H"] // of(u) - 2 * gg)
                            dst, w = qT[b][:, 2 * gg:2 * gg + n, :].rearrange("p g q -> p (g q)"), n * SQ
                        nc.scalar.activation(dst, bank[:, 0:w], ACT.Copy).then_inc(free, 1)
                    elif kind == "ff_g":
                        _, tag, b, i = step
                        bank, free = filled(act, step)
                        for k, m in enumerate(range(2 * i, min(2 * i + 2, FC))):
                            c = 12 + (0 if tag == "ff1" else 10) + FC + m
                            ins = nc.scalar.activation(gate[:, m, :], bank[:, k * SQ:(k + 1) * SQ], ACT.Identity, bias=cols[:, c:c + 1])
                        ins.then_inc(free, 1)
                    elif kind == "gelu":
                        _, tag, b = step
                        for i in (1, 2):
                            taken(act, ("ff_g", tag, b, i))
                        nc.scalar.activation(gate[:, :, :], gate[:, :, :], ACT.Gelu).then_inc(S["gate_ready"], 1)
                    elif kind == "c_s":
                        taken(act, step)
                        nc.scalar.activation(cs[:, :], cs[:, :], ACT.Exp, scale=20.0 ** -0.5).then_inc(S["c_exp"], 1)

            @block.vector
            def _(dve):
                links = [0]

                def link(ins):
                    links[0] += 1
                    ins.then_inc(dve_link, 1)
                    dve.wait_ge(dve_link, links[0])

                def split_low(stack, t0, t1, rows, dh, which, src):
                    lo = dh if which == "k" else 2 * dh
                    high = stack[0:rows, t0:t1, :, 0:dh].rearrange("p t h d -> p (t h) d").bitcast(F32)
                    out = stack[0:rows, t0:t1, :, lo:lo + dh].rearrange("p t h d -> p (t h) d")
                    return nc.vector.tensor_tensor(out, src.rearrange("p (h d) -> p h d", d=dh), high, ALU.subtract)

                for step in order:
                    kind = step[0]
                    if kind == "max":
                        _, n, i = step
                        u, b = quads[n]["u"], quads[n]["b"]
                        a = ATT[u]
                        t, rows, heads = quads[n]["items"][i]
                        o = value["max_full", step]
                        dve.wait_ge(S["max_full"], o)
                        nc.vector.tensor_reduce(mx[b][0:rows, t, heads[0]:heads[-1] + 1],
                                                mx_ps[(o - 1) % N_MX][0:rows, 0:a["hpm"] * a["nk"]].rearrange("p (h k) -> p h k", k=a["nk"]),
                                                AX.X, ALU.max).then_inc(S["max_taken"], 1)
                    elif kind == "negm":
                        n = step[1]
                        u, b, qd = quads[n]["u"], quads[n]["b"], quads[n]["qd"]
                        dh = ATT[u]["dh"]
                        tiles = q_tiles(u)
                        t0, t1, rows = tiles[0][0], tiles[-1][0] + 1, tiles[0][1]
                        dve.wait_ge(S["max_taken"], value["max_taken", ("max", n, len(quads[n]["items"]) - 1)])
                        m = mx[b][0:rows, t0:t1, 4 * qd:4 * qd + 4]
                        st = query_stack(u, b)[0:rows, t0:t1, 4 * qd:4 * qd + 4, :]
                        link(nc.vector.tensor_scalar(st[:, :, :, 3 * dh], m, -1.0, None, ALU.mult))
                        nc.vector.scalar_tensor_tensor(out=st[:, :, :, 3 * dh + 1], in0=m, scalar=-1.0,
                                                       in1=st[:, :, :, 3 * dh].bitcast(F32),
                                                       op0=ALU.mult, op1=ALU.subtract).then_inc(S["negm_ready"], 1)
                    elif kind == "mtr":
                        n = step[1]
                        u, b, qd = quads[n]["u"], quads[n]["b"], quads[n]["qd"]
                        bank, done = filled(dve, step)
                        g0, g1 = 4 * qd // of(u), (4 * qd + 4) // of(u)
                        nq = ATT[u]["nq"]
                        nc.vector.tensor_copy(query_op(u, b)[:, g0:g1, :].rearrange("p g q -> p (g q)"),
                                              bank[:, 0:(g1 - g0) * nq]).then_inc(done, 1)
                    elif kind == "kv_proj":
                        _, u, b, t = step
                        bank, done = filled(dve, step)
                        dve.wait_ge(S["k_high"], value["k_high", step])
                        kr = chunk_rows(ATT[u]["nk"], t)
                        ks = ks20 if ATT[u]["dh"] == 8 else ks8
                        split_low(ks, t % 2, t % 2 + 1, kr, ATT[u]["dh"], "k", bank[0:kr, 0:D]).then_inc(done, 1)
                    elif kind == "qkv_proj":
                        _, u, b, t = step
                        bank, done = filled(dve, step)
                        dve.wait_ge(S["k_high"], value["k_high", step])
                        split_low(ks20, t, t + 1, P, 8, "k", bank[:, D:2 * D])
                        split_low(qs20[b], t, t + 1, P, 8, "q", bank[:, 0:D]).then_inc(done, 1)
                    elif kind == "x_keys":
                        b = step[1]
                        dve.wait_ge(S["k_high"], value["k_high", step])
                        split_low(ks8, 0, TQ, P, 20, "k", x[b][:, :, :].rearrange("p t d -> p (t d)")).then_inc(S["x_split"], 1)
                    elif kind in ("q_proj", "ca_q"):
                        b = step[-1]
                        bank, done = filled(dve, step)
                        dve.wait_ge(S["q_high"], value["q_high", step])
                        if kind == "ca_q":
                            split_low(qs8[b], TQ, TQ + 1, C, 20, "q", bank[0:C, 0:D]).then_inc(done, 1)
                        else:
                            u = step[1]
                            split_low(query_stack(u, b), 0, TQ, P, ATT[u]["dh"], "q", bank[:, 0:TQ * D]).then_inc(done, 1)
                    elif kind == "ln":
                        _, tag, b = step
                        taken(dve, (*ROWS_FROM[tag], b))
                        nc.vector.bn_stats(stats[:, 0, :], x[b][:, 0, :])
                        link(nc.vector.bn_stats(stats[:, 1, :], x[b][:, 1, :]))
                        nc.vector.bn_aggr(mv[:, 0, :], stats[:, 0, :])
                        nc.vector.bn_aggr(mv[:, 1, :], stats[:, 1, :]).then_inc(S["var_ready"], 1)
                        dve.wait_ge(S["rstd_ready"], value["rstd_ready", step])
                        for t in range(TQ):
                            ins = nc.vector.tensor_scalar(nat[b][:, t, :], x[b][:, t, :], mv[:, t, 0:1], rstd[:, t:t + 1],
                                                          ALU.subtract, ALU.mult)
                        ins.then_inc(S["xn_ready"], 1)
                    elif kind == "o_nat":
                        _, u, b, i = step
                        bank, done = filled(dve, step)
                        parts = parts_of(u, i)
                        rows, dh, nh = parts[0][2], ATT[u]["dh"], 4 * len(parts)
                        v = bank[0:rows, 0:nh * 32].rearrange("p (h s) -> p h s", s=32)
                        k = 3 if u == 4 else i
                        link(nc.vector.reciprocal(rinv[0:rows, k, 0:nh], v[:, :, dh]))
                        inv = rinv[0:rows, k, 0:nh].unsqueeze(2).broadcast_to([rows, nh, dh])
                        if u == 4:
                            out = natc[:, :].rearrange("p (h d) -> p h d", d=dh)
                        elif u == 3:
                            out = nat[b][:, :, :].rearrange("p t (h d) -> p (t h) d", d=dh)
                        elif i < 2:
                            out = nat[b][:, i, 0:P].rearrange("p (h d) -> p h d", d=dh)
                        if u in (3, 4) or i < 2:
                            nc.vector.tensor_tensor(out, v[:, :, 0:dh], inv, ALU.mult).then_inc(done, 1)
                        else:
                            for t in range(TQ):
                                ins = nc.vector.tensor_tensor(nat[b][:, t, P:D].rearrange("p (h d) -> p h d", d=dh),
                                                              v[:, 4 * t:4 * t + 4, 0:dh], inv[:, 4 * t:4 * t + 4, :], ALU.mult)
                            ins.then_inc(done, 1)
                    elif kind in ("o_proj", "ff_o"):
                        _, u, b = step
                        bank, done = filled(dve, step)
                        dve.wait_ge(S["x_biased"], value["x_biased", ("x_bias", u, b)])
                        nc.vector.tensor_tensor(x[b][:, :, :].rearrange("p t d -> p (t d)"), bank[:, 0:TQ * D],
                                                xb[b][:, :, :].rearrange("p t d -> p (t d)"), ALU.add).then_inc(done, 1)
                    elif kind == "ff_a":
                        _, tag, b, i = step
                        bank, done = filled(dve, step)
                        dve.wait_ge(S["gate_ready"], value["gate_ready", ("gelu", tag, b)])
                        for k, m in enumerate(range(2 * i, min(2 * i + 2, FC))):
                            c = 12 + (0 if tag == "ff1" else 10) + m
                            ins = nc.vector.scalar_tensor_tensor(out=gate[:, m, :], in0=bank[:, k * SQ:(k + 1) * SQ],
                                                                 scalar=cols[:, c:c + 1], in1=gate[:, m, :],
                                                                 op0=ALU.add, op1=ALU.mult)
                        ins.then_inc(done, 1)
                    elif kind == "ca_kv":
                        b = step[1]
                        bank, done = filled(dve, step)
                        for dst, mask, k in ((kbd[b], kmask, bank[:, 0:NCA]), (kbd2[b], kmask2, bank[0:D2, 8:8 + NCA])):
                            rows = mask.shape[0]
                            nc.vector.tensor_tensor(dst[:, :].rearrange("p (h k) -> p h k", h=8),
                                                    k.unsqueeze(1).broadcast_to([rows, 8, NCA]),
                                                    mask[:, :].rearrange("p (h k) -> p h k", h=8), ALU.mult)
                        nc.vector.tensor_tensor(vbd[b][:, :], bank[0:32, 64:64 + D], vmask[:, :], ALU.mult).then_inc(done, 1)
                    elif kind == "c_s":
                        bank, done = filled(dve, step)
                        v = bank[0:C, 0:32].rearrange("p (h k) -> p h k", h=8)
                        cv = cs[:, :].rearrange("p (h k) -> p h k", h=8)
                        spread_h = cmax[:, :].unsqueeze(2).broadcast_to([C, 8, NCA])
                        link(nc.vector.tensor_reduce(cmax[:, :], v, AX.X, ALU.max))
                        nc.vector.tensor_tensor(cv, v, spread_h, ALU.subtract).then_inc(done, 1)
                        dve.wait_ge(S["c_exp"], value["c_exp", step])
                        link(nc.vector.tensor_reduce(cmax[:, :], cv, AX.X, ALU.add))
                        link(nc.vector.reciprocal(cmax[:, :], cmax[:, :]))
                        nc.vector.tensor_tensor(cv, cv, spread_h, ALU.mult).then_inc(S["c_probs"], 1)
                    elif kind == "c_o":
                        b = step[1]
                        bank, done = filled(dve, step)
                        taken(dve, ("o_tr", 3, b))
                        nc.vector.tensor_tensor(hT[b][:, :], bank[:, 0:SQ], hT[b][:, :], ALU.add)
                        nc.vector.tensor_tensor(hT2[b][:, :], bank[0:D2, SQ:2 * SQ], hT2[b][:, :], ALU.add).then_inc(done, 1)

            @block.gpsimd
            def _(pool):
                links = 6
                for step in order:
                    kind = step[0]
                    if kind == "ln":
                        pool.wait_ge(S["var_ready"], value["var_ready", step])
                        links += 1
                        nc.gpsimd.tensor_scalar(rstd[:, :], mv[:, :, 1], EPS, None, ALU.add).then_inc(pool_link, 1)
                        pool.wait_ge(pool_link, links)
                        nc.gpsimd.tensor_tensor(rstd[:, :], rstd[:, :], halfpow[:, :], ALU.pow).then_inc(S["rstd_ready"], 1)
                    elif kind == "x_bias":
                        _, tag, b = step
                        if tag != 0:
                            taken(pool, (*ROWS_FROM[tag], b))
                        else:
                            pool.wait_ge(s_in[b], 2 * 16)
                            if b >= 2:
                                taken(pool, ("ff_o", "ff3", b - 2))
                        c = BIAS[tag] * D
                        nc.gpsimd.tensor_tensor(xb[b][:, :, :], x[b][:, :, :],
                                                bias[:, c:c + D].unsqueeze(1).broadcast_to([P, TQ, D]), ALU.add).then_inc(S["x_biased"], 1)
                    elif kind == "m_zero":
                        _, u, b = step
                        first = [q["n"] for q in quads if q["u"] == u and q["b"] == b][0]
                        before = [q["n"] for q in quads[:first] if q["b"] % 2 == b % 2 and
                                  (q["u"] == u if u in (3, 4) else ATT[q["u"]]["sr"] == 32)]
                        if before:
                            taken(pool, ("mtr", before[-1]))
                        tiles = q_tiles(u)
                        dh = ATT[u]["dh"]
                        nc.gpsimd.memset(query_stack(u, b)[:, tiles[0][0]:tiles[-1][0] + 1, :, 3 * dh:3 * dh + 2].bitcast(F32), 0.0).then_inc(S["m_zeroed"], 1)


def kernel(**inputs):
    import concourse.bacc as bacc
    from concourse.bass_utils import run_bass_kernel_spmd

    w = {k: np.asarray(v) for k, v in inputs.items()}
    blocks = ("L1_xattn_", "L3_xattn_")
    ln_names = [b + n for b in blocks for n in ("n1", "n2", "n3")]
    mains = [w["L0_xattn_Wq"], w["L0_xattn_Wo"], w["L2_xattn_Wq"], w["L2_xattn_Wout"]]
    wide = [np.concatenate([w[b + n] for n in ("q1", "k1", "v1", "o1_w", "q2", "o2_w", "ff_w1")], axis=1) for b in blocks]
    down = [w[b + "ff_w2"].reshape(FC, P, D).transpose(1, 0, 2).reshape(P, FC * D) for b in blocks]
    idx = np.linspace(0, C - 1, SQ).astype(np.int64)
    head = np.arange(D) // 20
    kmask = np.repeat((head[:, None] == np.arange(8)[None, :]).astype(np.float32), NCA, axis=1)
    arrays = {
        "x": w["x"], "ctx": w["ctx_768"],
        "w_main": np.concatenate([m[:P] for m in mains], axis=1),
        "w_main2": np.concatenate([m[P:] for m in mains], axis=1),
        "w_blk": np.stack([np.concatenate([a[:P], d], axis=1) for a, d in zip(wide, down)]),
        "w_blk2": np.stack([a[P:] for a in wide]),
        "w_blkc": np.stack([np.concatenate([w[b + "k2"], w[b + "v2"]], axis=1) for b in blocks]),
        "w_ctx": np.concatenate([w["L0_xattn_Wk"], w["L0_xattn_Wv"], w["L2_xattn_Wk"], w["L2_xattn_Wv"],
                                 w["L2_xattn_Wk_ca"], w["L2_xattn_Wv_ca"]], axis=1),
        "w_qca": w["L2_xattn_Wq_ca"],
        "cols": np.concatenate([np.stack([w[n + s][:P] for n in ln_names for s in ("_g", "_b")], axis=1)]
                               + [w[b + "ff_b1"].reshape(2 * FC, P).T for b in blocks], axis=1),
        "cols2": np.stack([w[n + s][P:] for n in ln_names for s in ("_g", "_b")], axis=1),
        "bias": np.concatenate([w[n] for n in (
            "L0_xattn_bo", "L1_xattn_o1_b", "L1_xattn_o2_b", "L1_xattn_ff_b2", "L2_xattn_b_out", "L3_xattn_o1_b",
            "L3_xattn_o2_b", "L3_xattn_ff_b2")])[None, :],
        "ident": np.eye(P, dtype=np.float32),
        "spread": (np.arange(C)[:, None] == idx[None, :]).astype(np.float32),
        "kmask": kmask[:P], "kmask2": kmask[P:],
        "vmask": kmask.T,
    }
    nc = bacc.Bacc("TRN2", target_bir_lowering=False, num_devices=1)
    arrays = {k: np.ascontiguousarray(v) for k, v in arrays.items()}
    io = {k: nc.dram_tensor("in_" + k, v.shape, mybir.dt.from_np(v.dtype), kind="ExternalInput").ap() for k, v in arrays.items()}
    io["out"] = nc.dram_tensor("out_rows", (B, SQ, D), F32, kind="ExternalOutput").ap()
    build(nc, io)
    r = run_bass_kernel_spmd(nc, [{"in_" + k: v for k, v in arrays.items()}], core_ids=[0])
    return r.results[0]["out_rows"]
```

```python
from contextlib import ExitStack

import numpy as np

import concourse.bass as bass
from concourse import mybir

F32 = mybir.dt.float32
FR = mybir.dt.float32r
ALU = mybir.AluOpType
ACT = mybir.ActivationFunctionType
AX = mybir.AxisListType

B, SQ, D = 4, 256, 160
SK, C = 512, 96
P = 128
TQ = SQ // P
D2 = D - P
FF = 4 * D
FC = FF // P
NCA = 4
NENC = SK - NCA
EPS = 1e-5
PAIRS = B // 2

ATT = {
    0: dict(kind="cross", H=20, dh=8, sr=32, nq=SQ, nk=SK, hps=2, hpm=1),
    1: dict(kind="self", H=20, dh=8, sr=32, nq=SQ, nk=SQ, hps=2, hpm=2),
    2: dict(kind="cross", H=20, dh=8, sr=32, nq=SQ, nk=SK, hps=2, hpm=1),
    3: dict(kind="enc", H=8, dh=20, sr=64, nq=SQ, nk=NENC, hps=2, hpm=1),
    4: dict(kind="ca", H=8, dh=20, sr=64, nq=C, nk=SQ, hps=4, hpm=2),
    5: dict(kind="self", H=20, dh=8, sr=32, nq=SQ, nk=SQ, hps=2, hpm=2),
    6: dict(kind="cross", H=20, dh=8, sr=32, nq=SQ, nk=SK, hps=2, hpm=1),
}
PHASES = [(0,), (1,), (2,), (4, 3), (5,), (6,)]
MTR_DUE = 0
WARM_UP = 8
LAST_FEED = ("ff3", B - 1)
C_SPAN = 0
N_CONST = 10
N_ST = 2
N_SP = 3
N_MX = 2
N_P = 6
RING = 4
PV_LAG = 2
FIRST_W = 3
K_LEAD = 4
TAIL = 40
BG_LEAD = 11
M_LEAD = 8

W_MAIN = {"q0": (0, 160), "o0": (160, 320), "q3": (320, 480), "o3": (480, 640)}
W_BLOCK = {"qkv": (0, 480), "o1": (480, 640), "q2": (640, 800), "o2": (800, 960), "w1": (960, 2240)}
W_CTX = {0: (0, 320), 3: (320, 640), "ca": (640, 960)}
BIAS = {0: 0, 1: 1, 2: 2, "ff1": 3, 3: 4, 5: 5, 6: 6, "ff3": 7}
LNS = {1: 0, 2: 1, "ff1": 2, 5: 3, 6: 4, "ff3": 5}


def chunk_rows(nk, c):
    return min(P, nk - P * c)


def q_tiles(u):
    return [(t, P) for t in range(TQ)] if ATT[u]["nq"] == SQ else [(TQ, ATT[u]["nq"])]


def merge(one, other):
    out, j = [], 0
    for i, s in enumerate(one):
        out.append(s)
        while j < (i + 1) * len(other) // len(one):
            out.append(other[j])
            j += 1
    return out + other[j:]


def background(ph, b):
    def ctx_keys(u):
        s = []
        for pair in range(2):
            s += [("kv_proj", u, b, t) for t in (2 * pair, 2 * pair + 1)]
            s += [("k_tr", u, b, pair, gg) for gg in range(3 if ATT[u]["sr"] == 32 else 2)]
        return s

    def queries(u):
        n = 3 if ATT[u]["sr"] == 32 else 2
        return [("m_zero", u, b), ("q_proj", u, b)] + [("q_tr", u, b, gg) for gg in range(n)]

    def own_keys(u):
        return ([("m_zero", u, b)] + [("qkv_proj", u, b, t) for t in range(TQ)] + [("k_tr", u, b, 0, gg) for gg in range(3)]
                + [("q_tr", u, b, gg) for gg in range(3)])

    def output(u):
        return [("o_nat", u, b, i) for i in range(3)] + [("o_tr", u, b), ("o_proj", u, b)]

    def feed(tag):
        if (tag, b) == LAST_FEED:
            return ([("ln", tag, b), ("x_bias", tag, b), ("norm", tag, b), ("h_tr", tag, b)]
                    + [(kind, tag, b, i) for i in range(3) for kind in ("ff_g", "ff_a")] + [("ff_o", tag, b)])
        return ([("ln", tag, b), ("x_bias", tag, b), ("norm", tag, b), ("h_tr", tag, b)] + [("ff_g", tag, b, i) for i in range(3)] + [("gelu", tag, b)]
                + [("ff_a", tag, b, i) for i in range(3)] + [("ff_o", tag, b)])

    if ph == -1:
        return [[[("ctx_tr", b)] + ctx_keys(0), [("x_bias", 0, b), ("h_tr", 0, b)] + queries(0)]]
    if ph == 0:
        return [[output(0) + [("ln", 1, b), ("x_bias", 1, b), ("norm", 1, b), ("h_tr", 1, b)] + own_keys(1)]]
    if ph == 1:
        return [[output(1) + [("ln", 2, b), ("x_bias", 2, b), ("norm", 2, b), ("h_tr", 2, b)] + queries(2), ctx_keys(2)]]
    if ph == 2:
        return [[output(2) + feed("ff1"), [("m_zero", 4, b), ("ca_q", b), ("q_tr", 4, b, 0)] + ctx_keys(3) + [("ca_kv", b)]],
                [[("x_keys", b), ("k_tr", 4, b, 0, 0), ("k_tr", 4, b, 0, 1)], [("x_bias", 3, b), ("h_tr", 3, b)] + queries(3)]]
    if ph == 3:
        return [[[("o_nat", 3, b, 0), ("o_tr", 3, b), ("c_o", b), ("o_proj", 3, b), ("ln", 5, b), ("x_bias", 5, b), ("norm", 5, b), ("h_tr", 5, b)] + own_keys(5)]]
    if ph == 4:
        return [[output(5) + [("ln", 6, b), ("x_bias", 6, b), ("norm", 6, b), ("h_tr", 6, b)] + queries(6), ctx_keys(6)]]
    last = [output(6) + feed("ff3") + [("store", b)]]
    if b + 2 >= B:
        return [last]
    keys, rest = background(-1, b + 2)[0]
    return [last + [keys], [rest]]


def last_rows(b):
    return [("o_nat", 4, b, 0), ("c_tr", b), ("c_q", b), ("c_s", b), ("c_norm", b), ("c_p", b)]


def plan():
    quads, slots, span = [], [], {}
    for r in range(PAIRS):
        for ph, us in enumerate(PHASES):
            for b in (2 * r, 2 * r + 1):
                first = len(slots)
                for u in us:
                    a = ATT[u]
                    n_c = -(-a["nk"] // P)
                    for qd in range(a["H"] // 4):
                        n, start = len(quads), len(slots)
                        for c in range(n_c):
                            for h in range(4 * qd, 4 * qd + 4, a["hps"]):
                                slots.append(dict(n=n, u=u, b=b, c=c, heads=list(range(h, h + a["hps"])),
                                                  last=c == n_c - 1 and h + a["hps"] == 4 * qd + 4))
                        quads.append(dict(n=n, b=b, u=u, qd=qd, start=start, n_c=n_c, first=start == first,
                                          slots=list(range(start, len(slots))),
                                          items=[(t, rows, list(range(h, h + a["hpm"])))
                                                 for h in range(4 * qd, 4 * qd + 4, a["hpm"]) for t, rows in q_tiles(u)]))
                span[ph, b] = (first, len(slots))
    due = {}

    def put(s, rank, step):
        due[step] = (s, rank, len(due))

    for q in quads:
        n, s0 = q["n"], q["start"]
        w = FIRST_W if q["first"] else len(quads[n - 1]["slots"])
        hi = s0 - M_LEAD
        lo = hi - w
        m = len(q["items"])
        put(lo - K_LEAD, 0, ("kdma", n))
        for i in range(m):
            put(lo + (i * w) // m, 1, ("max", n, i))
        put(hi, 2, ("negm", n))
        put(hi + MTR_DUE, 3, ("mtr", n))
        for c in range(q["n_c"]):
            last = max(s for s in q["slots"] if slots[s]["c"] == c)
            put(last + PV_LAG, 2, ("pv", n, c))
        put(q["slots"][-1] + PV_LAG, 3, ("oev", n))
    total = len(slots)
    windows = [(-80, 0, background(-1, 0), None), (0, span[0, 1][0], background(-1, 1), None)]
    for r in range(PAIRS):
        for ph in range(len(PHASES)):
            for b in (2 * r, 2 * r + 1):
                if ph + 1 < len(PHASES):
                    hi = span[ph + 1, b][0]
                else:
                    hi = span[0, b + 2][0] if r + 1 < PAIRS else total + TAIL
                if PHASES[ph] == (4, 3):
                    q = [q for q in quads if q["b"] == b and q["u"] == 4][-1]
                    windows.append((q["slots"][-1] + PV_LAG + 1, span[ph, b][1] + C_SPAN, [[last_rows(b)]], ("oev", q["n"])))
                windows.append((span[ph, b][1] + PV_LAG + 1, hi, background(ph, b),
                                ("oev", [q["n"] for q in quads if q["b"] == b and q["u"] in PHASES[ph]][-1])))
    stages = [[], []]
    for lo, hi, parts, after in windows:
        hi -= M_LEAD + FIRST_W + K_LEAD + 1
        steps = [s for lists in parts for s in spread_lists(lists)]
        for i, s in enumerate(steps):
            put(lo - BG_LEAD + (i * max(hi - lo, 1)) / len(steps), 4, s)
        b = parts[0][0][0][1 if parts[0][0][0][0] == "ctx_tr" else 2]
        stages[b % 2] += [(after, lists) for lists in parts]
    for s in range(total):
        put(s, -1, ("st", s))
    order = simulate(quads, slots, due, stages)
    return order, quads, slots


def takes_buffer(step):
    kind = step[0]
    if kind in ("kv_proj", "qkv_proj", "k_tr", "x_keys"):
        u, b = (4, step[1]) if kind == "x_keys" else step[1:3]
        last = kind == "k_tr" and step[4] == (1 if ATT[u]["sr"] == 64 else 2)
        return "ks", (u, b, step[3] // 2 if kind == "kv_proj" else step[3] if kind == "k_tr" else 0), last
    if kind in ("ff_g", "gelu", "ff_a", "ff_o"):
        return "gate", step[2], kind == "ff_o"
    if kind in ("c_tr", "c_q", "c_s", "c_norm", "c_p", "c_o") or kind == "o_nat" and step[1] == 4:
        return "c", step[2 if kind == "o_nat" else 1], kind == "c_o"
    return None


def dirty(quads, n):
    return n >= RING and ATT[quads[n]["u"]]["sr"] == 32 and ATT[quads[n - RING]["u"]]["sr"] == 64


def spread_lists(lists):
    return merge(*lists) if len(lists) == 2 else lists[0]


def cost(step, quads):
    kind = step[0]
    act = lambda *ns: [("act", sum(60 + 0.834 * n for n in ns))]
    dve = lambda *ns: [("dve", sum(60 + 1.05 * n for n in ns))]
    f32 = lambda n: 1.67 * n
    if kind in ("kdma", "max", "negm", "mtr", "pv", "oev"):
        q = quads[step[1]]
        u = q["u"]
        a = ATT[u]
        dh, nq, nk, groups = a["dh"], a["nq"], a["nk"], 4 * a["sr"] // P
    elif kind in ("kv_proj", "k_tr", "q_tr", "q_proj", "qkv_proj", "o_nat") and len(step) > 2:
        a = ATT[step[1]]
        n_g = a["H"] * a["sr"] // P
    if kind == "kdma":
        return 0, [("dma", 2600)]
    if kind == "clear":
        return 0, [("pool", 2400)]
    if kind == "low":
        return 0, dve(*{"kv_proj": [160], "qkv_proj": [160, 160], "q_proj": [320], "ca_q": [160]}[step[1][0]])
    if kind == "max":
        rows = a["hpm"] * nk
        return 4 + 0.417 * rows, [("dve", 60 + 1.05 * rows)]
    if kind == "negm":
        return 0, [("dve", 280)]
    if kind == "mtr":
        return TR * groups * len(q_tiles(u)), dve(groups * nq)
    if kind == "st":
        return 218, act(512)
    if kind == "pv":
        return 4 * nq * 0.47, []
    if kind == "oev":
        return 0, act(nq)
    if kind in ("k_tr", "q_tr"):
        if step[1] == 4 and kind == "q_tr":
            return 4 * TR, act(4 * C)
        n = min(2, n_g - 2 * step[-1])
        return 2 * n * TR, act(n * SQ)
    if kind == "o_nat":
        n = len(parts_of(step[1], step[3]))
        return n * TR, dve(4 * n, 32 * n, LINK)
    if kind in ("ff_g", "ff_a"):
        n = min(2, FC - 2 * step[3])
        return n * f32(2 * SQ), (act if kind == "ff_g" else dve)(*n * [SQ])
    return {
        "ctx_tr": (4 * TR, act(32, 512)), "kv_proj": (f32(320), act(320, 160)),
        "q_proj": (f32(640), act(640)), "qkv_proj": (f32(960), act(320, 320, 160)),
        "h_tr": (4 * TR, act(256, 256)), "o_tr": (4 * TR, act(256, 256)),
        "o_proj": (f32(640), dve(320)), "ln": (0, [("dve", 760), ("pool", 910)]), "norm": (0, dve(200, 200)),
        "x_bias": (0, [("pool", 821)]), "m_zero": (0, [("pool", 340)]), "x_keys": (0, act(640, 320) + dve(320)),
        "gelu": (0, [("act", 3700)]), "ff_o": (f32(10 * D), dve(320)), "ca_q": (f32(160), act(320)),
        "ca_kv": (350, dve(32, 32, 160)), "c_tr": (2 * TR, act(96, 96)), "c_q": (f32(4 * 96), act(96, 96)),
        "c_s": (f32(64), dve(32, 32) + act(32)), "c_norm": (0, dve(32, 8, 32)), "c_p": (f32(256), act(256)), "c_o": (f32(512), dve(256, 256)),
        "store": (0, []),
    }[kind]


LINK = 60
TR = 109
HANDOFF = 210
DMA_LATENCY = 2000


def simulate(quads, slots, due, stages):
    streams = [[("st", s) for s in range(len(slots))], [], [], [], []]
    for q in quads:
        n = q["n"]
        streams[1] += [("kdma", n)] + [("max", n, i) for i in range(len(q["items"]))] + [("negm", n)]
        streams[2].append(("mtr", n))
        if dirty(quads, n):
            streams[4].append(("clear", n))
        streams[3] += [("pv", n, c) for c in range(q["n_c"])] + [("oev", n)]
    last_of, produced = {}, {}
    for step in due:
        if step[0] in ("k_tr", "q_tr"):
            last_of[step[:3]] = step
    pv_of = {}
    for q in quads:
        for c in range(q["n_c"]):
            for s in q["slots"]:
                if slots[s]["c"] == c:
                    pv_of[s] = ("pv", q["n"], c)

    def needs(step):
        kind = step[0]
        if kind == "kdma":
            q = quads[step[1]]
            return ([last_of["k_tr", q["u"], q["b"]]] + ([("st", quads[q["n"] - RING]["slots"][-1])] if q["n"] >= RING else [])
                    + ([("clear", q["n"])] if dirty(quads, q["n"]) else []))
        if kind == "clear":
            return [("st", quads[step[1] - RING]["slots"][-1])]
        if kind == "max":
            q = quads[step[1]]
            return [last_of["q_tr", q["u"], q["b"]], ("kdma", q["n"])]
        if kind == "negm":
            return [("max", step[1], len(quads[step[1]]["items"]) - 1)]
        if kind == "mtr":
            return [("negm", step[1])]
        if kind == "st":
            s = step[1]
            return [("mtr", slots[s]["n"])] + ([("st", s - N_ST)] if s >= N_ST else []) + ([pv_of[s - N_P]] if s >= N_P else [])
        if kind == "pv":
            return ([("st", max(s for s in quads[step[1]]["slots"] if slots[s]["c"] == step[2]))]
                    + ([("oev", step[1] - 1)] if step[1] and step[2] == 0 else []))
        if kind == "oev":
            return [("pv", step[1], quads[step[1]]["n_c"] - 1)]
        if kind == "kv_proj":
            return [("ctx_tr", step[2])]
        if kind == "k_tr":
            u, b, pr = step[1:4]
            return [("x_keys", b)] if u == 4 else [("low", ("qkv_proj", u, b, 1))] if ATT[u]["kind"] == "self" else [("low", ("kv_proj", u, b, 2 * pr + 1))]
        if kind == "q_tr":
            u, b = step[1:3]
            return [("low", ("ca_q", b) if u == 4 else ("qkv_proj", u, b, 1) if ATT[u]["kind"] == "self" else ("q_proj", u, b)),
                    ("m_zero", u, b)]
        if kind in ("q_proj", "qkv_proj"):
            return [("h_tr", step[1], step[2])]
        if kind == "o_tr":
            return [("o_nat", step[1], step[2], i) for i in range(1 if step[1] == 3 else 3)]
        if kind == "o_proj":
            return [("c_o", step[2]) if step[1] == 3 else ("o_tr", *step[1:]), ("x_bias", *step[1:])]
        if kind == "h_tr":
            tag, b = step[1:]
            return [("norm", tag, b)] if tag in LNS else [("ff_o", "ff1", b)] if tag == 3 else []
        if kind in ("ln", "x_bias"):
            return [(*ROWS_FROM[step[1]], step[2])] if step[1] else []
        if kind == "norm":
            return [("ln", *step[1:])]
        if kind == "low":
            return [step[1]]
        if kind in ("ff_g", "ff_a"):
            return [("h_tr", *step[1:3])]
        if kind == "gelu":
            return [("ff_g", *step[1:], i) for i in range(3)]
        if kind == "ff_o":
            return [("ff_a", *step[1:], i) for i in range(3)]
        if kind == "x_keys":
            return [("ff_o", "ff1", step[1])]
        chain = {"c_tr": ("o_nat", 4, step[1], 0), "c_q": ("c_tr", step[1]), "c_s": ("c_q", step[1]),
                 "c_norm": ("c_s", step[1]),
                 "c_p": ("c_norm", step[1]), "c_o": ("c_p", step[1]), "store": ("ff_o", "ff3", step[1])}
        return [chain[kind]] if kind in chain else []

    clock = dict(pe=0, act=0, dve=0, pool=0, dma=0)
    done, order, uses, maxes = {}, [], [], []
    active, active_low = [[], []], []
    held = {}
    heads = [list(x) for x in streams]
    while any(heads) or any(stages) or any(map(any, active)) or any(active_low):
        for p in range(2):
            if not any(active[p]) and stages[p] and (stages[p][0][0] is None or stages[p][0][0] in done):
                active[p] = [list(x) for x in stages[p].pop(0)[1]]
        best = None
        for li in heads + active[0] + active[1] + active_low:
            if not li:
                continue
            step = li[0]
            need = needs(step)
            if any(x not in done for x in need):
                continue
            lock = takes_buffer(step)
            if lock and held.get(lock[0]) not in (None, lock[1]):
                continue
            start = max([done[x] for x in need], default=0)
            if step[0] in SPARE and len(uses) >= N_SP:
                if uses[-N_SP] not in done:
                    continue
                start = max(start, done[uses[-N_SP]])
            if step[0] == "max" and len(maxes) >= N_MX:
                start = max(start, done[maxes[-N_MX]])
            key = (max(start, clock["pe"]), due.get(step)) if cost(step, quads)[0] else (max(start, clock["pe"]), (-10**6, 0, 0))
            if best is None or key < best[0]:
                best = (key, start, li, step)
        key, start, li, step = best
        li.pop(0)
        order.append(step)
        lock = takes_buffer(step)
        if lock:
            held[lock[0]] = None if lock[2] else lock[1]
        pe, after = cost(step, quads)
        t = start
        if pe:
            t = clock["pe"] = max(start, clock["pe"]) + pe
        for eng, ns in after:
            t = clock[eng] = max(t + HANDOFF, clock[eng]) + ns
        done[step] = t + (DMA_LATENCY if step[0] == "kdma" else HANDOFF)
        if step[0] in LOW:
            uses.append(("low", step))
            active_low.append([("low", step)])
        elif step[0] in SPARE:
            uses.append(step)
        if step[0] == "max":
            maxes.append(step)
    return order


SPARE = {"ctx_tr", "kv_proj", "k_tr", "q_proj", "q_tr", "qkv_proj", "o_nat", "o_tr", "o_proj", "h_tr", "ff_g", "ff_a",
         "ff_o", "ca_q", "ca_kv", "c_tr", "c_q", "c_s", "c_p", "c_o", "mtr"}

LOW = {"kv_proj", "qkv_proj", "q_proj", "ca_q"}

SIGNALS = {
    "scores_full": {"st"}, "probs_ready": {"st"}, "max_full": {"max"}, "max_taken": {"max"}, "negm_ready": {"negm"},
    "out_full": {"pv_last"}, "out_taken": {"oev"}, "k_high": {"kv_proj", "x_keys", "qkv_proj"}, "x_split": {"x_keys"},
    "q_high": {"q_proj", "ca_q"}, "m_zeroed": {"m_zero"}, "cleared": {"clear"}, "x_biased": {"x_bias"}, "var_ready": {"ln"},
    "rstd_ready": {"ln"}, "xn_ready": {"norm"}, "gate_ready": {"gelu"}, "c_exp": {"c_s"}, "c_probs": {"c_norm"},
}

ROWS_FROM = {1: ("o_proj", 0), 2: ("o_proj", 1), "ff1": ("o_proj", 2), 3: ("ff_o", "ff1"), 5: ("o_proj", 3),
             6: ("o_proj", 5), "ff3": ("o_proj", 6)}


def parts_of(u, i):
    if u == 4:
        return [(qd, 0, C) for qd in range(2)]
    if u == 3:
        return [(qd, t, P) for t in range(TQ) for qd in range(2)]
    return [(qd, i, P) for qd in range(4)] if i < 2 else [(4, t, P) for t in range(TQ)]


def build(nc, io):
    order, quads, slots = plan()
    value, seen, turn, uses = {}, {}, {}, 0
    for step in order:
        kinds = {step[0]}
        if step[0] == "pv" and step[2] == -(-ATT[quads[step[1]]["u"]]["nk"] // P) - 1:
            kinds.add("pv_last")
        for name, by in SIGNALS.items():
            if kinds & by:
                seen[name] = seen.get(name, 0) + 1
                value[name, step] = seen[name]
        if step[0] in SPARE:
            turn[step] = (uses % N_SP, uses // N_SP)
            uses += 1

    def slot_value(name, s):
        return value[name, ("st", s)]

    with ExitStack() as ctx:
        def sb(name, shape, dt=F32):
            return ctx.enter_context(nc.sbuf_tensor(name, shape, dt))

        def sem(name):
            return ctx.enter_context(nc.semaphore(name))

        st_ps = [ctx.enter_context(nc.psum_tensor(f"st_ps{i}", [P, 512], F32)) for i in range(N_ST)]
        mx_ps = [ctx.enter_context(nc.psum_tensor(f"mx_ps{i}", [P, 512], F32)) for i in range(N_MX)]
        pv_ps = ctx.enter_context(nc.psum_tensor("pv_ps", [P, 512], F32))
        sp_ps = [ctx.enter_context(nc.psum_tensor(f"sp_ps{i}", [P, 512], F32)) for i in range(N_SP)]

        wm = sb("wm", [P, 640])
        wm2 = sb("wm2", [D2, 640])
        wb = sb("wb", [P, 3040])
        wb2 = sb("wb2", [D2, 2240])
        wbc = sb("wbc", [C, 320])
        wc = sb("wc", [C, 960])
        wqca = sb("wqca", [NCA, D])
        cols = sb("cols", [P, 32])
        cols2 = sb("cols2", [D2, 12])
        bias = sb("bias", [P, 8 * D])
        ident = sb("ident", [P, P])
        identr = sb("identr", [P, P], FR)
        spread = sb("spread", [C, SQ])
        kmask = sb("kmask", [P, 32])
        kmask2 = sb("kmask2", [D2, 32])
        vmask = sb("vmask", [32, D])
        halfpow = sb("halfpow", [P, TQ])
        def two(name, shape, dt=F32):
            return PAIRS * [sb(f"{name}{i}", shape, dt) for i in range(2)]

        x = [sb(f"x{b}", [P, TQ, D]) for b in range(B)]
        ctx_n = two("ctx_n", [P, 4, C])
        ca_n = two("ca_n", [NCA, C])
        xb = two("xb", [P, TQ, D])
        nat = two("nat", [P, TQ, D])
        natc = sb("natc", [C, D])
        hT = two("hT", [P, SQ])
        hT2 = two("hT2", [D2, SQ])
        ctxT = two("ctxT", [C, SK])
        caT8 = two("caT8", [C, 32])
        kdense = two("kdense", [P, 5, SK])
        v20 = two("v20", [P, 4, 20, 9])
        v8 = two("v8", [P, 6, 8, 21])
        qs20 = two("qs20", [P, TQ, 20, 32], FR)
        qs8 = two("qs8", [P, TQ + 1, 8, 64], FR)
        qT = two("qT", [P, 5, SQ], FR)
        qTc = two("qTc", [P, 4, C], FR)
        mx = two("mx", [P, TQ + 1, 20])
        oT = two("oT", [P, 5, SQ])
        oTc = two("oTc", [P, 2, C])
        kbd = two("kbd", [P, 32])
        kbd2 = two("kbd2", [D2, 32])
        vbd = two("vbd", [32, D])
        ks20 = sb("ks20", [P, 2, 20, 32], FR)
        ks8 = sb("ks8", [P, 2, 8, 64], FR)
        ring = sb("ring", [P, RING, 4, SK], FR)
        probs = sb("probs", [P, N_P, 512])
        gate = sb("gate", [P, FC, SQ])
        stats = two("stats", [P, TQ, 6])
        mv = two("mv", [P, TQ, 2])
        rstd = two("rstd", [P, TQ])
        rinv = two("rinv", [P, 4, 20])
        cT = sb("cT", [P, C])
        cT2 = sb("cT2", [D2, C])
        cq = sb("cq", [P, C])
        cq2 = sb("cq2", [D2, C])
        cs = sb("cs", [C, 32])
        cmax = sb("cmax", [C, 8])
        cpT = sb("cpT", [32, SQ])

        S = {name: sem(name) for name in SIGNALS}
        spare_full = [sem(f"spare_full{i}") for i in range(N_SP)]
        spare_taken = [sem(f"spare_taken{i}") for i in range(N_SP)]
        ring_in = [sem(f"ring_in{i}") for i in range(RING)]
        s_in = [sem(f"inputs_in{b}") for b in range(B)]
        s_x = [sem(f"rows_in{b}") for b in range(B)]
        s_ident, s_wc = sem("ident_in"), sem("context_weights_in")
        s_ca = [sem(f"last_rows_in{b}") for b in range(B)]
        s_blk = [sem(f"block_weights{i}") for i in range(2 * PAIRS)]
        s_used = sem("probs_used")
        dve_link = sem("dve_link")
        act_link = sem("act_link")
        pool_link = sem("pool_link")
        s_out = sem("stored")
        s_w = sem("weights_in")
        s_setup = sem("setup_done")
        s_warm = sem("zeros_ready")
        def of(u):
            return P // ATT[u]["sr"]

        def region(u, h):
            return h % 4 if of(u) == 4 else 2 * (h % 2) + h % 4 // 2

        def key_op(n, h):
            return ring[:, n % RING, region(quads[n]["u"], h), :]

        ring_dmas = {n: 4 * (n // RING + 1) for n in range(len(quads))}

        used_after, count = {}, 0
        for step in order:
            if step[0] == "pv":
                for s in quads[step[1]]["slots"]:
                    if slots[s]["c"] == step[2]:
                        if slots[s]["last"]:
                            used_after[s] = (S["out_full"], step[1] + 1)
                        else:
                            count += 1
                            used_after[s] = (s_used, count)

        def query_op(u, b):
            return qTc[b] if ATT[u]["kind"] == "ca" else qT[b]

        def dense_keys(u, b, g):
            if u == 4:
                return oT[b][:, 2 + g, :] if g < 2 else kdense[b][:, 4, (g - 2) * SQ:(g - 1) * SQ]
            return kdense[b][:, g, :]

        def taken(eng, step):
            b, k = turn[step]
            eng.wait_ge(spare_taken[b], k + 1)

        def query_stack(u, b):
            return qs20[b] if ATT[u]["sr"] == 32 else qs8[b]

        def block_in(eng, u, b):
            eng.wait_ge(s_blk[2 * (b // 2) + (0 if u in (1, 2) else 1)], 48)

        def wts(name, lo=0, hi=None):
            a, b = W_BLOCK[name]
            return slice(a + lo, a + hi if hi is not None else b)

        def context_in(sp, b):
            sp.dma_start(ctx_n[b][:, :, :], io["ctx"][b].rearrange("(t r) c -> r t c", r=P)).then_inc(s_in[b], 16)

        def rows_in(sp, b):
            sp.dma_start(x[b][:, :, :], io["x"][b].rearrange("(t r) d -> r t d", r=P)).then_inc(s_x[b], 16)

        with nc.Block() as block:
            @block.sync
            def _(sp):
                context_in(sp, 0)
                sp.dma_start(ident[:, :], io["ident"]).then_inc(s_ident, 16)
                sp.dma_start(wc[:, :], io["w_ctx"]).then_inc(s_wc, 16)
                rows_in(sp, 0)
                for dst, src in ((wm, "w_main"), (wm2, "w_main2"), (cols, "cols"), (cols2, "cols2"), (wqca, "w_qca"),
                                 (spread, "spread"), (kmask, "kmask"), (kmask2, "kmask2"), (vmask, "vmask")):
                    sp.dma_start(dst[:, :], io[src]).then_inc(s_w, 16)
                sp.dma_start(bias[:, :], io["bias"].broadcast_to([P, 8 * D])).then_inc(s_w, 16)

            @block.scalar
            def _(act):
                act.wait_ge(s_ident, 16)
                nc.scalar.activation(identr[:, :], ident[:, :], ACT.Copy).then_inc(s_setup, 1)

            @block.vector
            def _(dve):
                nc.vector.memset(probs[:, 0, :], 0.0).then_inc(s_warm, 1)
                nc.vector.memset(ring[:, :, :, :].bitcast(F32), 0.0)
                nc.vector.memset(pv_ps[:, :], 0.0)
                nc.vector.memset(v20[0][:, :, :, 8:9], 1.0)
                nc.vector.memset(v20[1][:, :, :, 8:9], 1.0)
                nc.vector.memset(v8[0][:, :, :, 20:21], 1.0)
                nc.vector.memset(v8[1][:, :, :, 20:21], 1.0).then_inc(s_setup, 1)

            @block.tensor
            def _(pe):
                pe.wait_ge(s_warm, 1)
                for _ in range(WARM_UP):
                    pe.matmul(st_ps[0][:, :], probs[:, 0, 0:P], probs[:, 0, :], start=True, stop=True)

            @block.gpsimd
            def _(pool):
                for t in (ks20, ks8, *qs20[:2], *qs8[:2]):
                    nc.gpsimd.memset(t[:, :, :, :].bitcast(F32), 0.0).then_inc(pool_link, 1)
                pool.wait_ge(pool_link, 6)
                nc.gpsimd.memset(ks20[:, :, :, 24:26].bitcast(F32), 1.0)
                nc.gpsimd.memset(ks8[:, :, :, 60:62].bitcast(F32), 1.0)
                nc.gpsimd.memset(halfpow[:, :], -0.5).then_inc(s_setup, 1)

        with nc.Block() as block:
            @block.sync
            def _(sp):
                def block_weights(k):
                    for dst, src in ((wb, "w_blk"), (wb2, "w_blk2"), (wbc, "w_blkc")):
                        sp.dma_start(dst[:, :], io[src][k % 2]).then_inc(s_blk[k], 16)

                def last_rows_in(b):
                    sp.dma_start(ca_n[b][:, :], io["ctx"][b][NENC:SK, :]).then_inc(s_ca[b], 16)

                context_in(sp, 1)
                for b in range(1, B):
                    rows_in(sp, b)
                for b in range(2):
                    last_rows_in(b)
                block_weights(0)
                for step in order:
                    if step[0] == "kdma":
                        n = step[1]
                        u, b, qd = quads[n]["u"], quads[n]["b"], quads[n]["qd"]
                        a = ATT[u]
                        taken(sp, [s for s in order if s[0] == "k_tr" and s[1] == u and s[2] == b][-1])
                        if n >= RING:
                            sp.wait_ge(S["scores_full"], quads[n - RING]["slots"][-1] + 1)
                        if dirty(quads, n):
                            sp.wait_ge(S["cleared"], value["cleared", ("clear", n)])
                        for h in range(4 * qd, 4 * qd + 4):
                            j, g = h % of(u), h // of(u)
                            rows = slice(a["sr"] * j, a["sr"] * (j + 1))
                            sp.dma_start(ring[rows, n % RING, region(u, h), 0:a["nk"]].bitcast(F32),
                                         dense_keys(u, b, g)[rows, 0:a["nk"]]).then_inc(ring_in[n % RING], 16)
                    elif step[0] == "ctx_tr" and step[1] + 2 < B:
                        taken(sp, step)
                        context_in(sp, step[1] + 2)
                    elif step[0] == "ff_o" and step[2] % 2 == 1 and step != ("ff_o", "ff3", B - 1):
                        taken(sp, step)
                        block_weights(2 * (step[2] // 2) + (1 if step[1] == "ff1" else 2))
                    elif step[0] == "store":
                        b = step[1]
                        taken(sp, ("ff_o", "ff3", b))
                        sp.dma_start(io["out"][b].rearrange("(t r) d -> r t d", r=P), x[b][:, :, :]).then_inc(s_out, 16)
                        if b + 2 < B:
                            taken(sp, ("ca_q", b))
                            last_rows_in(b + 2)
                sp.wait_ge(s_out, 16 * B)

            @block.tensor
            def _(pe):
                def take(step):
                    b, k = turn[step]
                    if k:
                        pe.wait_ge(spare_taken[b], k)
                    return sp_ps[b], spare_full[b]

                def two_part(out, lhs, lhs2, rhs, rhs2):
                    pe.matmul(out, lhs, rhs, start=True, stop=False)
                    return pe.matmul(out, lhs2, rhs2, start=False, stop=True)

                for step in order:
                    kind = step[0]
                    if kind == "st":
                        s = step[1]
                        sl = slots[s]
                        n, u, b, c = sl["n"], sl["u"], sl["b"], sl["c"]
                        a = ATT[u]
                        if s == quads[n]["start"]:
                            taken(pe, ("mtr", n))
                        if s >= N_ST:
                            pe.wait_ge(S["probs_ready"], slot_value("probs_ready", s - N_ST))
                        kr = chunk_rows(a["nk"], c)
                        for i, h in enumerate(sl["heads"]):
                            mm = pe.matmul(st_ps[s % N_ST][0:kr, i * a["nq"]:(i + 1) * a["nq"]],
                                           key_op(n, h)[:, c * P:c * P + kr], query_op(u, b)[:, h // of(u), :],
                                           start=True, stop=True)
                        mm.then_inc(S["scores_full"], 1)
                    elif kind == "max":
                        _, n, i = step
                        u, b = quads[n]["u"], quads[n]["b"]
                        a = ATT[u]
                        t, rows, heads = quads[n]["items"][i]
                        if i == 0:
                            last = [s for s in order if s[0] == "q_tr" and s[1] == u and s[2] == b][-1]
                            taken(pe, last)
                            pe.wait_ge(ring_in[n % RING], 16 * ring_dmas[n])
                        o = value["max_full", step] - 1
                        if o >= N_MX:
                            pe.wait_ge(S["max_taken"], o - N_MX + 1)
                        tt = 0 if t == TQ else t
                        for j, h in enumerate(heads):
                            mm = pe.matmul(mx_ps[o % N_MX][0:rows, j * a["nk"]:(j + 1) * a["nk"]],
                                           query_op(u, b)[:, h // of(u), tt * P:tt * P + rows],
                                           key_op(n, h)[:, 0:a["nk"]], start=True, stop=True)
                        mm.then_inc(S["max_full"], 1)
                    elif kind == "mtr":
                        n = step[1]
                        u, b, qd = quads[n]["u"], quads[n]["b"], quads[n]["qd"]
                        a = ATT[u]
                        bank, full = take(step)
                        pe.wait_ge(S["negm_ready"], value["negm_ready", ("negm", n)])
                        gs = range(4 * qd // of(u), (4 * qd + 4) // of(u))
                        for k, g in enumerate(gs):
                            for i, (t, rows) in enumerate(q_tiles(u)):
                                mm = pe.matmul(bank[:, k * a["nq"] + i * P:k * a["nq"] + i * P + rows],
                                               query_stack(u, b)[0:rows, t, g * of(u):(g + 1) * of(u), :].rearrange("p h s -> p (h s)"),
                                               identr[0:rows, 0:rows], start=True, stop=True)
                        mm.then_inc(full, 1)
                    elif kind == "pv":
                        _, n, c = step
                        u, b, qd = quads[n]["u"], quads[n]["b"], quads[n]["qd"]
                        a = ATT[u]
                        mine = [s for s in quads[n]["slots"] if slots[s]["c"] == c]
                        if c == 0 and n:
                            pe.wait_ge(S["out_taken"], n)
                        pe.wait_ge(S["probs_ready"], slot_value("probs_ready", mine[-1]))
                        if c == 0 and qd == 0:
                            last = [s for s in order if s[0] in ("kv_proj", "qkv_proj", "x_keys") and
                                    (s[1:3] == (u, b) if s[0] != "x_keys" else (u == 4 and s[1] == b))][-1]
                            pe.wait_ge(S["k_high"], value["k_high", last])
                        kr = chunk_rows(a["nk"], c)
                        for s in mine:
                            for i, h in enumerate(slots[s]["heads"]):
                                j = h % 4
                                v = v20[b][0:kr, c, h, :] if a["dh"] == 8 else v8[b][0:kr, c + (4 if u == 4 else 0), h, :]
                                mm = pe.matmul(pv_ps[32 * j:32 * j + a["dh"] + 1, 0:a["nq"]], v,
                                               probs[0:kr, s % N_P, i * a["nq"]:(i + 1) * a["nq"]],
                                               start=(c == 0), stop=(c == -(-a["nk"] // P) - 1), tile_position=(0, 32 * j))
                            if s == mine[-1] and c == -(-a["nk"] // P) - 1:
                                mm.then_inc(S["out_full"], 1)
                            else:
                                mm.then_inc(s_used, 1)
                    elif kind == "ctx_tr":
                        b = step[1]
                        bank, full = take(step)
                        pe.wait_ge(s_in[b], 16)
                        if b == 0:
                            pe.wait_ge(s_ident, 16)
                        for t in range(4):
                            mm = pe.transpose(bank[0:C, t * P:(t + 1) * P], ctx_n[b][:, t, :], ident[:, :])
                        mm.then_inc(full, 1)
                    elif kind == "kv_proj":
                        _, u, b, t = step
                        bank, full = take(step)
                        if t == 0:
                            taken(pe, ("ctx_tr", b))
                            if (u, b) == (0, 0):
                                pe.wait_ge(s_wc, 16)
                            if u in (2, 6):
                                block_in(pe, u, b)
                        kr = chunk_rows(ATT[u]["nk"], t)
                        w = wbc[:, :] if u in (2, 6) else wc[:, W_CTX[u][0]:W_CTX[u][1]]
                        pe.matmul(bank[0:kr, 0:320], ctxT[b][:, t * P:t * P + kr], w, start=True, stop=True).then_inc(full, 1)
                    elif kind == "k_tr":
                        _, u, b, pr, gg = step
                        bank, full = take(step)
                        if u == 4:
                            pe.wait_ge(S["x_split"], value["x_split", ("x_keys", b)])
                        elif ATT[u]["kind"] == "self":
                            for t in range(2):
                                taken(pe, ("qkv_proj", u, b, t))
                        else:
                            for t in range(2):
                                taken(pe, ("kv_proj", u, b, 2 * pr + t))
                        ks = ks20 if ATT[u]["sr"] == 32 else ks8
                        ng = ATT[u]["H"] // of(u)
                        for k, g in enumerate(range(2 * gg, min(2 * gg + 2, ng))):
                            for t in range(2):
                                kr = chunk_rows(ATT[u]["nk"], 2 * pr + t)
                                mm = pe.matmul(bank[:, k * SQ + t * P:k * SQ + t * P + kr],
                                               ks[0:kr, t, g * of(u):(g + 1) * of(u), :].rearrange("p h s -> p (h s)"),
                                               identr[0:kr, 0:kr], start=True, stop=True)
                        mm.then_inc(full, 1)
                    elif kind == "h_tr":
                        _, tag, b = step
                        bank, full = take(step)
                        src = nat[b] if tag in LNS else x[b]
                        if tag in LNS:
                            pe.wait_ge(S["xn_ready"], value["xn_ready", ("norm", tag, b)])
                        elif tag == 3:
                            taken(pe, ("ff_o", "ff1", b))
                        else:
                            pe.wait_ge(s_x[b], 16)
                        for t in range(TQ):
                            pe.transpose(bank[:, t * P:(t + 1) * P], src[:, t, 0:P], ident[:, :])
                            mm = pe.transpose(bank[:, SQ + t * P:SQ + (t + 1) * P], src[:, t, D2:D], ident[:, :])
                        mm.then_inc(full, 1)
                    elif kind == "q_proj":
                        _, u, b = step
                        bank, full = take(step)
                        taken(pe, ("h_tr", u, b))
                        if (u, b) == (0, 0):
                            pe.wait_ge(s_w, N_CONST * 16)
                        if u in (0, 3):
                            w, w2 = (wm[:, slice(*W_MAIN[f"q{u}"])], wm2[:, slice(*W_MAIN[f"q{u}"])])
                        else:
                            w, w2 = wb[:, wts("q2")], wb2[:, wts("q2")]
                        for t in range(TQ):
                            ts = slice(t * P, (t + 1) * P)
                            mm = two_part(bank[:, t * D:(t + 1) * D], hT[b][:, ts], hT2[b][:, ts], w, w2)
                        mm.then_inc(full, 1)
                    elif kind == "qkv_proj":
                        _, u, b, t = step
                        bank, full = take(step)
                        taken(pe, ("h_tr", u, b))
                        block_in(pe, u, b)
                        ts = slice(t * P, (t + 1) * P)
                        two_part(bank[:, 0:480], hT[b][:, ts], hT2[b][:, ts], wb[:, wts("qkv")], wb2[:, wts("qkv")]).then_inc(full, 1)
                    elif kind == "ca_q":
                        b = step[1]
                        bank, full = take(step)
                        pe.wait_ge(s_ca[b], 16)
                        pe.matmul(bank[0:C, 0:D], ca_n[b][:, :], wqca[:, :], start=True, stop=True).then_inc(full, 1)
                    elif kind == "q_tr":
                        _, u, b, gg = step
                        bank, full = take(step)
                        if ATT[u]["kind"] == "self":
                            for t in range(TQ):
                                taken(pe, ("qkv_proj", u, b, t))
                        else:
                            taken(pe, ("ca_q", b) if u == 4 else ("q_proj", u, b))
                        if gg == 0:
                            pe.wait_ge(S["m_zeroed"], value["m_zeroed", ("m_zero", u, b)])
                        ng = ATT[u]["H"] // of(u)
                        nq = ATT[u]["nq"]
                        for k, g in enumerate(range(4) if u == 4 else range(2 * gg, min(2 * gg + 2, ng))):
                            for i, (t, rows) in enumerate(q_tiles(u)):
                                mm = pe.matmul(bank[:, k * nq + i * P:k * nq + i * P + rows],
                                               query_stack(u, b)[0:rows, t, g * of(u):(g + 1) * of(u), :].rearrange("p h s -> p (h s)"),
                                               identr[0:rows, 0:rows], start=True, stop=True)
                        mm.then_inc(full, 1)
                    elif kind == "o_nat":
                        _, u, b, i = step
                        bank, full = take(step)
                        last = [q["n"] for q in quads if q["u"] == u and q["b"] == b][-1]
                        pe.wait_ge(S["out_taken"], last + 1)
                        for k, (qd, t, rows) in enumerate(parts_of(u, i)):
                            src = oTc[b][:, qd, :] if u == 4 else oT[b][:, qd, t * P:(t + 1) * P]
                            mm = pe.transpose(bank[0:rows, k * P:(k + 1) * P], src, ident[:, :])
                        mm.then_inc(full, 1)
                    elif kind == "o_tr":
                        _, u, b = step
                        bank, full = take(step)
                        for i in range(1 if u == 3 else 3):
                            taken(pe, ("o_nat", u, b, i))
                        for t in range(TQ):
                            pe.transpose(bank[:, t * P:(t + 1) * P], nat[b][:, t, 0:P], ident[:, :])
                            mm = pe.transpose(bank[:, SQ + t * P:SQ + (t + 1) * P], nat[b][:, t, D2:D], ident[:, :])
                        mm.then_inc(full, 1)
                    elif kind == "o_proj":
                        _, u, b = step
                        bank, full = take(step)
                        taken(pe, ("c_o", b) if u == 3 else ("o_tr", u, b))
                        if u in (0, 3):
                            w, w2 = (wm[:, slice(*W_MAIN[f"o{u}"])], wm2[:, slice(*W_MAIN[f"o{u}"])])
                        else:
                            name = "o1" if u in (1, 5) else "o2"
                            w, w2 = wb[:, wts(name)], wb2[:, wts(name)]
                        for t in range(TQ):
                            ts = slice(t * P, (t + 1) * P)
                            mm = two_part(bank[:, t * D:(t + 1) * D], hT[b][:, ts], hT2[b][:, ts], w, w2)
                        mm.then_inc(full, 1)
                    elif kind in ("ff_g", "ff_a"):
                        _, tag, b, i = step
                        bank, full = take(step)
                        taken(pe, ("h_tr", tag, b))
                        for k, m in enumerate(range(2 * i, min(2 * i + 2, FC))):
                            lo = (FF if kind == "ff_g" else 0) + m * P
                            mm = two_part(bank[:, k * SQ:(k + 1) * SQ], wb[:, wts("w1", lo, lo + P)], wb2[:, wts("w1", lo, lo + P)],
                                          hT[b][:, :], hT2[b][:, :])
                        mm.then_inc(full, 1)
                    elif kind == "ff_o":
                        _, tag, b = step
                        bank, full = take(step)
                        for t in range(TQ):
                            for m in range(FC):
                                if t == 0 and m % 2 == 0:
                                    taken(pe, ("ff_a", tag, b, m // 2))
                                mm = pe.matmul(bank[:, t * D:(t + 1) * D], gate[:, m, t * P:(t + 1) * P],
                                               wb[:, 2240 + m * D:2240 + (m + 1) * D], start=(m == 0), stop=(m == FC - 1))
                        mm.then_inc(full, 1)
                    elif kind == "ca_kv":
                        b = step[1]
                        bank, full = take(step)
                        wk = W_CTX["ca"][0]
                        pe.matmul(bank[:, 0:NCA], wc[:, wk:wk + P], ctxT[b][:, NENC:SK], start=True, stop=True)
                        pe.matmul(bank[0:D2, 8:8 + NCA], wc[:, wk + P:wk + D], ctxT[b][:, NENC:SK], start=True, stop=True)
                        pe.matmul(bank[0:32, 64:64 + D], caT8[b][:, :], wc[:, wk + D:wk + 2 * D], start=True, stop=True).then_inc(full, 1)
                    elif kind == "c_tr":
                        b = step[1]
                        bank, full = take(step)
                        taken(pe, ("o_nat", 4, b, 0))
                        pe.transpose(bank[:, 0:C], natc[:, 0:P], ident[0:C, 0:C])
                        pe.transpose(bank[:, P:P + C], natc[:, D2:D], ident[0:C, 0:C]).then_inc(full, 1)
                    elif kind == "c_q":
                        bank, full = take(step)
                        taken(pe, ("c_tr", step[1]))
                        a = W_MAIN["q3"][0]
                        two_part(bank[:, 0:C], wm[:, a:a + P], wm2[:, a:a + P], cT[:, :], cT2[:, :])
                        two_part(bank[0:D2, P:P + C], wm[:, a + P:a + D], wm2[:, a + P:a + D], cT[:, :], cT2[:, :]).then_inc(full, 1)
                    elif kind == "c_s":
                        b = step[1]
                        bank, full = take(step)
                        taken(pe, ("c_q", b))
                        taken(pe, ("ca_kv", b))
                        two_part(bank[0:C, 0:32], cq[:, :], cq2[:, :], kbd[b][:, :], kbd2[b][:, :]).then_inc(full, 1)
                    elif kind == "c_p":
                        b = step[1]
                        bank, full = take(step)
                        pe.wait_ge(S["c_probs"], value["c_probs", ("c_norm", b)])
                        pe.matmul(bank[0:32, 0:SQ], cs[:, :], spread[:, :], start=True, stop=True).then_inc(full, 1)
                    elif kind == "c_o":
                        b = step[1]
                        bank, full = take(step)
                        taken(pe, ("c_p", b))
                        pe.matmul(bank[:, 0:SQ], vbd[b][:, 0:P], cpT[:, :], start=True, stop=True)
                        pe.matmul(bank[0:D2, SQ:2 * SQ], vbd[b][:, P:D], cpT[:, :], start=True, stop=True).then_inc(full, 1)

            def filled(eng, step):
                b, k = turn[step]
                eng.wait_ge(spare_full[b], k + 1)
                return sp_ps[b], spare_taken[b]

            def high_slots(stack, t0, t1, rows, dh, which):
                step = 2 * dh if which == "k" else dh
                v = stack[0:rows, t0:t1, :, 0:3 * dh].rearrange("p t h (s d) -> p (t h) s d", s=3)
                return v[:, :, 0:3:2, :] if which == "k" else v[:, :, 0:2, :]

            @block.scalar
            def _(act):
                def split_high(stack, t0, t1, rows, dh, which, src):
                    out = high_slots(stack, t0, t1, rows, dh, which)
                    n = (t1 - t0) * (D // dh)
                    v = src.rearrange("p (h d) -> p h d", d=dh).unsqueeze(2).broadcast_to([rows, n, 2, dh])
                    return nc.scalar.activation(out, v, ACT.Copy)

                for step in order:
                    kind = step[0]
                    if kind == "st":
                        s = step[1]
                        a = ATT[slots[s]["u"]]
                        act.wait_ge(S["scores_full"], s + 1)
                        if s >= N_P:
                            act.wait_ge(*used_after[s - N_P])
                        kr = chunk_rows(a["nk"], slots[s]["c"])
                        w = a["hps"] * a["nq"]
                        nc.scalar.activation(probs[0:kr, s % N_P, 0:w], st_ps[s % N_ST][0:kr, 0:w], ACT.Exp,
                                             scale=float(a["dh"]) ** -0.5).then_inc(S["probs_ready"], 1)
                    elif kind == "oev":
                        n = step[1]
                        u, b, qd = quads[n]["u"], quads[n]["b"], quads[n]["qd"]
                        act.wait_ge(S["out_full"], n + 1)
                        dst = oTc[b][:, qd, :] if u == 4 else oT[b][:, qd, :]
                        nc.scalar.activation(dst, pv_ps[:, 0:ATT[u]["nq"]], ACT.Copy).then_inc(S["out_taken"], 1)
                    elif kind == "ctx_tr":
                        b = step[1]
                        bank, free = filled(act, step)
                        nc.scalar.activation(caT8[b][:, :].rearrange("p (h k) -> p h k", h=8),
                                             bank[0:C, NENC:SK].unsqueeze(1).broadcast_to([C, 8, NCA]), ACT.Copy)
                        nc.scalar.activation(ctxT[b][:, :], bank[0:C, :], ACT.Copy).then_inc(free, 1)
                    elif kind == "kv_proj":
                        _, u, b, t = step
                        dh = ATT[u]["dh"]
                        bank, free = filled(act, step)
                        kr = chunk_rows(ATT[u]["nk"], t)
                        ks, v = (ks20, v20[b]) if dh == 8 else (ks8, v8[b])
                        split_high(ks, t % 2, t % 2 + 1, kr, dh, "k", bank[0:kr, 0:D])
                        nc.scalar.activation(v[0:kr, t, :, 0:dh], bank[0:kr, D:2 * D].rearrange("p (h d) -> p h d", d=dh),
                                             ACT.Copy).then_inc(S["k_high"], 1)
                    elif kind == "qkv_proj":
                        _, u, b, t = step
                        bank, free = filled(act, step)
                        split_high(ks20, t, t + 1, P, 8, "k", bank[:, D:2 * D])
                        split_high(qs20[b], t, t + 1, P, 8, "q", bank[:, 0:D])
                        nc.scalar.activation(v20[b][:, t, :, 0:8], bank[:, 2 * D:3 * D].rearrange("p (h d) -> p h d", d=8),
                                             ACT.Copy).then_inc(S["k_high"], 1)
                    elif kind == "x_keys":
                        b = step[1]
                        taken(act, ("ff_o", "ff1", b))
                        prev = [s for s in order[:order.index(step)] if s[0] == "k_tr"][-1]
                        act.wait_ge(spare_full[turn[prev][0]], turn[prev][1] + 1)
                        split_high(ks8, 0, TQ, P, 20, "k", x[b][:, :, :].rearrange("p t d -> p (t d)"))
                        nc.scalar.activation(v8[b][:, 4:6, :, 0:20].rearrange("p t h d -> p (t h) d"),
                                             x[b][:, :, :].rearrange("p t (h d) -> p (t h) d", d=20), ACT.Copy).then_inc(S["k_high"], 1)
                    elif kind == "k_tr":
                        _, u, b, pr, gg = step
                        bank, free = filled(act, step)
                        ng = ATT[u]["H"] // of(u)
                        n = min(2, ng - 2 * gg)
                        w = chunk_rows(ATT[u]["nk"], 2 * pr) + chunk_rows(ATT[u]["nk"], 2 * pr + 1)
                        if u == 4:
                            dst = (oT[b][:, 2:4, :] if gg == 0 else kdense[b][:, 4, :].rearrange("p (g k) -> p g k", g=2))
                        else:
                            dst = kdense[b][:, 2 * gg:2 * gg + n, pr * SQ:pr * SQ + w]
                        nc.scalar.activation(dst, bank[:, 0:n * SQ].rearrange("p (g k) -> p g k", g=n)[:, :, 0:w], ACT.Copy).then_inc(free, 1)
                    elif kind == "h_tr":
                        _, tag, b = step
                        bank, free = filled(act, step)
                        if tag in LNS:
                            if (tag, b) == (1, 0):
                                act.wait_ge(s_w, N_CONST * 16)
                            c = 2 * LNS[tag]
                            nc.scalar.activation(hT[b][:, :], bank[:, 0:SQ], ACT.Identity, scale=cols[:, c:c + 1], bias=cols[:, c + 1:c + 2])
                            nc.scalar.activation(hT2[b][:, :], bank[P - D2:P, SQ:2 * SQ], ACT.Identity, scale=cols2[:, c:c + 1], bias=cols2[:, c + 1:c + 2]).then_inc(free, 1)
                        else:
                            nc.scalar.activation(hT[b][:, :], bank[:, 0:SQ], ACT.Copy)
                            nc.scalar.activation(hT2[b][:, :], bank[P - D2:P, SQ:2 * SQ], ACT.Copy).then_inc(free, 1)
                    elif kind == "o_tr":
                        b = step[2]
                        bank, free = filled(act, step)
                        nc.scalar.activation(hT[b][:, :], bank[:, 0:SQ], ACT.Copy)
                        nc.scalar.activation(hT2[b][:, :], bank[P - D2:P, SQ:2 * SQ], ACT.Copy).then_inc(free, 1)
                    elif kind in ("c_tr", "c_q"):
                        bank, free = filled(act, step)
                        dst, dst2 = (cT, cT2) if kind == "c_tr" else (cq, cq2)
                        nc.scalar.activation(dst[:, :], bank[:, 0:C], ACT.Copy)
                        last = slice(P - D2, P) if kind == "c_tr" else slice(0, D2)
                        nc.scalar.activation(dst2[:, :], bank[last, P:P + C], ACT.Copy).then_inc(free, 1)
                    elif kind == "c_p":
                        bank, free = filled(act, step)
                        nc.scalar.activation(cpT[:, :], bank[0:32, 0:SQ], ACT.Copy).then_inc(free, 1)
                    elif kind == "q_proj":
                        _, u, b = step
                        bank, free = filled(act, step)
                        dh = ATT[u]["dh"]
                        split_high(query_stack(u, b), 0, TQ, P, dh, "q", bank[:, 0:TQ * D]).then_inc(S["q_high"], 1)
                    elif kind == "ca_q":
                        b = step[1]
                        bank, free = filled(act, step)
                        split_high(qs8[b], TQ, TQ + 1, C, 20, "q", bank[0:C, 0:D]).then_inc(S["q_high"], 1)
                    elif kind == "q_tr":
                        _, u, b, gg = step
                        bank, free = filled(act, step)
                        if u == 4:
                            dst, w = qTc[b][:, :, :].rearrange("p g q -> p (g q)"), 4 * C
                        else:
                            n = min(2, ATT[u]["H"] // of(u) - 2 * gg)
                            dst, w = qT[b][:, 2 * gg:2 * gg + n, :].rearrange("p g q -> p (g q)"), n * SQ
                        nc.scalar.activation(dst, bank[:, 0:w], ACT.Copy).then_inc(free, 1)
                    elif kind == "ff_g":
                        _, tag, b, i = step
                        bank, free = filled(act, step)
                        for k, m in enumerate(range(2 * i, min(2 * i + 2, FC))):
                            c = 12 + (0 if tag == "ff1" else 10) + FC + m
                            ins = nc.scalar.activation(gate[:, m, :], bank[:, k * SQ:(k + 1) * SQ],
                                                       ACT.Gelu if (tag, b) == LAST_FEED else ACT.Identity, bias=cols[:, c:c + 1])
                        ins.then_inc(free, 1)
                    elif kind == "gelu":
                        _, tag, b = step
                        for i in (1, 2):
                            taken(act, ("ff_g", tag, b, i))
                        nc.scalar.activation(gate[:, :, :], gate[:, :, :], ACT.Gelu).then_inc(S["gate_ready"], 1)
                    elif kind == "c_s":
                        taken(act, step)
                        nc.scalar.activation(cs[:, :], cs[:, :], ACT.Exp, scale=20.0 ** -0.5).then_inc(S["c_exp"], 1)

            @block.vector
            def _(dve):
                links = [0]

                def link(ins):
                    links[0] += 1
                    ins.then_inc(dve_link, 1)
                    dve.wait_ge(dve_link, links[0])

                def split_low(stack, t0, t1, rows, dh, which, src):
                    lo = dh if which == "k" else 2 * dh
                    high = stack[0:rows, t0:t1, :, 0:dh].rearrange("p t h d -> p (t h) d").bitcast(F32)
                    out = stack[0:rows, t0:t1, :, lo:lo + dh].rearrange("p t h d -> p (t h) d")
                    return nc.vector.tensor_tensor(out, src.rearrange("p (h d) -> p h d", d=dh), high, ALU.subtract)

                def step_low(step):
                    bank, done = filled(dve, step)
                    if step[0] == "kv_proj":
                        _, u, b, t = step
                        dve.wait_ge(S["k_high"], value["k_high", step])
                        kr = chunk_rows(ATT[u]["nk"], t)
                        ks = ks20 if ATT[u]["dh"] == 8 else ks8
                        ins = split_low(ks, t % 2, t % 2 + 1, kr, ATT[u]["dh"], "k", bank[0:kr, 0:D])
                    elif step[0] == "qkv_proj":
                        _, u, b, t = step
                        dve.wait_ge(S["k_high"], value["k_high", step])
                        split_low(ks20, t, t + 1, P, 8, "k", bank[:, D:2 * D])
                        ins = split_low(qs20[b], t, t + 1, P, 8, "q", bank[:, 0:D])
                    elif step[0] == "ca_q":
                        dve.wait_ge(S["q_high"], value["q_high", step])
                        ins = split_low(qs8[step[1]], TQ, TQ + 1, C, 20, "q", bank[0:C, 0:D])
                    else:
                        _, u, b = step
                        dve.wait_ge(S["q_high"], value["q_high", step])
                        ins = split_low(query_stack(u, b), 0, TQ, P, ATT[u]["dh"], "q", bank[:, 0:TQ * D])
                    ins.then_inc(done, 1)

                for step in order:
                    kind = step[0]
                    if kind == "max":
                        _, n, i = step
                        u, b = quads[n]["u"], quads[n]["b"]
                        a = ATT[u]
                        t, rows, heads = quads[n]["items"][i]
                        o = value["max_full", step]
                        dve.wait_ge(S["max_full"], o)
                        nc.vector.tensor_reduce(mx[b][0:rows, t, heads[0]:heads[-1] + 1],
                                                mx_ps[(o - 1) % N_MX][0:rows, 0:a["hpm"] * a["nk"]].rearrange("p (h k) -> p h k", k=a["nk"]),
                                                AX.X, ALU.max).then_inc(S["max_taken"], 1)
                    elif kind == "negm":
                        n = step[1]
                        u, b, qd = quads[n]["u"], quads[n]["b"], quads[n]["qd"]
                        dh = ATT[u]["dh"]
                        tiles = q_tiles(u)
                        t0, t1, rows = tiles[0][0], tiles[-1][0] + 1, tiles[0][1]
                        dve.wait_ge(S["max_taken"], value["max_taken", ("max", n, len(quads[n]["items"]) - 1)])
                        m = mx[b][0:rows, t0:t1, 4 * qd:4 * qd + 4]
                        st = query_stack(u, b)[0:rows, t0:t1, 4 * qd:4 * qd + 4, :]
                        link(nc.vector.tensor_scalar(st[:, :, :, 3 * dh], m, -1.0, None, ALU.mult))
                        nc.vector.scalar_tensor_tensor(out=st[:, :, :, 3 * dh + 1], in0=m, scalar=-1.0,
                                                       in1=st[:, :, :, 3 * dh].bitcast(F32),
                                                       op0=ALU.mult, op1=ALU.subtract).then_inc(S["negm_ready"], 1)
                    elif kind == "mtr":
                        n = step[1]
                        u, b, qd = quads[n]["u"], quads[n]["b"], quads[n]["qd"]
                        bank, done = filled(dve, step)
                        g0, g1 = 4 * qd // of(u), (4 * qd + 4) // of(u)
                        nq = ATT[u]["nq"]
                        nc.vector.tensor_copy(query_op(u, b)[:, g0:g1, :].rearrange("p g q -> p (g q)"),
                                              bank[:, 0:(g1 - g0) * nq]).then_inc(done, 1)
                    elif kind == "low":
                        step_low(step[1])
                    elif kind == "x_keys":
                        b = step[1]
                        dve.wait_ge(S["k_high"], value["k_high", step])
                        split_low(ks8, 0, TQ, P, 20, "k", x[b][:, :, :].rearrange("p t d -> p (t d)")).then_inc(S["x_split"], 1)
                    elif kind == "ln":
                        _, tag, b = step
                        taken(dve, (*ROWS_FROM[tag], b))
                        nc.vector.bn_stats(stats[b][:, 0, :], x[b][:, 0, :])
                        link(nc.vector.bn_stats(stats[b][:, 1, :], x[b][:, 1, :]))
                        nc.vector.bn_aggr(mv[b][:, 0, :], stats[b][:, 0, :])
                        nc.vector.bn_aggr(mv[b][:, 1, :], stats[b][:, 1, :]).then_inc(S["var_ready"], 1)
                    elif kind == "norm":
                        _, tag, b = step
                        dve.wait_ge(S["rstd_ready"], value["rstd_ready", ("ln", tag, b)])
                        for t in range(TQ):
                            ins = nc.vector.tensor_scalar(nat[b][:, t, :], x[b][:, t, :], mv[b][:, t, 0:1], rstd[b][:, t:t + 1],
                                                          ALU.subtract, ALU.mult)
                        ins.then_inc(S["xn_ready"], 1)
                    elif kind == "o_nat":
                        _, u, b, i = step
                        bank, done = filled(dve, step)
                        parts = parts_of(u, i)
                        rows, dh, nh = parts[0][2], ATT[u]["dh"], 4 * len(parts)
                        v = bank[0:rows, 0:nh * 32].rearrange("p (h s) -> p h s", s=32)
                        k = 3 if u == 4 else i
                        link(nc.vector.reciprocal(rinv[b][0:rows, k, 0:nh], v[:, :, dh]))
                        inv = rinv[b][0:rows, k, 0:nh].unsqueeze(2).broadcast_to([rows, nh, dh])
                        if u == 4:
                            out = natc[:, :].rearrange("p (h d) -> p h d", d=dh)
                        elif u == 3:
                            out = nat[b][:, :, :].rearrange("p t (h d) -> p (t h) d", d=dh)
                        elif i < 2:
                            out = nat[b][:, i, 0:P].rearrange("p (h d) -> p h d", d=dh)
                        if u in (3, 4) or i < 2:
                            nc.vector.tensor_tensor(out, v[:, :, 0:dh], inv, ALU.mult).then_inc(done, 1)
                        else:
                            for t in range(TQ):
                                ins = nc.vector.tensor_tensor(nat[b][:, t, P:D].rearrange("p (h d) -> p h d", d=dh),
                                                              v[:, 4 * t:4 * t + 4, 0:dh], inv[:, 4 * t:4 * t + 4, :], ALU.mult)
                            ins.then_inc(done, 1)
                    elif kind in ("o_proj", "ff_o"):
                        _, u, b = step
                        bank, done = filled(dve, step)
                        dve.wait_ge(S["x_biased"], value["x_biased", ("x_bias", u, b)])
                        nc.vector.tensor_tensor(x[b][:, :, :].rearrange("p t d -> p (t d)"), bank[:, 0:TQ * D],
                                                xb[b][:, :, :].rearrange("p t d -> p (t d)"), ALU.add).then_inc(done, 1)
                    elif kind == "ff_a":
                        _, tag, b, i = step
                        bank, done = filled(dve, step)
                        if (tag, b) == LAST_FEED:
                            taken(dve, ("ff_g", tag, b, i))
                        else:
                            dve.wait_ge(S["gate_ready"], value["gate_ready", ("gelu", tag, b)])
                        for k, m in enumerate(range(2 * i, min(2 * i + 2, FC))):
                            c = 12 + (0 if tag == "ff1" else 10) + m
                            ins = nc.vector.scalar_tensor_tensor(out=gate[:, m, :], in0=bank[:, k * SQ:(k + 1) * SQ],
                                                                 scalar=cols[:, c:c + 1], in1=gate[:, m, :],
                                                                 op0=ALU.add, op1=ALU.mult)
                        ins.then_inc(done, 1)
                    elif kind == "ca_kv":
                        b = step[1]
                        bank, done = filled(dve, step)
                        if b == 0:
                            dve.wait_ge(s_w, N_CONST * 16)
                        for dst, mask, k in ((kbd[b], kmask, bank[:, 0:NCA]), (kbd2[b], kmask2, bank[0:D2, 8:8 + NCA])):
                            rows = mask.shape[0]
                            nc.vector.tensor_tensor(dst[:, :].rearrange("p (h k) -> p h k", h=8),
                                                    k.unsqueeze(1).broadcast_to([rows, 8, NCA]),
                                                    mask[:, :].rearrange("p (h k) -> p h k", h=8), ALU.mult)
                        nc.vector.tensor_tensor(vbd[b][:, :], bank[0:32, 64:64 + D], vmask[:, :], ALU.mult).then_inc(done, 1)
                    elif kind == "c_s":
                        bank, done = filled(dve, step)
                        v = bank[0:C, 0:32].rearrange("p (h k) -> p h k", h=8)
                        cv = cs[:, :].rearrange("p (h k) -> p h k", h=8)
                        spread_h = cmax[:, :].unsqueeze(2).broadcast_to([C, 8, NCA])
                        link(nc.vector.tensor_reduce(cmax[:, :], v, AX.X, ALU.max))
                        nc.vector.tensor_tensor(cv, v, spread_h, ALU.subtract).then_inc(done, 1)
                    elif kind == "c_norm":
                        cv = cs[:, :].rearrange("p (h k) -> p h k", h=8)
                        spread_h = cmax[:, :].unsqueeze(2).broadcast_to([C, 8, NCA])
                        dve.wait_ge(S["c_exp"], value["c_exp", ("c_s", step[1])])
                        link(nc.vector.tensor_reduce(cmax[:, :], cv, AX.X, ALU.add))
                        link(nc.vector.reciprocal(cmax[:, :], cmax[:, :]))
                        nc.vector.tensor_tensor(cv, cv, spread_h, ALU.mult).then_inc(S["c_probs"], 1)
                    elif kind == "c_o":
                        b = step[1]
                        bank, done = filled(dve, step)
                        taken(dve, ("o_tr", 3, b))
                        nc.vector.tensor_tensor(hT[b][:, :], bank[:, 0:SQ], hT[b][:, :], ALU.add)
                        nc.vector.tensor_tensor(hT2[b][:, :], bank[0:D2, SQ:2 * SQ], hT2[b][:, :], ALU.add).then_inc(done, 1)

            @block.gpsimd
            def _(pool):
                links = 6
                for step in order:
                    kind = step[0]
                    if kind == "ln":
                        b = step[2]
                        pool.wait_ge(S["var_ready"], value["var_ready", step])
                        links += 1
                        nc.gpsimd.tensor_scalar(rstd[b][:, :], mv[b][:, :, 1], EPS, None, ALU.add).then_inc(pool_link, 1)
                        pool.wait_ge(pool_link, links)
                        nc.gpsimd.tensor_tensor(rstd[b][:, :], rstd[b][:, :], halfpow[:, :], ALU.pow).then_inc(S["rstd_ready"], 1)
                    elif kind == "clear":
                        n = step[1]
                        pool.wait_ge(S["scores_full"], quads[n - RING]["slots"][-1] + 1)
                        nc.gpsimd.memset(ring[:, n % RING, :, :].bitcast(F32), 0.0).then_inc(S["cleared"], 1)
                    elif kind == "x_bias":
                        _, tag, b = step
                        if tag != 0:
                            taken(pool, (*ROWS_FROM[tag], b))
                        else:
                            pool.wait_ge(s_x[b], 16)
                            if b == 0:
                                pool.wait_ge(s_w, N_CONST * 16)
                            if b >= 2:
                                taken(pool, ("ff_o", "ff3", b - 2))
                        c = BIAS[tag] * D
                        nc.gpsimd.tensor_tensor(xb[b][:, :, :], x[b][:, :, :],
                                                bias[:, c:c + D].unsqueeze(1).broadcast_to([P, TQ, D]), ALU.add).then_inc(S["x_biased"], 1)
                    elif kind == "m_zero":
                        _, u, b = step
                        first = [q["n"] for q in quads if q["u"] == u and q["b"] == b][0]
                        before = [q["n"] for q in quads[:first] if q["b"] % 2 == b % 2 and
                                  (q["u"] == u if u in (3, 4) else ATT[q["u"]]["sr"] == 32)]
                        if before:
                            taken(pool, ("mtr", before[-1]))
                        tiles = q_tiles(u)
                        dh = ATT[u]["dh"]
                        nc.gpsimd.memset(query_stack(u, b)[:, tiles[0][0]:tiles[-1][0] + 1, :, 3 * dh:3 * dh + 2].bitcast(F32), 0.0).then_inc(S["m_zeroed"], 1)


def kernel(**inputs):
    import concourse.bacc as bacc
    from concourse.bass_utils import run_bass_kernel_spmd

    w = {k: np.asarray(v) for k, v in inputs.items()}
    blocks = ("L1_xattn_", "L3_xattn_")
    ln_names = [b + n for b in blocks for n in ("n1", "n2", "n3")]
    mains = [w["L0_xattn_Wq"], w["L0_xattn_Wo"], w["L2_xattn_Wq"], w["L2_xattn_Wout"]]
    wide = [np.concatenate([w[b + n] for n in ("q1", "k1", "v1", "o1_w", "q2", "o2_w", "ff_w1")], axis=1) for b in blocks]
    down = [w[b + "ff_w2"].reshape(FC, P, D).transpose(1, 0, 2).reshape(P, FC * D) for b in blocks]
    idx = np.linspace(0, C - 1, SQ).astype(np.int64)
    head = np.arange(D) // 20
    kmask = np.repeat((head[:, None] == np.arange(8)[None, :]).astype(np.float32), NCA, axis=1)
    arrays = {
        "x": w["x"], "ctx": w["ctx_768"],
        "w_main": np.concatenate([m[:P] for m in mains], axis=1),
        "w_main2": np.concatenate([m[P:] for m in mains], axis=1),
        "w_blk": np.stack([np.concatenate([a[:P], d], axis=1) for a, d in zip(wide, down)]),
        "w_blk2": np.stack([a[P:] for a in wide]),
        "w_blkc": np.stack([np.concatenate([w[b + "k2"], w[b + "v2"]], axis=1) for b in blocks]),
        "w_ctx": np.concatenate([w["L0_xattn_Wk"], w["L0_xattn_Wv"], w["L2_xattn_Wk"], w["L2_xattn_Wv"],
                                 w["L2_xattn_Wk_ca"], w["L2_xattn_Wv_ca"]], axis=1),
        "w_qca": w["L2_xattn_Wq_ca"],
        "cols": np.concatenate([np.stack([w[n + s][:P] for n in ln_names for s in ("_g", "_b")], axis=1)]
                               + [w[b + "ff_b1"].reshape(2 * FC, P).T for b in blocks], axis=1),
        "cols2": np.stack([w[n + s][P:] for n in ln_names for s in ("_g", "_b")], axis=1),
        "bias": np.concatenate([w[n] for n in (
            "L0_xattn_bo", "L1_xattn_o1_b", "L1_xattn_o2_b", "L1_xattn_ff_b2", "L2_xattn_b_out", "L3_xattn_o1_b",
            "L3_xattn_o2_b", "L3_xattn_ff_b2")])[None, :],
        "ident": np.eye(P, dtype=np.float32),
        "spread": (np.arange(C)[:, None] == idx[None, :]).astype(np.float32),
        "kmask": kmask[:P], "kmask2": kmask[P:],
        "vmask": kmask.T,
    }
    nc = bacc.Bacc("TRN2", target_bir_lowering=False, num_devices=1)
    arrays = {k: np.ascontiguousarray(v) for k, v in arrays.items()}
    io = {k: nc.dram_tensor("in_" + k, v.shape, mybir.dt.from_np(v.dtype), kind="ExternalInput").ap() for k, v in arrays.items()}
    io["out"] = nc.dram_tensor("out_rows", (B, SQ, D), F32, kind="ExternalOutput").ap()
    build(nc, io)
    r = run_bass_kernel_spmd(nc, [{"in_" + k: v for k, v in arrays.items()}], core_ids=[0])
    return r.results[0]["out_rows"]
```
